# Optimizing a Trainium2 kernel written in Bass

```python
import numpy as np
import jax
import jax.numpy as jnp

def _softmax(x, axis=-1):
    return jax.nn.softmax(x, axis=axis)

def _gelu(x):
    return jax.nn.gelu(x, approximate=True)

def _silu(x):
    return jax.nn.silu(x)

def _sigmoid(x):
    return jax.nn.sigmoid(x)

def _layernorm(x, axis=-1, eps=1e-05):
    m = jnp.mean(x, axis=axis, keepdims=True)
    v = jnp.var(x, axis=axis, keepdims=True)
    return (x - m) / jnp.sqrt(v + eps)

def _scatter_add(tgt, idx, src, axis=0):
    return tgt.at[idx].add(src)

def _segment_sum(src, seg, n):
    return jax.ops.segment_sum(src, seg, n)
kernel_name = 'mk_seq_preln_d2_jaxref_r8_0b3ecd'

def setup_inputs(seed: int=0):
    np.random.seed(seed)
    _w = jnp.asarray

    def _L0_attn_setup():
        import jax, jax.numpy as jnp
        import numpy as np
        NUM_HEADS = 16
        NUM_KV_HEADS = 4
        HEAD_DIM = 128
        D_MODEL = 256
        key = jax.random.key(seed)
        ks = jax.random.split(key, 6)
        B, S, d = (2, 256, D_MODEL)
        s_in = 1.0 / np.sqrt(d)
        return {'inputs_q': jax.random.normal(ks[0], (B, S, d), jnp.float32), 'wq': jax.random.normal(ks[1], (d, NUM_HEADS * HEAD_DIM), jnp.float32) * s_in, 'bq': jnp.zeros((NUM_HEADS * HEAD_DIM,), jnp.float32), 'wk': jax.random.normal(ks[2], (d, NUM_KV_HEADS * HEAD_DIM), jnp.float32) * s_in, 'bk': jnp.zeros((NUM_KV_HEADS * HEAD_DIM,), jnp.float32), 'wv': jax.random.normal(ks[3], (d, NUM_KV_HEADS * HEAD_DIM), jnp.float32) * s_in, 'bv': jnp.zeros((NUM_KV_HEADS * HEAD_DIM,), jnp.float32), 'wo': jax.random.normal(ks[4], (NUM_HEADS * HEAD_DIM, d), jnp.float32) * s_in, 'bo': jnp.zeros((d,), jnp.float32)}
    _L0_attn_in = _L0_attn_setup()

    def _L0_ffn_setup():
        import jax, jax.numpy as jnp
        import numpy as np
        H, LAT, INTER, E, G, TOPK_G, TOP_K = (256, 128, 128, 32, 4, 2, 8)
        SHARED_INTER = 512
        ROUTED_SCALE = 2.5
        B, S = (2, 128)

        def relu2(x):
            return jnp.square(jax.nn.relu(x))
        key = jax.random.key(seed)
        ks = jax.random.split(key, 9)
        w = 0.02
        return {'hidden_states': jax.random.normal(ks[0], (B, S, H), jnp.float32), 'gate_w': jax.random.normal(ks[1], (E, H), jnp.float32) * w, 'gate_bias': jax.random.normal(ks[2], (E,), jnp.float32) * w, 'fc1_w': jax.random.normal(ks[3], (LAT, H), jnp.float32) * w, 'fc2_w': jax.random.normal(ks[4], (H, LAT), jnp.float32) * w, 'w1': jax.random.normal(ks[5], (E, INTER, LAT), jnp.float32) * w, 'w2': jax.random.normal(ks[6], (E, LAT, INTER), jnp.float32) * w, 'shared_up_w': jax.random.normal(ks[7], (SHARED_INTER, H), jnp.float32) * w, 'shared_down_w': jax.random.normal(ks[8], (H, SHARED_INTER), jnp.float32) * w}
    _L0_ffn_in = _L0_ffn_setup()

    def _L1_attn_setup():
        import jax, jax.numpy as jnp
        import numpy as np
        EMBED = 256
        HEADS = 16
        HEAD_DIM = EMBED // HEADS
        CHUNK = 128
        BASE = 10000.0
        EPS = 1e-06

        def _alibi_log_decay(h):
            slopes = 2.0 ** (-8.0 * (jnp.arange(h, dtype=jnp.float32) + 1.0) / h)
            return -slopes

        def _lrpe_rotate(x):
            b, n, h, d = x.shape
            half = d // 2
            theta = BASE ** (-2.0 * jnp.arange(half, dtype=jnp.float32) / d)
            ang = jnp.arange(n, dtype=jnp.float32)[:, None] * theta[None, :]
            cos = jnp.cos(ang)[None, :, None, :]
            sin = jnp.sin(ang)[None, :, None, :]
            x1, x2 = (x[..., :half], x[..., half:])
            return jnp.concatenate([x1 * cos - x2 * sin, x1 * sin + x2 * cos], axis=-1)

        def _lightning_attn(q, k, v, log_lam):
            b, n, h, d = q.shape
            C = CHUNK
            nc = n // C
            qc = q.reshape(b, nc, C, h, d).transpose(1, 0, 2, 3, 4)
            kc = k.reshape(b, nc, C, h, d).transpose(1, 0, 2, 3, 4)
            vc = v.reshape(b, nc, C, h, d).transpose(1, 0, 2, 3, 4)
            i = jnp.arange(C, dtype=jnp.float32)
            diff = i[:, None] - i[None, :]
            D = jnp.where(diff[None] >= 0, jnp.exp(log_lam[:, None, None] * diff[None]), 0.0)
            decay_q = jnp.exp(log_lam[None, :] * (i[:, None] + 1.0))
            decay_k = jnp.exp(log_lam[None, :] * (C - 1.0 - i[:, None]))
            lam_C = jnp.exp(log_lam * C)

            def step(S, qkv):
                qi, ki, vi = qkv
                scores = jnp.einsum('bthd,bshd->bhts', qi, ki) * D[None]
                o_intra = jnp.einsum('bhts,bshd->bthd', scores, vi)
                o_inter = jnp.einsum('bthd,bhde->bthe', qi * decay_q[None, :, :, None], S)
                S_new = lam_C[None, :, None, None] * S + jnp.einsum('bshd,bshe->bhde', ki * decay_k[None, :, :, None], vi)
                return (S_new, o_intra + o_inter)
            S0 = jnp.zeros((b, h, d, d), q.dtype)
            _, o = jax.lax.scan(step, S0, (qc, kc, vc))
            return o.transpose(1, 0, 2, 3, 4).reshape(b, n, h, d)

        def _gated_group_rmsnorm(o, gate, weight):
            b, n, d = o.shape
            x = o * jax.nn.sigmoid(gate)
            xg = x.reshape(b, n, HEADS, HEAD_DIM)
            ms = jnp.mean(xg * xg, axis=-1, keepdims=True)
            xg = xg * jax.lax.rsqrt(ms + EPS)
            return xg.reshape(b, n, d) * weight
        key = jax.random.key(seed)
        ks = jax.random.split(key, 8)
        b, n, d = (2, 256, EMBED)
        std = 0.02
        return {'x': jax.random.normal(ks[0], (b, n, d), jnp.float32), 'Wq': jax.random.normal(ks[1], (d, d), jnp.float32) * std, 'Wk': jax.random.normal(ks[2], (d, d), jnp.float32) * std, 'Wv': jax.random.normal(ks[3], (d, d), jnp.float32) * std, 'Wo': jax.random.normal(ks[4], (d, d), jnp.float32) * std, 'Wg1': jax.random.normal(ks[5], (d, HEAD_DIM), jnp.float32) * std, 'Wg2': jax.random.normal(ks[6], (HEAD_DIM, d), jnp.float32) * std, 'norm_weight': jnp.ones((d,), jnp.float32)}
    _L1_attn_in = _L1_attn_setup()

    def _L1_ffn_setup():
        import jax, jax.numpy as jnp
        import numpy as np
        TOP_K = 6
        CAP_FACTOR = 2

        def _moe_block(x2d, wg_router, w_gate, w_up, w_down, ws_gate, ws_up, ws_down):
            T, D = x2d.shape
            E = wg_router.shape[0]
            scores = jax.nn.softmax(x2d @ wg_router.T, axis=-1)
            topk_w, topk_idx = jax.lax.top_k(scores, TOP_K)
            topk_w = topk_w / (jnp.sum(topk_w, axis=-1, keepdims=True) + 1e-20)
            flat_idx = topk_idx.reshape(-1)
            oh = jax.nn.one_hot(flat_idx, E, dtype=jnp.int32)
            pos = jnp.cumsum(oh, axis=0) - 1
            pos_in_e = jnp.take_along_axis(pos, flat_idx[:, None], axis=1)[:, 0]
            C = CAP_FACTOR * (T * TOP_K // E)
            valid = pos_in_e < C
            safe_pos = jnp.where(valid, pos_in_e, 0)
            tok_id = jnp.repeat(jnp.arange(T), TOP_K)
            vmask = valid[:, None].astype(x2d.dtype)
            x_rep = x2d[tok_id] * vmask
            xe = jnp.zeros((E, C, D), x2d.dtype).at[flat_idx, safe_pos].add(x_rep)
            g = jnp.einsum('ecd,edf->ecf', xe, w_gate)
            u = jnp.einsum('ecd,edf->ecf', xe, w_up)
            ye = jnp.einsum('ecf,efd->ecd', jax.nn.silu(g) * u, w_down)
            y_tok = ye[flat_idx, safe_pos] * vmask
            y = jnp.sum(y_tok.reshape(T, TOP_K, D) * topk_w[..., None], axis=1)
            sh = jax.nn.silu(x2d @ ws_gate) * (x2d @ ws_up) @ ws_down
            return y + sh
        key = jax.random.key(seed)
        ks = jax.random.split(key, 9)
        B, S, D, F, E = (1, 256, 256, 176, 32)
        FS = F * 2
        s = 0.02
        return {'hidden_states': jax.random.normal(ks[0], (B, S, D), jnp.float32), 'wg_router': jax.random.normal(ks[1], (E, D), jnp.float32) * s, 'w_gate': jax.random.normal(ks[2], (E, D, F), jnp.float32) * s, 'w_up': jax.random.normal(ks[3], (E, D, F), jnp.float32) * s, 'w_down': jax.random.normal(ks[4], (E, F, D), jnp.float32) * s, 'ws_gate': jax.random.normal(ks[5], (D, FS), jnp.float32) * s, 'ws_up': jax.random.normal(ks[6], (D, FS), jnp.float32) * s, 'ws_down': jax.random.normal(ks[7], (FS, D), jnp.float32) * s}
    _L1_ffn_in = _L1_ffn_setup()
    _d = {'L0_attn_inputs_q': _L0_attn_in['inputs_q'], 'L0_attn_wq': _L0_attn_in['wq'], 'L0_attn_bq': _L0_attn_in['bq'], 'L0_attn_wk': _L0_attn_in['wk'], 'L0_attn_bk': _L0_attn_in['bk'], 'L0_attn_wv': _L0_attn_in['wv'], 'L0_attn_bv': _L0_attn_in['bv'], 'L0_attn_wo': _L0_attn_in['wo'], 'L0_attn_bo': _L0_attn_in['bo'], 'L0_ffn_gate_w': _L0_ffn_in['gate_w'], 'L0_ffn_gate_bias': _L0_ffn_in['gate_bias'], 'L0_ffn_fc1_w': _L0_ffn_in['fc1_w'], 'L0_ffn_fc2_w': _L0_ffn_in['fc2_w'], 'L0_ffn_w1': _L0_ffn_in['w1'], 'L0_ffn_w2': _L0_ffn_in['w2'], 'L0_ffn_shared_up_w': _L0_ffn_in['shared_up_w'], 'L0_ffn_shared_down_w': _L0_ffn_in['shared_down_w'], 'L1_attn_Wq': _L1_attn_in['Wq'], 'L1_attn_Wk': _L1_attn_in['Wk'], 'L1_attn_Wv': _L1_attn_in['Wv'], 'L1_attn_Wo': _L1_attn_in['Wo'], 'L1_attn_Wg1': _L1_attn_in['Wg1'], 'L1_attn_Wg2': _L1_attn_in['Wg2'], 'L1_attn_norm_weight': _L1_attn_in['norm_weight'], 'L1_ffn_wg_router': _L1_ffn_in['wg_router'], 'L1_ffn_w_gate': _L1_ffn_in['w_gate'], 'L1_ffn_w_up': _L1_ffn_in['w_up'], 'L1_ffn_w_down': _L1_ffn_in['w_down'], 'L1_ffn_ws_gate': _L1_ffn_in['ws_gate'], 'L1_ffn_ws_up': _L1_ffn_in['ws_up'], 'L1_ffn_ws_down': _L1_ffn_in['ws_down']}
    _x0 = _d['L0_attn_inputs_q']
    _d['L0_attn_inputs_q'] = jax.random.normal(jax.random.fold_in(jax.random.key(seed), 1), (1, 1024, 256), dtype=_x0.dtype)
    del _x0
    return _d

def reference(L0_attn_inputs_q, L0_attn_wq, L0_attn_bq, L0_attn_wk, L0_attn_bk, L0_attn_wv, L0_attn_bv, L0_attn_wo, L0_attn_bo, L0_ffn_gate_w, L0_ffn_gate_bias, L0_ffn_fc1_w, L0_ffn_fc2_w, L0_ffn_w1, L0_ffn_w2, L0_ffn_shared_up_w, L0_ffn_shared_down_w, L1_attn_Wq, L1_attn_Wk, L1_attn_Wv, L1_attn_Wo, L1_attn_Wg1, L1_attn_Wg2, L1_attn_norm_weight, L1_ffn_wg_router, L1_ffn_w_gate, L1_ffn_w_up, L1_ffn_w_down, L1_ffn_ws_gate, L1_ffn_ws_up, L1_ffn_ws_down):

    def _L0_attn_ref(inputs_q, wq, bq, wk, bk, wv, bv, wo, bo):
        import jax, jax.numpy as jnp
        import numpy as np
        NUM_HEADS = 16
        NUM_KV_HEADS = 4
        HEAD_DIM = 128
        D_MODEL = 256
        B, S, _ = inputs_q.shape
        H, Hk, D = (NUM_HEADS, NUM_KV_HEADS, HEAD_DIM)
        G = H // Hk
        og_dtype = inputs_q.dtype
        xq = (inputs_q @ wq + bq).reshape(B, S, H, D)
        xk = (inputs_q @ wk + bk).reshape(B, S, Hk, D)
        xv = (inputs_q @ wv + bv).reshape(B, S, Hk, D)
        xq = xq.astype(jnp.float32)
        xk = xk.astype(jnp.float32)
        scale = 1.0 / np.sqrt(D)
        qg = (xq * scale).reshape(B, S, Hk, G, D)
        attn = jnp.einsum('bqhgd,bkhd->bhgqk', qg, xk)
        attn = jax.nn.softmax(attn.astype(jnp.float32), axis=-1).astype(xq.dtype)
        out = jnp.einsum('bhgqk,bkhd->bqhgd', attn.astype(xv.dtype), xv)
        out = out.astype(og_dtype).reshape(B, S, H * D)
        return out @ wo + bo

    def _L0_ffn_ref(hidden_states, gate_w, gate_bias, fc1_w, fc2_w, w1, w2, shared_up_w, shared_down_w):
        import jax, jax.numpy as jnp
        import numpy as np
        H, LAT, INTER, E, G, TOPK_G, TOP_K = (256, 128, 128, 32, 4, 2, 8)
        SHARED_INTER = 512
        ROUTED_SCALE = 2.5
        B, S = (2, 128)

        def relu2(x):
            return jnp.square(jax.nn.relu(x))
        orig_shape = hidden_states.shape
        x = hidden_states.reshape(-1, H)
        T = x.shape[0]
        logits = jnp.einsum('th,eh->te', x.astype(jnp.float32), gate_w)
        scores = jax.nn.sigmoid(logits)
        sb = scores + gate_bias
        grp = sb.reshape(T, G, E // G)
        group_scores = jax.lax.top_k(grp, 2)[0].sum(-1)
        _, gidx = jax.lax.top_k(group_scores, TOPK_G)
        gmask = jax.nn.one_hot(gidx, G, dtype=sb.dtype).sum(1)
        masked = jnp.where(gmask[:, :, None] > 0, grp, -jnp.inf).reshape(T, E)
        _, topi = jax.lax.top_k(masked, TOP_K)
        wsel = jnp.take_along_axis(scores, topi, axis=1)
        wsel = wsel / wsel.sum(-1, keepdims=True) * ROUTED_SCALE
        cw = jnp.zeros((T, E), jnp.float32).at[jnp.arange(T)[:, None], topi].add(wsel)
        x_lat = x @ fc1_w.T
        h = relu2(jnp.einsum('tl,eil->eti', x_lat, w1))
        h = h * cw.T[:, :, None]
        y_lat = jnp.einsum('eti,eli->tl', h, w2)
        routed = y_lat @ fc2_w.T
        shared = relu2(x @ shared_up_w.T) @ shared_down_w.T
        return (shared + routed).reshape(orig_shape)

    def _L1_attn_ref(x, Wq, Wk, Wv, Wo, Wg1, Wg2, norm_weight):
        import jax, jax.numpy as jnp
        import numpy as np
        EMBED = 256
        HEADS = 16
        HEAD_DIM = EMBED // HEADS
        CHUNK = 128
        BASE = 10000.0
        EPS = 1e-06

        def _alibi_log_decay(h):
            slopes = 2.0 ** (-8.0 * (jnp.arange(h, dtype=jnp.float32) + 1.0) / h)
            return -slopes

        def _lrpe_rotate(x):
            b, n, h, d = x.shape
            half = d // 2
            theta = BASE ** (-2.0 * jnp.arange(half, dtype=jnp.float32) / d)
            ang = jnp.arange(n, dtype=jnp.float32)[:, None] * theta[None, :]
            cos = jnp.cos(ang)[None, :, None, :]
            sin = jnp.sin(ang)[None, :, None, :]
            x1, x2 = (x[..., :half], x[..., half:])
            return jnp.concatenate([x1 * cos - x2 * sin, x1 * sin + x2 * cos], axis=-1)

        def _lightning_attn(q, k, v, log_lam):
            b, n, h, d = q.shape
            C = CHUNK
            nc = n // C
            qc = q.reshape(b, nc, C, h, d).transpose(1, 0, 2, 3, 4)
            kc = k.reshape(b, nc, C, h, d).transpose(1, 0, 2, 3, 4)
            vc = v.reshape(b, nc, C, h, d).transpose(1, 0, 2, 3, 4)
            i = jnp.arange(C, dtype=jnp.float32)
            diff = i[:, None] - i[None, :]
            D = jnp.where(diff[None] >= 0, jnp.exp(log_lam[:, None, None] * diff[None]), 0.0)
            decay_q = jnp.exp(log_lam[None, :] * (i[:, None] + 1.0))
            decay_k = jnp.exp(log_lam[None, :] * (C - 1.0 - i[:, None]))
            lam_C = jnp.exp(log_lam * C)

            def step(S, qkv):
                qi, ki, vi = qkv
                scores = jnp.einsum('bthd,bshd->bhts', qi, ki) * D[None]
                o_intra = jnp.einsum('bhts,bshd->bthd', scores, vi)
                o_inter = jnp.einsum('bthd,bhde->bthe', qi * decay_q[None, :, :, None], S)
                S_new = lam_C[None, :, None, None] * S + jnp.einsum('bshd,bshe->bhde', ki * decay_k[None, :, :, None], vi)
                return (S_new, o_intra + o_inter)
            S0 = jnp.zeros((b, h, d, d), q.dtype)
            _, o = jax.lax.scan(step, S0, (qc, kc, vc))
            return o.transpose(1, 0, 2, 3, 4).reshape(b, n, h, d)

        def _gated_group_rmsnorm(o, gate, weight):
            b, n, d = o.shape
            x = o * jax.nn.sigmoid(gate)
            xg = x.reshape(b, n, HEADS, HEAD_DIM)
            ms = jnp.mean(xg * xg, axis=-1, keepdims=True)
            xg = xg * jax.lax.rsqrt(ms + EPS)
            return xg.reshape(b, n, d) * weight
        b, n, d = x.shape
        q = (x @ Wq).reshape(b, n, HEADS, HEAD_DIM)
        k = (x @ Wk).reshape(b, n, HEADS, HEAD_DIM)
        v = (x @ Wv).reshape(b, n, HEADS, HEAD_DIM)
        q = jax.nn.silu(q)
        k = jax.nn.silu(k)
        q = _lrpe_rotate(q)
        k = _lrpe_rotate(k)
        log_lam = _alibi_log_decay(HEADS)
        o = _lightning_attn(q, k, v, log_lam).reshape(b, n, d)
        gate = x @ Wg1 @ Wg2
        o = _gated_group_rmsnorm(o, gate, norm_weight)
        return o @ Wo

    def _L1_ffn_ref(hidden_states, wg_router, w_gate, w_up, w_down, ws_gate, ws_up, ws_down):
        import jax, jax.numpy as jnp
        import numpy as np
        TOP_K = 6
        CAP_FACTOR = 2

        def _moe_block(x2d, wg_router, w_gate, w_up, w_down, ws_gate, ws_up, ws_down):
            T, D = x2d.shape
            E = wg_router.shape[0]
            scores = jax.nn.softmax(x2d @ wg_router.T, axis=-1)
            topk_w, topk_idx = jax.lax.top_k(scores, TOP_K)
            topk_w = topk_w / (jnp.sum(topk_w, axis=-1, keepdims=True) + 1e-20)
            flat_idx = topk_idx.reshape(-1)
            oh = jax.nn.one_hot(flat_idx, E, dtype=jnp.int32)
            pos = jnp.cumsum(oh, axis=0) - 1
            pos_in_e = jnp.take_along_axis(pos, flat_idx[:, None], axis=1)[:, 0]
            C = CAP_FACTOR * (T * TOP_K // E)
            valid = pos_in_e < C
            safe_pos = jnp.where(valid, pos_in_e, 0)
            tok_id = jnp.repeat(jnp.arange(T), TOP_K)
            vmask = valid[:, None].astype(x2d.dtype)
            x_rep = x2d[tok_id] * vmask
            xe = jnp.zeros((E, C, D), x2d.dtype).at[flat_idx, safe_pos].add(x_rep)
            g = jnp.einsum('ecd,edf->ecf', xe, w_gate)
            u = jnp.einsum('ecd,edf->ecf', xe, w_up)
            ye = jnp.einsum('ecf,efd->ecd', jax.nn.silu(g) * u, w_down)
            y_tok = ye[flat_idx, safe_pos] * vmask
            y = jnp.sum(y_tok.reshape(T, TOP_K, D) * topk_w[..., None], axis=1)
            sh = jax.nn.silu(x2d @ ws_gate) * (x2d @ ws_up) @ ws_down
            return y + sh
        B, S, D = hidden_states.shape
        x2d = hidden_states.reshape(-1, D)
        out = _moe_block(x2d, wg_router, w_gate, w_up, w_down, ws_gate, ws_up, ws_down)
        return out.reshape(B, S, D)
    x = L0_attn_inputs_q
    x = x + _L0_attn_ref(_layernorm(x, axis=-1), L0_attn_wq, L0_attn_bq, L0_attn_wk, L0_attn_bk, L0_attn_wv, L0_attn_bv, L0_attn_wo, L0_attn_bo)
    x = x + _L0_ffn_ref(_layernorm(x, axis=-1), L0_ffn_gate_w, L0_ffn_gate_bias, L0_ffn_fc1_w, L0_ffn_fc2_w, L0_ffn_w1, L0_ffn_w2, L0_ffn_shared_up_w, L0_ffn_shared_down_w)
    x = x + _L1_attn_ref(_layernorm(x, axis=-1), L1_attn_Wq, L1_attn_Wk, L1_attn_Wv, L1_attn_Wo, L1_attn_Wg1, L1_attn_Wg2, L1_attn_norm_weight)
    x = x + _L1_ffn_ref(_layernorm(x, axis=-1), L1_ffn_wg_router, L1_ffn_w_gate, L1_ffn_w_up, L1_ffn_w_down, L1_ffn_ws_gate, L1_ffn_ws_up, L1_ffn_ws_down)
    return x

_drawn_inputs = setup_inputs


def setup_inputs(seed=0):
    import zlib

    import numpy as np

    out = dict(_drawn_inputs(seed))
    spreads = {'L0_attn_bq': (0.0, 0.335),
     'L0_attn_bk': (0.0, 2.0),
     'L0_attn_bv': (0.0, 0.1),
     'L0_attn_bo': (0.0, 0.1),
     'L1_attn_norm_weight': (1.0, 0.6)}
    factors = {'L0_ffn_gate_w': 8.0,
     'L0_ffn_gate_bias': 8.0,
     'L0_ffn_fc1_w': 8.0,
     'L0_ffn_fc2_w': 8.0,
     'L0_ffn_w1': 8.0,
     'L0_ffn_w2': 8.0,
     'L1_attn_Wg1': 64.0,
     'L1_attn_Wg2': 64.0,
     'L1_ffn_wg_router': 8.0,
     'L1_ffn_w_gate': 21.367,
     'L1_ffn_w_up': 8.0,
     'L1_ffn_w_down': 8.0,
     'L1_ffn_ws_gate': 21.125,
     'L1_ffn_ws_up': 19.705,
     'L1_ffn_ws_down': 19.891,
     'L0_ffn_shared_up_w': 8.0,
     'L0_ffn_shared_down_w': 8.0,
     'L1_attn_Wq': 8.0,
     'L1_attn_Wk': 8.0,
     'L1_attn_Wv': 8.0,
     'L1_attn_Wo': 8.0}
    for name, (base, spread) in spreads.items():
        noise = np.random.default_rng([zlib.crc32(name.encode()), seed]).standard_normal(out[name].shape)
        drawn = base * np.exp(spread * noise) if base else spread * noise
        out[name] = jnp.asarray(drawn.astype(out[name].dtype))
    for name, factor in factors.items():
        out[name] = (out[name] * factor).astype(out[name].dtype)
    return out
```

```python
import numpy as np

import concourse.bass as bass
from concourse import mybir
from contextlib import ExitStack

F32 = mybir.dt.float32
F32R = mybir.dt.float32r
I32 = mybir.dt.int32
BF16 = mybir.dt.bfloat16
ALU = mybir.AluOpType
ACT = mybir.ActivationFunctionType
AX = mybir.AxisListType

P = 128
BANK = 512
T, D = 1024, 256
TT, DC = T // P, D // P
NB = T // BANK
LN_EPS = 1e-5


class Net:
    pass


def product(nc, out, lhs_h, lhs_l, rhs_h, rhs_l, start, stop):
    nc.tensor.matmul(out, lhs_h, rhs_h, start=start, stop=False)
    nc.tensor.matmul(out, lhs_h, rhs_l, start=False, stop=False)
    return nc.tensor.matmul(out, lhs_l, rhs_h, start=False, stop=stop)


def inverse_root(nc, dve, out, var, eps, a, s, done, n):
    nc.vector.tensor_scalar(a, var, eps, None, ALU.add).then_inc(done, 1)
    dve.wait_ge(done, n + 1)
    nc.vector.tensor_scalar(s.bitcast(I32), a.bitcast(I32), 1, None, ALU.logical_shift_right).then_inc(done, 1)
    dve.wait_ge(done, n + 2)
    nc.vector.tensor_scalar(out.bitcast(I32), s.bitcast(I32), -1.0, float(0x5F3759DF), ALU.mult, ALU.add).then_inc(done, 1)
    n += 3
    for _ in range(3):
        dve.wait_ge(done, n)
        nc.vector.scalar_tensor_tensor(s, out, -0.5, out, ALU.mult, ALU.mult).then_inc(done, 1)
        dve.wait_ge(done, n + 1)
        nc.vector.tensor_tensor(s, s, a, ALU.mult).then_inc(done, 1)
        dve.wait_ge(done, n + 2)
        nc.vector.scalar_tensor_tensor(out, s, 1.5, out, ALU.add, ALU.mult).then_inc(done, 1)
        n += 3
    return n


def norm_phase(nc, net, tag, add_delta, bias_row, normalise, keep_full, out):
    with ExitStack() as mem:
        sb = lambda n, s, d=F32: mem.enter_context(nc.sbuf_tensor(f"{tag}_{n}", s, d))
        x, delta, ps = net.x, net.delta, net.ps
        xc = sb("xc", [P, TT, D])
        bias = sb("bias", [P, D])
        stats = sb("stats", [P, TT, 6])
        moments = sb("moments", [P, TT, 2])
        rstd, root = sb("rstd", [P, TT]), sb("root", [P, 2, TT])
        (loaded, delta_turned, x_added, biased, stats_done, moments_done, rstd_done, xc_done, xc_turned, high_done,
         parts_done, full_done, stored) = net.norm_sems
        base = dict(net.norm_counts)

        def wait(eng, sem, n):
            eng.wait_ge(sem, base[sem.name] + n)

        pairs = TT // 2
        with nc.Block() as block:

            @block.sync
            def _(sp):
                if bias_row is not None:
                    sp.dma_start(bias[:, :], bias_row.partition_broadcast(P)).then_inc(loaded, 16)
                if not add_delta:
                    sp.dma_start(x[:, :, :], net.dram["x"].rearrange("(i p) d -> p i d", p=P)).then_inc(loaded, 16)
                    sp.dma_start(net.ident[:, :], net.dram["ident"]).then_inc(loaded, 16)
                if out is not None:
                    for j in range(pairs):
                        wait(sp, x_added, j + 1)
                        sp.dma_start(out.rearrange("(i p) d -> p i d", p=P)[:, 2 * j:2 * j + 2, :],
                                     x[:, 2 * j:2 * j + 2, :]).then_inc(stored, 16)
                    wait(sp, stored, 16 * pairs)

            @block.tensor
            def _(pe):
                if add_delta:
                    for j in range(pairs):
                        for k in range(2):
                            for c in range(DC):
                                i = 2 * j + k
                                last = nc.tensor.transpose(ps[:, j, k * D + c * P:k * D + (c + 1) * P],
                                                           delta[:, c, i * P:(i + 1) * P], net.ident[:, :])
                        last.then_inc(delta_turned, 1)
                if normalise:
                    if not add_delta:
                        wait(pe, loaded, 32)
                    for n in range(NB):
                        for k in range(4):
                            wait(pe, xc_done, 4 * n + k + 1)
                            for c in range(DC):
                                i = 4 * n + k
                                last = nc.tensor.transpose(ps[:, 4 + 2 * n + c, k * P:(k + 1) * P],
                                                           xc[:, i, c * P:(c + 1) * P], net.ident[:, :])
                        last.then_inc(xc_turned, 1)

            @block.vector
            def _(dve):
                if add_delta:
                    if bias_row is not None:
                        wait(dve, loaded, 16)
                        nc.vector.tensor_tensor(x[:, :, :], x[:, :, :], bias[:, :].unsqueeze(1).broadcast_to([P, TT, D]),
                                                ALU.add).then_inc(biased, 1)
                        wait(dve, biased, 1)
                    for j in range(pairs):
                        wait(dve, delta_turned, j + 1)
                        nc.vector.tensor_tensor(x[:, 2 * j:2 * j + 2, :], x[:, 2 * j:2 * j + 2, :],
                                                ps[:, j, :].rearrange("p (k d) -> p k d", k=2), ALU.add).then_inc(x_added, 1)
                else:
                    wait(dve, loaded, 32)
                if not normalise:
                    return
                for i in range(TT):
                    if add_delta:
                        wait(dve, x_added, i // 2 + 1)
                    nc.vector.bn_stats(stats[:, i, :], x[:, i, :]).then_inc(stats_done, 1)
                for i in range(TT):
                    wait(dve, stats_done, i + 1)
                    nc.vector.bn_aggr(moments[:, i, :], stats[:, i, :]).then_inc(moments_done, 1)
                wait(dve, moments_done, TT)
                n_rstd = inverse_root(nc, dve, rstd[:, :], moments[:, :, 1], LN_EPS, root[:, 0, :], root[:, 1, :], rstd_done, base[rstd_done.name])
                dve.wait_ge(rstd_done, n_rstd)
                for i in range(TT):
                    nc.vector.tensor_scalar(xc[:, i, :], x[:, i, :], moments[:, i, 0:1], rstd[:, i:i + 1],
                                            ALU.subtract, ALU.mult).then_inc(xc_done, 1)
                for n in range(NB):
                    for c in range(DC):
                        wait(dve, high_done, DC * n + c + 1)
                        nc.vector.tensor_tensor(net.xn_l[:, c, n * BANK:(n + 1) * BANK], ps[:, 4 + 2 * n + c, :],
                                                net.xn_h[:, c, n * BANK:(n + 1) * BANK].bitcast(F32), ALU.subtract).then_inc(parts_done, 1)
                wait(dve, parts_done, NB * DC)

            @block.scalar
            def _(act):
                if not normalise:
                    return
                for n in range(NB):
                    wait(act, xc_turned, n + 1)
                    for c in range(DC):
                        cols = slice(n * BANK, (n + 1) * BANK)
                        if keep_full:
                            nc.scalar.activation(net.xn[:, c, cols], ps[:, 4 + 2 * n + c, :], ACT.Copy).then_inc(full_done, 1)
                        nc.scalar.activation(net.xn_h[:, c, cols], ps[:, 4 + 2 * n + c, :], ACT.Copy).then_inc(high_done, 1)
                if keep_full:
                    wait(act, full_done, NB * DC)
                wait(act, high_done, NB * DC)

        for sem, count in ((loaded, 16 * ((bias_row is not None) + 2 * (not add_delta))), (delta_turned, pairs * add_delta),
                           (x_added, pairs * add_delta), (biased, add_delta and bias_row is not None),
                           (stats_done, TT * normalise), (moments_done, TT * normalise), (rstd_done, 12 * normalise),
                           (xc_done, TT * normalise), (xc_turned, NB * normalise), (high_done, NB * DC * normalise),
                           (parts_done, NB * DC * normalise), (full_done, NB * DC * keep_full),
                           (stored, 16 * pairs * (out is not None))):
            net.norm_counts[sem.name] += int(count)


HEADS, KV, DH = 16, 4, 128
PER = HEADS // KV
Q_SCALE = float(1.0 / np.sqrt(DH))


def softmax_attention_phase(nc, net):
    UNITS = PER * NB
    KT = TT
    STEPS = UNITS * KT
    TILES = UNITS * 4
    LAG = 4
    RING = 10
    GW = PER * DH

    jobs = [("k", 0), ("v", 0), ("q", 0)]
    for t in range(TILES):
        if (t + 3) % 8 == 0 and (t + 3) // 8 < PER:
            jobs.append(("q", (t + 3) // 8))
        jobs.append(("s", t))
    jobs += [("y", m) for m in range(DC)]
    assert len(jobs) % 2 == 0
    turn = {job: n for n, job in enumerate(jobs)}
    uses = len(jobs) // 2

    with ExitStack() as mem:
        sb = lambda n, s, d=F32: mem.enter_context(nc.sbuf_tensor(f"at_{n}", s, d))
        sem = lambda n: net.ctx.enter_context(nc.semaphore(f"at_{n}"))
        ps, xn_h, xn_l = net.ps, net.xn_h, net.xn_l
        w_raw = sb("w_raw", [P, 2 * GW + 4 * DH])
        wo_raw = sb("wo_raw", [P, PER, D])
        w_h, w_l = sb("w_h", [P, 2 * GW + 4 * DH], F32R), sb("w_l", [P, 2 * GW + 4 * DH], F32R)
        wo_h, wo_l = sb("wo_h", [P, PER, D], F32R), sb("wo_l", [P, PER, D], F32R)
        one = sb("one", [P, 1])
        bq, bk = sb("bq", [P, HEADS]), sb("bk", [P, KV])
        bv = sb("bv", [P, KV * DH])
        proj = sb("proj", [P, T])
        q_h, q_l = sb("q_h", [P, 2, T], F32R), sb("q_l", [P, 2, T], F32R)
        k_h, k_l = sb("k_h", [P, T], F32R), sb("k_l", [P, T], F32R)
        v_h, v_l = sb("v_h", [P, T], F32R), sb("v_l", [P, T], F32R)
        prob = sb("prob", [P, RING, T])
        pt_h, pt_l = sb("pt_h", [P, 2, BANK], F32R), sb("pt_l", [P, 2, BANK], F32R)
        o_h, o_l = sb("o_h", [P, PER, T], F32R), sb("o_l", [P, PER, T], F32R)
        neg_max, row_sum, inv_sum = sb("neg_max", [P, TILES]), sb("row_sum", [P, TILES]), sb("inv_sum", [P, TILES])

        def wq(part, c, hh):
            return part[:, c * GW + hh * DH:c * GW + (hh + 1) * DH]

        def wk(part, c):
            return part[:, 2 * GW + c * DH:2 * GW + (c + 1) * DH]

        def wv(part, c):
            return part[:, 2 * GW + (2 + c) * DH:2 * GW + (3 + c) * DH]

        def slot(job):
            s = 2 * (turn[job] % 2)
            return ps[:, s:s + 2, :]

        def turned(j):
            return ps[:, 4 + j % 2, :]

        def o_bank(u):
            return ps[:, 6 + u % 2, :]

        consts, w_loaded, wo_loaded = sem("consts"), sem("w_loaded"), sem("wo_loaded")
        bq_scaled, delta_zero = sem("bq_scaled"), sem("delta_zero")
        w_high, w_split, wo_split = sem("w_high"), sem("w_split"), sem("wo_split")
        slot_full = [sem("slot_full0"), sem("slot_full1")]
        slot_free = [sem("slot_free0"), sem("slot_free1")]
        projected, proj_high, proj_split = sem("projected"), sem("proj_high"), sem("proj_split")
        maxed, exped, inverted, normed = sem("maxed"), sem("exped"), sem("inverted"), sem("normed")
        pt_full, pt_high, pt_split, pv_done = sem("pt_full"), sem("pt_high"), sem("pt_split"), sem("pv_done")
        o_high, o_split, y_added = sem("o_high"), sem("o_split"), sem("y_added")

        def lift(eng, *sems):
            for s in sems:
                eng.sem_inc(s, 1)

        def is_full(eng, g, job):
            n = turn[job]
            eng.wait_ge(slot_full[n % 2], g * uses + n // 2 + 1)

        with nc.Block() as block:

            @block.sync
            def _(sp):
                sp.dma_start(bq[:, :], net.dram["bq"]).then_inc(consts, 16)
                sp.dma_start(bk[:, :], net.dram["bk"]).then_inc(consts, 16)
                sp.dma_start(bv[:, :], net.dram["bv"].partition_broadcast(P)).then_inc(consts, 16)
                with sp.Fori(0, KV) as g:
                    sp.wait_ge(w_split, 1 + g)
                    sp.dma_start(w_raw[:, 0:2 * GW].rearrange("p (c n) -> p c n", c=DC),
                                 net.dram["wq"][g]).then_inc(w_loaded, 16)
                    sp.dma_start(w_raw[:, 2 * GW:2 * GW + 2 * DH].rearrange("p (c n) -> p c n", c=DC),
                                 net.dram["wk"][g]).then_inc(w_loaded, 16)
                    sp.dma_start(w_raw[:, 2 * GW + 2 * DH:].rearrange("p (c n) -> p c n", c=DC),
                                 net.dram["wv"][g]).then_inc(w_loaded, 16)
                    sp.wait_ge(wo_split, 1 + g)
                    sp.dma_start(wo_raw[:, :, :], net.dram["wo"][g]).then_inc(wo_loaded, 16)

            @block.gpsimd
            def _(pool):
                nc.gpsimd.memset(net.delta[:, :, :], 0.0).then_inc(delta_zero, 1)
                nc.gpsimd.memset(one[:, :], 1.0).then_inc(delta_zero, 1)
                pool.wait_ge(delta_zero, 2)
                lift(pool, w_split, wo_split)
                with pool.Fori(0, KV) as g:
                    pool.wait_ge(w_loaded, 48 * (g + 1))
                    pool.wait_ge(proj_split, 1 + 6 * g)
                    nc.gpsimd.tensor_tensor(w_h[:, :], w_raw[:, :], one[:, :].broadcast_to([P, 2 * GW + 4 * DH]), ALU.mult).then_inc(w_high, 1)
                    pool.wait_ge(w_high, 2 * g + 1)
                    nc.gpsimd.tensor_tensor(w_l[:, :], w_raw[:, :], w_h[:, :].bitcast(F32), ALU.subtract).then_inc(w_split, 1)
                    pool.wait_ge(wo_loaded, 16 * (g + 1))
                    pool.wait_ge(y_added, 1 + DC * g)
                    nc.gpsimd.tensor_tensor(wo_h[:, :, :], wo_raw[:, :, :], one[:, :].unsqueeze(2).broadcast_to([P, PER, D]), ALU.mult).then_inc(w_high, 1)
                    pool.wait_ge(w_high, 2 * g + 2)
                    nc.gpsimd.tensor_tensor(wo_l[:, :, :], wo_raw[:, :, :], wo_h[:, :, :].bitcast(F32),
                                            ALU.subtract).then_inc(wo_split, 1)
                    for t in range(TILES):
                        pool.wait_ge(inverted, g * TILES + t + 1)
                        nc.gpsimd.tensor_tensor(prob[:, t % RING, :], prob[:, t % RING, :],
                                                inv_sum[:, t:t + 1].broadcast_to([P, T]), ALU.mult).then_inc(normed, 1)

            @block.tensor
            def _(pe):
                def begin(g, job):
                    n = turn[job]
                    pe.wait_ge(slot_free[n % 2], 1 + g * uses + n // 2)

                def project(g, job):
                    begin(g, job)
                    for n in range(NB):
                        for c in range(DC):
                            wt = (wk(w_h, c), wk(w_l, c)) if job[0] == "k" else (wq(w_h, c, job[1]), wq(w_l, c, job[1]))
                            cols = slice(n * BANK, (n + 1) * BANK)
                            last = product(nc, slot(job)[:, n, :], *wt, xn_h[:, c, cols], xn_l[:, c, cols],
                                           c == 0, c == DC - 1)
                    last.then_inc(slot_full[turn[job] % 2], 1)

                def project_values(g):
                    job = ("v", 0)
                    begin(g, job)
                    for i in range(TT):
                        to = slot(job)[:, i // 4, (i % 4) * P:(i % 4 + 1) * P]
                        for c in range(DC):
                            toks = slice(i * P, (i + 1) * P)
                            last = product(nc, to, xn_h[:, c, toks], xn_l[:, c, toks], wv(w_h, c), wv(w_l, c),
                                           c == 0, c == DC - 1)
                    last.then_inc(slot_full[turn[job] % 2], 1)

                def half_scores(g, s):
                    t, n = divmod(s, 2)
                    hh, i = divmod(t, TT)
                    if n == 0:
                        begin(g, ("s", t))
                        if i == 0:
                            pe.wait_ge(proj_split, 1 + 6 * g + 3 + hh)
                    keys = slice(n * BANK, (n + 1) * BANK)
                    last = product(nc, slot(("s", t))[:, n, :], q_h[:, hh % 2, i * P:(i + 1) * P],
                                   q_l[:, hh % 2, i * P:(i + 1) * P], k_h[:, keys], k_l[:, keys], True, True)
                    if n == 1:
                        last.then_inc(slot_full[turn["s", t] % 2], 1)

                def turn_probabilities(g, j):
                    u, kt = divmod(j, KT)
                    if kt == 0:
                        pe.wait_ge(normed, g * TILES + 4 * u + 4)
                    pe.wait_ge(pt_split, 1 + g * STEPS + max(j - 1, 0))
                    for i in range(4):
                        last = nc.tensor.transpose(turned(j)[:, i * P:(i + 1) * P],
                                                   prob[:, (4 * u + i) % RING, kt * P:(kt + 1) * P], net.ident[:, :])
                    last.then_inc(pt_full, 1)

                def weigh_values(g, j):
                    u, kt = divmod(j, KT)
                    if kt == 0:
                        pe.wait_ge(o_split, 1 + g * UNITS + max(u - 1, 0))
                    pe.wait_ge(pt_split, 1 + g * STEPS + j + 1)
                    keys = slice(kt * P, (kt + 1) * P)
                    product(nc, o_bank(u), v_h[:, keys], v_l[:, keys], pt_h[:, j % 2, :], pt_l[:, j % 2, :],
                            kt == 0, kt == KT - 1).then_inc(pv_done, 1)

                lift(pe, pt_full, pv_done)
                with pe.Fori(0, KV) as g:
                    pe.wait_ge(w_split, 1 + g + 1)
                    project(g, ("k", 0))
                    project_values(g)
                    project(g, ("q", 0))
                    for s in range(STEPS + KT + LAG):
                        if s % 2 == 0 and turn.get(("q", (s // 2 + 3) // 8)) is not None and (s // 2 + 3) % 8 == 0 and s < STEPS:
                            project(g, ("q", (s // 2 + 3) // 8))
                        j = s - KT - LAG
                        if 0 <= j + 1 < STEPS:
                            turn_probabilities(g, j + 1)
                        if s < STEPS:
                            half_scores(g, s)
                        if j >= 0:
                            weigh_values(g, j)
                    pe.wait_ge(wo_split, 1 + g + 1)
                    pe.wait_ge(o_split, 1 + UNITS * (g + 1))
                    for m in range(DC):
                        begin(g, ("y", m))
                        for n in range(NB):
                            cols = slice(n * BANK, (n + 1) * BANK)
                            for hh in range(PER):
                                last = product(nc, slot(("y", m))[:, n, :], wo_h[:, hh, m * P:(m + 1) * P],
                                               wo_l[:, hh, m * P:(m + 1) * P], o_h[:, hh, cols], o_l[:, hh, cols],
                                               hh == 0, hh == PER - 1)
                        last.then_inc(slot_full[turn["y", m] % 2], 1)

            @block.scalar
            def _(act):
                def add_bias(g, job, n):
                    is_full(act, g, job)
                    if n == 0:
                        act.wait_ge(proj_split, 1 + 6 * g)
                    else:
                        act.wait_ge(proj_split, 1 + 6 * g + n)
                    to = proj[:, :].rearrange("p (n t) -> p n t", n=NB)
                    if job[0] == "k":
                        ins = nc.scalar.activation(to, slot(job), ACT.Identity, bias=bk[:, bass.ds(g, 1)])
                    else:
                        ins = nc.scalar.activation(to, slot(job), ACT.Identity, bias=bq[:, bass.ds(g * PER + job[1], 1)],
                                                   scale=Q_SCALE)
                    ins.then_inc(projected, 1)

                def exp_scores(g, t):
                    act.wait_ge(maxed, g * TILES + t + 1)
                    if t < RING:
                        act.wait_ge(pt_full, 1 + g * STEPS)
                    else:
                        act.wait_ge(pt_full, 1 + g * STEPS + 8 * ((t - RING) // 4) + 8)
                    nc.scalar.activation(prob[:, t % RING, :].rearrange("p (n k) -> p n k", n=NB), slot(("s", t)), ACT.Exp,
                                         bias=neg_max[:, t:t + 1], accum_out=row_sum[:, t:t + 1]).then_inc(exped, 1)

                act.wait_ge(bq_scaled, 1)
                with act.Fori(0, KV) as g:
                    add_bias(g, ("k", 0), 0)
                    add_bias(g, ("q", 0), 2)
                    for s in range(STEPS + KT + LAG):
                        if s % 2 == 0 and (s // 2 + 3) % 8 == 0 and s < STEPS and (s // 2 + 3) // 8 < PER:
                            add_bias(g, ("q", (s // 2 + 3) // 8), 2 + (s // 2 + 3) // 8)
                        j = s - KT - LAG
                        if 0 <= j + 1 < STEPS:
                            act.wait_ge(pt_full, 1 + g * STEPS + j + 2)
                            act.wait_ge(pv_done, 1 + g * STEPS + max(j, 0))
                            nc.scalar.activation(pt_h[:, (j + 1) % 2, :], turned(j + 1), ACT.Copy).then_inc(pt_high, 1)
                        if s % 2 == 0 and 2 <= s <= STEPS:
                            exp_scores(g, s // 2 - 1)
                        if j >= 0 and j % KT == KT - 1:
                            u = j // KT
                            if u == 0:
                                act.wait_ge(y_added, 1 + DC * g)
                            act.wait_ge(pv_done, 1 + g * STEPS + j + 1)
                            nc.scalar.activation(o_h[:, u // NB, (u % NB) * BANK:(u % NB + 1) * BANK], o_bank(u),
                                                 ACT.Copy).then_inc(o_high, 1)

            @block.vector
            def _(dve):
                def split(g, n):
                    to_h, to_l = {0: (k_h[:, :], k_l[:, :]), 1: (v_h[:, :], v_l[:, :])}.get(
                        n, (q_h[:, (n - 2) % 2, :], q_l[:, (n - 2) % 2, :]))
                    nc.vector.tensor_copy(to_h, proj[:, :]).then_inc(proj_high, 1)
                    dve.wait_ge(proj_high, 6 * g + n + 1)
                    nc.vector.tensor_tensor(to_l, proj[:, :], to_h.bitcast(F32), ALU.subtract).then_inc(proj_split, 1)

                def free(job):
                    return slot_free[turn[job] % 2]

                def invert_sum(g, t):
                    dve.wait_ge(exped, g * TILES + t + 1)
                    nc.vector.reciprocal(inv_sum[:, t:t + 1], row_sum[:, t:t + 1]).then_inc(inverted, 1)
                    dve.sem_inc(free(("s", t)), 1)

                dve.wait_ge(consts, 48)
                nc.vector.tensor_scalar(bq[:, :], bq[:, :], Q_SCALE, None, ALU.mult).then_inc(bq_scaled, 1)
                dve.wait_ge(delta_zero, 1)
                lift(dve, proj_split, y_added, *slot_free, pt_split, o_split)
                with dve.Fori(0, KV) as g:
                    dve.wait_ge(projected, 6 * g + 1)
                    dve.sem_inc(free(("k", 0)), 1)
                    split(g, 0)
                    is_full(dve, g, ("v", 0))
                    dve.wait_ge(proj_split, 1 + 6 * g + 1)
                    nc.vector.tensor_tensor(proj[:, :].rearrange("p (i d) -> p i d", d=DH),
                                            slot(("v", 0)).rearrange("p n (i d) -> p (n i) d", d=DH),
                                            bv[:, bass.ds(g * DH, DH)].unsqueeze(1).broadcast_to([P, TT, DH]),
                                            ALU.add).then_inc(projected, 1)
                    dve.wait_ge(projected, 6 * g + 2)
                    dve.sem_inc(free(("v", 0)), 1)
                    split(g, 1)
                    dve.wait_ge(projected, 6 * g + 3)
                    dve.sem_inc(free(("q", 0)), 1)
                    split(g, 2)
                    for s in range(STEPS + KT + LAG):
                        if s % 2 == 0 and (s // 2 + 3) % 8 == 0 and s < STEPS and (s // 2 + 3) // 8 < PER:
                            hh = (s // 2 + 3) // 8
                            dve.wait_ge(projected, 6 * g + 3 + hh)
                            dve.sem_inc(free(("q", hh)), 1)
                            split(g, 2 + hh)
                        if s % 2 == 1 and 3 <= s <= STEPS + 1:
                            invert_sum(g, (s - 3) // 2)
                        j = s - KT - LAG
                        if 0 <= j + 1 < STEPS:
                            dve.wait_ge(pt_high, g * STEPS + j + 2)
                            nc.vector.tensor_tensor(pt_l[:, (j + 1) % 2, :], turned(j + 1), pt_h[:, (j + 1) % 2, :].bitcast(F32),
                                                    ALU.subtract).then_inc(pt_split, 1)
                        if s % 2 == 1 and s < STEPS:
                            t = s // 2
                            is_full(dve, g, ("s", t))
                            nc.vector.tensor_reduce(neg_max[:, t:t + 1], slot(("s", t)), AX.XY, ALU.max,
                                                    negate=True).then_inc(maxed, 1)
                        if j >= 0 and j % KT == KT - 1:
                            u = j // KT
                            dve.wait_ge(o_high, g * UNITS + u + 1)
                            cols = slice((u % NB) * BANK, (u % NB + 1) * BANK)
                            nc.vector.tensor_tensor(o_l[:, u // NB, cols], o_bank(u), o_h[:, u // NB, cols].bitcast(F32),
                                                    ALU.subtract).then_inc(o_split, 1)
                    for m in range(DC):
                        is_full(dve, g, ("y", m))
                        dve.wait_ge(y_added, 1 + DC * g)
                        nc.vector.tensor_tensor(net.delta[:, m, :].rearrange("p (n t) -> p n t", n=NB),
                                                net.delta[:, m, :].rearrange("p (n t) -> p n t", n=NB),
                                                slot(("y", m)), ALU.add).then_inc(y_added, 1)
                        dve.wait_ge(y_added, 1 + DC * g + m + 1)
                        dve.sem_inc(free(("y", m)), 1)
                        


EXP0, GROUPS, LAT, INTER, SHARED0 = 32, 4, 128, 128, 512
ROUTED_SCALE = 2.5
SH0 = SHARED0 // P
BIG, TAKEN = 1e30, 3e38


def squared_relu_experts_phase(nc, net):
    BODY, RAW, RING, ROWS = 8, 4, 4, 2
    SPLIT_LAG, DOWN_LAG, AHEAD = 2, 4, 2
    EG = EXP0 // GROUPS
    with ExitStack() as mem:
        sb = lambda n, s, d=F32: mem.enter_context(nc.sbuf_tensor(f"f0_{n}", s, d))
        sem = lambda n: net.ctx.enter_context(nc.semaphore(f"f0_{n}"))
        ps, xn, xn_h, xn_l = net.ps, net.xn, net.xn_h, net.xn_l
        gate, gate_bias = sb("gate", [P, DC, EXP0]), sb("gate_bias", [P, EXP0])
        FC1, UP, DOWN, FC2 = 0, DC * LAT, DC * (LAT + SHARED0), DC * (LAT + SHARED0) + SH0 * D
        w = sb("w", [P, FC2 + D])
        w_h, w_l = sb("w_h", [P, FC2 + D], F32R), sb("w_l", [P, FC2 + D], F32R)
        e_raw = sb("e_raw", [P, RAW, 2, P])
        e_h, e_l = sb("e_h", [P, BODY, 2, P], F32R), sb("e_l", [P, BODY, 2, P], F32R)
        lat_h, lat_l = sb("lat_h", [P, T], F32R), sb("lat_l", [P, T], F32R)
        relu, act = sb("relu", [P, 2, T]), sb("act", [P, RING, T])
        a_h, a_l = sb("a_h", [P, RING, T], F32R), sb("a_l", [P, RING, T], F32R)
        s_h, s_l = sb("s_h", [P, SH0, T], F32R), sb("s_l", [P, SH0, T], F32R)
        cw_row = sb("cw_row", [P, ROWS, T])
        score, biased = sb("score", [P, TT, EXP0]), sb("biased", [P, TT, EXP0])
        best, found = sb("best", [P, TT, GROUPS, 8]), sb("found", [P, TT, EXP0])
        g_score, g_out = sb("g_score", [P, TT, GROUPS + 6]), sb("g_out", [P, TT, GROUPS + 6])
        g_best, g_take = sb("g_best", [P, TT, 8]), sb("g_take", [P, TT, 8])
        cw, total = sb("cw", [P, TT, EXP0]), sb("total", [P, TT])
        cw_t = sb("cw_t", [EXP0, T])
        cw_dram = net.cw_dram[0]

        consts, w_loaded = sem("consts"), sem("w_loaded")
        w_high, w_split = sem("w_high"), sem("w_split")
        logits, scored, routed = sem("logits"), sem("scored"), sem("routed")
        cw_turned, cw_copied, cw_stored = sem("cw_turned"), sem("cw_copied"), sem("cw_stored")
        e_loaded = [sem(f"e_loaded{r}") for r in range(RAW)]
        row_loaded = [sem(f"row_loaded{r}") for r in range(ROWS)]
        e_high, e_split = sem("e_high"), sem("e_split")
        slot_full = sem("slot_full")
        lat_high, lat_split = sem("lat_high"), sem("lat_split")
        relued, squared, weighed = sem("relued"), sem("squared"), sem("weighed")
        act_high, act_split, down_done = sem("act_high"), sem("act_split"), sem("down_done")
        y_full, y_copied, chain = sem("y_full"), sem("y_copied"), sem("chain")

        def slot(n):
            return ps[:, 2 * (n % 2):2 * (n % 2) + 2, :]

        def blocks(ap):
            return ap.rearrange("p (n t) -> p n t", n=NB)

        def steps(eng, loop_end, last, step):
            for n in range(BODY):
                step(0, n)
            with eng.Fori(1, loop_end) as it:
                for r in range(BODY):
                    step(it, r)
            for n in range(loop_end * BODY, last):
                step(*divmod(n, BODY))

        def known(it, r, low, high=EXP0 + BODY):
            return not isinstance(it, int) or low <= it * BODY + r < high

        with nc.Block() as block:

            @block.sync
            def _(sp):
                sp.dma_start(gate[:, :, :], net.dram["gate0"]).then_inc(consts, 16)
                sp.dma_start(gate_bias[:, :], net.dram["gate_bias"].partition_broadcast(P)).then_inc(consts, 16)
                for name, at, end in (("fc1", FC1, UP), ("sup0", UP, DOWN), ("sdn0", DOWN, FC2), ("fc2", FC2, FC2 + D)):
                    sp.dma_start(w[:, at:end], net.dram[name]).then_inc(w_loaded, 16)

                def load_expert(it, r):
                    n = it * BODY + r
                    if known(it, r, RAW):
                        sp.wait_ge(e_split, n - RAW + 1)
                    sp.dma_start(e_raw[:, r % RAW, :, :], net.dram["we0"][n]).then_inc(e_loaded[r % RAW], 16)

                def load_row(it, r):
                    n = it * BODY + r
                    if known(it, r, ROWS):
                        sp.wait_ge(weighed, n - ROWS + 1)
                    sp.dma_start(cw_row[:, r % ROWS, :], cw_dram[n].partition_broadcast(P))\
                        .then_inc(row_loaded[r % ROWS], 16)

                for r in range(RAW):
                    load_expert(0, r)
                sp.wait_ge(cw_copied, 1)
                sp.dma_start(cw_dram, cw_t[:, :]).then_inc(cw_stored, 16)
                sp.wait_ge(cw_stored, 16)

                def step(it, r):
                    load_row(it, r)
                    if known(it, r, 0, EXP0 - RAW):
                        load_expert(it, r + RAW)

                steps(sp, EXP0 // BODY - 1, EXP0, step)

            @block.tensor
            def _(pe):
                pe.wait_ge(consts, 34)
                for i in range(TT):
                    for c in range(DC):
                        last = nc.tensor.matmul(ps[:, 6, i * EXP0:(i + 1) * EXP0], xn[:, c, i * P:(i + 1) * P],
                                                gate[:, c, :], start=c == 0, stop=c == DC - 1)
                last.then_inc(logits, 1)

                def project(n, at, width, k):
                    for b in range(NB):
                        cols = slice(b * BANK, (b + 1) * BANK)
                        for c in range(DC):
                            part = slice(at + c * width + k * P, at + c * width + (k + 1) * P)
                            last = product(nc, slot(n)[:, b, :], w_h[:, part], w_l[:, part], xn_h[:, c, cols],
                                           xn_l[:, c, cols], c == 0, c == DC - 1)
                    last.then_inc(slot_full, 1)

                pe.wait_ge(w_split, 1)
                project(0, FC1, LAT, 0)
                for k in range(SH0):
                    if k == 1:
                        pe.wait_ge(lat_split, 1)
                    if k > 1:
                        pe.wait_ge(squared, k - 1)
                    project(1 + k, UP, SHARED0, k)
                pe.wait_ge(routed, 1)
                for i in range(TT):
                    last = nc.tensor.transpose(ps[0:EXP0, 6 + i // 4, (i % 4) * P:(i % 4 + 1) * P], cw[:, i, :], net.ident[:, :])
                last.then_inc(cw_turned, 1)

                def step(it, r):
                    n = it * BODY + r
                    if known(it, r, 0, EXP0):
                        pe.wait_ge(e_split, n + 1)
                        pe.wait_ge(squared, n + SH0 - 1)
                        for b in range(NB):
                            cols = slice(b * BANK, (b + 1) * BANK)
                            last = product(nc, slot(1 + SH0 + r)[:, b, :], e_h[:, r, 0, :], e_l[:, r, 0, :],
                                           lat_h[:, cols], lat_l[:, cols], True, True)
                        last.then_inc(slot_full, 1)
                    if known(it, r, DOWN_LAG):
                        m = (r - DOWN_LAG) % BODY
                        pe.wait_ge(act_split, n - DOWN_LAG + 1 + SH0)
                        first = it == 0 and r == DOWN_LAG if isinstance(it, int) else False
                        final = n == EXP0 - 1 + DOWN_LAG if isinstance(it, int) else False
                        for b in range(NB):
                            cols = slice(b * BANK, (b + 1) * BANK)
                            last = product(nc, ps[:, 4 + b, :], e_h[:, m, 1, :], e_l[:, m, 1, :], a_h[:, m % RING, cols],
                                           a_l[:, m % RING, cols], first, final)
                        last.then_inc(down_done, 1)

                steps(pe, EXP0 // BODY, EXP0 + DOWN_LAG, step)
                pe.wait_ge(squared, SH0 + EXP0)
                for m in range(DC):
                    for b in range(NB):
                        cols = slice(b * BANK, (b + 1) * BANK)
                        for k in range(SH0):
                            part = slice(DOWN + k * D + m * P, DOWN + k * D + (m + 1) * P)
                            product(nc, ps[:, 2 * m + b, :], w_h[:, part], w_l[:, part], s_h[:, k, cols], s_l[:, k, cols],
                                    k == 0, False)
                pe.wait_ge(lat_split, 2)
                for m in range(DC):
                    for b in range(NB):
                        cols = slice(b * BANK, (b + 1) * BANK)
                        part = slice(FC2 + m * P, FC2 + (m + 1) * P)
                        last = product(nc, ps[:, 2 * m + b, :], w_h[:, part], w_l[:, part], lat_h[:, cols], lat_l[:, cols],
                                       False, True)
                    last.then_inc(y_full, 1)

            @block.scalar
            def _(act_e):
                act_e.wait_ge(w_loaded, 64)
                nc.scalar.activation(w_h[:, :], w[:, :], ACT.Copy).then_inc(w_high, 1)
                act_e.wait_ge(logits, 1)
                nc.scalar.activation(score[:, :, :], ps[:, 6, 0:TT * EXP0].rearrange("p (i e) -> p i e", e=EXP0),
                                     ACT.Sigmoid).then_inc(scored, 1)
                act_e.wait_ge(slot_full, 1)
                nc.scalar.activation(blocks(lat_h[:, :]), slot(0), ACT.Copy).then_inc(lat_high, 1)

                def relu_slot(n, k):
                    act_e.wait_ge(slot_full, n + 2)
                    if not isinstance(n, int) or n >= 2:
                        act_e.wait_ge(squared, n - 1)
                    nc.scalar.activation(blocks(relu[:, k % 2, :]), slot(1 + k), ACT.Relu).then_inc(relued, 1)

                def high_weights(it, r):
                    act_e.wait_ge(e_loaded[r % RAW], 16 * (it * (BODY // RAW) + r // RAW) + 16)
                    if known(it, r, BODY):
                        act_e.wait_ge(down_done, it * BODY + (r - BODY + 1))
                    nc.scalar.activation(e_h[:, r % BODY, :, :], e_raw[:, r % RAW, :, :], ACT.Copy).then_inc(e_high, 1)

                for k in range(SH0):
                    relu_slot(k, k)
                    act_e.wait_ge(squared, k + 1)
                    nc.scalar.activation(s_h[:, k, :], act[:, k % RING, :], ACT.Copy).then_inc(act_high, 1)
                for r in range(AHEAD):
                    high_weights(0, r)

                def step(it, r):
                    n = it * BODY + r
                    if known(it, r, 0, EXP0):
                        relu_slot(n + SH0, r + SH0)
                    if known(it, r, 0, EXP0 - AHEAD):
                        high_weights(it, r + AHEAD)
                    if known(it, r, SPLIT_LAG):
                        m = (r - SPLIT_LAG) % RING
                        act_e.wait_ge(weighed, n - SPLIT_LAG + 1)
                        if known(it, r, SPLIT_LAG + RING):
                            act_e.wait_ge(down_done, n - SPLIT_LAG - RING + 1)
                        nc.scalar.activation(a_h[:, m, :], act[:, m, :], ACT.Copy).then_inc(act_high, 1)

                steps(act_e, EXP0 // BODY - 1, EXP0 + SPLIT_LAG, step)
                act_e.wait_ge(down_done, EXP0)
                nc.scalar.activation(blocks(lat_h[:, :]), ps[:, 4:6, :], ACT.Copy).then_inc(lat_high, 1)
                act_e.wait_ge(y_full, 1)
                nc.scalar.activation(blocks(net.delta[:, 0, :]), ps[:, 0:2, :], ACT.Copy).then_inc(y_copied, 1)

            @block.gpsimd
            def _(pool):
                nc.gpsimd.memset(g_score[:, :, :], -BIG).then_inc(consts, 1)
                nc.gpsimd.memset(g_take[:, :, :], -BIG).then_inc(consts, 1)

                def step(it, r):
                    pool.wait_ge(row_loaded[r % ROWS], 16 * (it * (BODY // ROWS) + r // ROWS) + 16)
                    pool.wait_ge(squared, it * BODY + r + SH0 + 1)
                    nc.gpsimd.tensor_tensor(act[:, r % RING, :], act[:, r % RING, :], cw_row[:, r % ROWS, :],
                                            ALU.mult).then_inc(weighed, 1)

                steps(pool, EXP0 // BODY, EXP0, step)

            @block.vector
            def _(dve):
                links = [0]

                def link(ins):
                    ins.then_inc(chain, 1)
                    links[0] += 1
                    dve.wait_ge(chain, links[0])

                dve.wait_ge(w_high, 1)
                nc.vector.tensor_tensor(w_l[:, :], w[:, :], w_h[:, :].bitcast(F32), ALU.subtract).then_inc(w_split, 1)
                dve.wait_ge(consts, 34)
                dve.wait_ge(scored, 1)
                link(nc.vector.tensor_tensor(biased[:, :, :], score[:, :, :],
                                             gate_bias[:, :].unsqueeze(1).broadcast_to([P, TT, EXP0]), ALU.add))
                for i in range(TT):
                    for g in range(GROUPS):
                        last = nc.vector.max(best[:, i, g, :], biased[:, i, g * EG:(g + 1) * EG])
                link(last)
                dve.wait_ge(lat_high, 1)
                nc.vector.tensor_tensor(blocks(lat_l[:, :]), slot(0), blocks(lat_h[:, :]).bitcast(F32),
                                        ALU.subtract).then_inc(lat_split, 1)

                def square(n, k):
                    if not isinstance(n, int) or n >= RING:
                        dve.wait_ge(act_split, n - RING + 1)
                    dve.wait_ge(relued, n + 1)
                    nc.vector.scalar_tensor_tensor(blocks(act[:, k % RING, :]), slot(1 + k), 0.0, blocks(relu[:, k % 2, :]),
                                                   ALU.max, ALU.mult).then_inc(squared, 1)

                def split_shared(k):
                    dve.wait_ge(act_high, k + 1)
                    nc.vector.tensor_tensor(s_l[:, k, :], act[:, k % RING, :], s_h[:, k, :].bitcast(F32),
                                            ALU.subtract).then_inc(act_split, 1)

                link(nc.vector.tensor_tensor(g_score[:, :, 0:GROUPS], best[:, :, :, 0], best[:, :, :, 1], ALU.add))
                square(0, 0)
                for i in range(TT):
                    last = nc.vector.max(g_best[:, i, :], g_score[:, i, 0:8])
                link(last)
                link(nc.vector.tensor_copy(g_take[:, :, 0:2], g_best[:, :, 0:2]))
                split_shared(0)
                square(1, 1)
                for i in range(TT):
                    last = nc.vector.match_replace(g_out[:, i, :], g_take[:, i, :], g_score[:, i, :], TAKEN)
                link(last)
                link(nc.vector.tensor_scalar(g_out[:, :, :], g_out[:, :, :], TAKEN, None, ALU.is_equal))
                link(nc.vector.tensor_scalar(g_out[:, :, :], g_out[:, :, :], 1.0, BIG, ALU.subtract, ALU.mult))
                link(nc.vector.tensor_tensor(biased[:, :, :].rearrange("p i (g e) -> p i g e", g=GROUPS),
                                             biased[:, :, :].rearrange("p i (g e) -> p i g e", g=GROUPS),
                                             g_out[:, :, 0:GROUPS].unsqueeze(3).broadcast_to([P, TT, GROUPS, EG]), ALU.add))
                split_shared(1)
                square(2, 2)
                for i in range(TT):
                    last = nc.vector.max(g_best[:, i, :], biased[:, i, :])
                link(last)
                for i in range(TT):
                    last = nc.vector.match_replace(found[:, i, :], g_best[:, i, :], biased[:, i, :], TAKEN)
                link(last)
                link(nc.vector.scalar_tensor_tensor(cw[:, :, :], found[:, :, :], TAKEN, score[:, :, :], ALU.is_equal, ALU.mult))
                link(nc.vector.tensor_reduce(total[:, :], cw[:, :, :], AX.X, ALU.add))
                link(nc.vector.reciprocal(total[:, :], total[:, :]))
                nc.vector.scalar_tensor_tensor(cw[:, :, :], cw[:, :, :], ROUTED_SCALE,
                                               total[:, :].unsqueeze(2).broadcast_to([P, TT, EXP0]), ALU.mult, ALU.mult)\
                    .then_inc(routed, 1)
                split_shared(2)
                square(3, 3)
                split_shared(3)
                dve.wait_ge(cw_turned, 1)
                nc.vector.tensor_copy(blocks(cw_t[:, :]), ps[0:EXP0, 6:8, :]).then_inc(cw_copied, 1)

                def low_weights(it, r):
                    dve.wait_ge(e_high, it * BODY + r + 1)
                    nc.vector.tensor_tensor(e_l[:, r % BODY, :, :], e_raw[:, r % RAW, :, :], e_h[:, r % BODY, :, :].bitcast(F32),
                                            ALU.subtract).then_inc(e_split, 1)

                for r in range(AHEAD):
                    low_weights(0, r)

                def step(it, r):
                    n = it * BODY + r
                    if known(it, r, 0, EXP0):
                        square(n + SH0, r + SH0)
                    if known(it, r, 0, EXP0 - AHEAD):
                        low_weights(it, r + AHEAD)
                    if known(it, r, SPLIT_LAG):
                        m = (r - SPLIT_LAG) % RING
                        dve.wait_ge(act_high, n - SPLIT_LAG + 1 + SH0)
                        nc.vector.tensor_tensor(a_l[:, m, :], act[:, m, :], a_h[:, m, :].bitcast(F32),
                                                ALU.subtract).then_inc(act_split, 1)

                steps(dve, EXP0 // BODY - 1, EXP0 + SPLIT_LAG, step)
                dve.wait_ge(lat_high, 2)
                nc.vector.tensor_tensor(blocks(lat_l[:, :]), ps[:, 4:6, :], blocks(lat_h[:, :]).bitcast(F32),
                                        ALU.subtract).then_inc(lat_split, 1)
                dve.wait_ge(y_full, 2)
                nc.vector.tensor_copy(blocks(net.delta[:, 1, :]), ps[:, 2:4, :]).then_inc(y_copied, 1)
                dve.wait_ge(y_copied, 2)


H1, HD, CHUNK = 16, 16, 128
ROPE_BASE, RMS_EPS = 10000.0, 1e-6


def decay_tables():
    half = HD // 2
    theta = ROPE_BASE ** (-2.0 * np.arange(half, dtype=np.float32) / HD)
    angle = (np.arange(T, dtype=np.float32)[:, None] * theta.astype(np.float32)[None, :]).astype(np.float32)
    cos, sin = np.cos(angle), np.sin(angle)
    by_tile = lambda a: a.reshape(TT, P, -1).transpose(1, 0, 2)
    log_lam = -(2.0 ** (-8.0 * (np.arange(H1, dtype=np.float32) + 1.0) / H1))
    at = np.arange(CHUNK, dtype=np.float32)
    diff = at[None, :] - at[:, None]
    decay = np.where(diff[:, None, :] >= 0, np.exp(np.minimum(log_lam[None, :, None] * diff[:, None, :], 0)), 0)
    head = np.arange(P) // HD
    return {
        "cos": by_tile(np.concatenate([cos, cos], 1)), "sin": by_tile(np.concatenate([-sin, sin], 1)),
        "decay": decay,
        "decay_q": np.exp(log_lam[None, :] * (at[:, None] + 1)),
        "decay_k": np.exp(log_lam[None, :] * (CHUNK - 1 - at[:, None])),
        "lam_c": np.exp(log_lam.reshape(DC, P // HD)[:, head].T * CHUNK),
        "same_head": (head[:, None] == head[None, :]) * 1.0,
        "in_pair": (head[:, None] % 2 == np.arange(2)[None, :]) * 1.0,
    }


def linear_attention_phase(nc, net):
    QK, VG = 2 * D, D + HD
    W = QK + VG
    PAIRS = P // 32
    with ExitStack() as mem:
        sb = lambda n, s, d=F32: mem.enter_context(nc.sbuf_tensor(f"la_{n}", s, d))
        sem = lambda n: net.ctx.enter_context(nc.semaphore(f"la_{n}"))
        ps, xn_h, xn_l = net.ps, net.xn_h, net.xn_l
        w, w_h, w_l = sb("w", [P, DC, W]), sb("w_h", [P, DC, W], F32R), sb("w_l", [P, DC, W], F32R)
        wo, wo_h, wo_l = sb("wo", [P, DC, D]), sb("wo_h", [P, DC, D], F32R), sb("wo_l", [P, DC, D], F32R)
        wg2, weight = sb("wg2", [HD, D]), sb("weight", [P, D])
        cos, sin = sb("cos", [P, TT, HD]), sb("sin", [P, TT, HD])
        decay = sb("decay", [P, H1, CHUNK])
        decay_q, decay_k = sb("decay_q", [P, H1]), sb("decay_k", [P, H1])
        lam_c, same_head, in_pair = sb("lam_c", [P, DC]), sb("same_head", [P, P]), sb("in_pair", [P, 2])
        act = sb("act", [P, 2, QK])
        by_cos, by_sin = sb("by_cos", [P, 2, QK]), sb("by_sin", [P, 2, QK])
        rot = sb("rot", [P, 2, QK])
        v, g1 = sb("v", [P, TT, D]), sb("g1", [P, TT, HD])
        kd = sb("kd", [P, 4, D])
        q_t = sb("q_t", [P, 4, DC, P])
        qp_h, qp_l = sb("qp_h", [P, 2, DC, 2, P], F32R), sb("qp_l", [P, 2, DC, 2, P], F32R)
        k_h, k_l = sb("k_h", [P, 2, DC, P], F32R), sb("k_l", [P, 2, DC, P], F32R)
        sc = sb("sc", [P, 2, H1, CHUNK])
        state, kv = sb("state", [P, DC, P]), sb("kv", [P, DC, P])
        inter = sb("inter", [P, 2, D])
        o, gate, sq = sb("o", [P, TT, D]), sb("gate", [P, TT, D]), sb("sq", [P, TT, D])
        g1_t = sb("g1_t", [HD, T])
        ms, rms, root = sb("ms", [P, TT, H1]), sb("rms", [P, TT, H1]), sb("root", [P, 2, TT * H1])
        o_h, o_l = sb("o_h", [P, DC, T], F32R), sb("o_l", [P, DC, T], F32R)

        w_loaded, consts = sem("w_loaded"), sem("consts")
        w_high, w_split = sem("w_high"), sem("w_split")
        projected, act_done, v_done = sem("projected"), sem("act_done"), sem("v_done")
        cos_done, sin_done, rotated, kd_done = sem("cos_done"), sem("sin_done"), sem("rotated"), sem("kd_done")
        turned, t_high, t_split = sem("turned"), sem("t_high"), sem("t_split")
        sc_full, sc_done = sem("sc_full"), sem("sc_done")
        out_full, kv_masked, state_done = sem("out_full"), sem("kv_masked"), sem("state_done")
        inter_done, o_done = sem("inter_done"), sem("o_done")
        g1_turned, g1_copied, gate_full, gate_done = sem("g1_turned"), sem("g1_copied"), sem("gate_full"), sem("gate_done")
        gated, squares, weighted, chain = sem("gated"), sem("squares"), sem("weighted"), sem("chain")
        o_turned, o_high, o_split = sem("o_turned"), sem("o_high"), sem("o_split")
        y_full, y_copied = sem("y_full"), sem("y_copied")

        SCORE_BANKS = [5, 6, 7, 4]
        STEPS = TT + 3
        HALF = TT // 2

        def heads(ap):
            return ap.rearrange("p (h e) -> p h e", e=HD)

        def of_pair(ap, r):
            return ap.rearrange("p (c r j) t -> p c r (j t)", c=DC, j=2)[:, :, r, :]

        with nc.Block() as block:

            @block.sync
            def _(sp):
                sp.dma_start(w[:, :, :], net.dram["w1a"]).then_inc(w_loaded, 16)
                sp.dma_start(wo[:, :, :], net.dram["wo1"]).then_inc(w_loaded, 16)
                for to, name in ((cos[:, :, :], "cos"), (sin[:, :, :], "sin"), (decay_k[:, :], "decay_k"),
                                 (in_pair[:, :], "in_pair"), (decay[:, :, :], "decay"), (decay_q[:, :], "decay_q"),
                                 (lam_c[:, :], "lam_c"), (same_head[:, :], "same_head"), (wg2[:, :], "wg2")):
                    sp.dma_start(to, net.dram[name]).then_inc(consts, 16)
                sp.dma_start(weight[:, :], net.dram["norm_weight"].partition_broadcast(P)).then_inc(consts, 16)

            @block.gpsimd
            def _(pool):
                nc.gpsimd.memset(state[:, :, :], 0.0).then_inc(state_done, 1)
                pool.wait_ge(consts, 160)
                for n in range(TT):
                    a = act[:, n % 2, :].rearrange("p (h j e) -> p h j e", j=2, e=HD // 2)
                    b = by_sin[:, n % 2, :].rearrange("p (h j e) -> p h j e", j=2, e=HD // 2)
                    s = sin[:, n, :].rearrange("p (j e) -> p j e", j=2)
                    pool.wait_ge(act_done, n + 1)
                    if n >= 2:
                        pool.wait_ge(rotated, n - 1)
                    for j in range(2):
                        nc.gpsimd.tensor_tensor(b[:, :, j, :], a[:, :, 1 - j, :],
                                                s[:, j, :].unsqueeze(1).broadcast_to([P, 2 * H1, HD // 2]), ALU.mult)\
                            .then_inc(sin_done, 1)
                    pool.wait_ge(rotated, n + 1)
                    if n >= 4:
                        pool.wait_ge(out_full, n - 3)
                    nc.gpsimd.tensor_tensor(heads(kd[:, n % 4, :]), heads(rot[:, n % 2, D:]),
                                            decay_k[:, :].unsqueeze(2).broadcast_to([P, H1, HD]), ALU.mult).then_inc(kd_done, 1)
                for half in range(2):
                    part = slice(half * HALF, (half + 1) * HALF)
                    pool.wait_ge(gated, half + 1)
                    nc.gpsimd.tensor_tensor(sq[:, part, :], o[:, part, :], o[:, part, :], ALU.mult).then_inc(squares, 1)

            @block.tensor
            def _(pe):
                def projections(n):
                    toks = slice(n * P, (n + 1) * P)
                    if n:
                        pe.wait_ge(act_done, n)
                        pe.wait_ge(v_done, n)
                    for bank, cols in ((0, slice(0, QK)), (1, slice(QK, W))):
                        for c in range(DC):
                            last = product(nc, ps[:, bank, 0:cols.stop - cols.start], xn_h[:, c, toks], xn_l[:, c, toks],
                                           w_h[:, c, cols], w_l[:, c, cols], c == 0, c == DC - 1)
                    last.then_inc(projected, 1)

                def transposes(n):
                    pe.wait_ge(rotated, n + 1)
                    if n:
                        pe.wait_ge(t_split, n)
                    for b in range(2 * DC):
                        last = nc.tensor.transpose(ps[:, 2, b * P:(b + 1) * P], rot[:, n % 2, b * P:(b + 1) * P], net.ident[:, :])
                    last.then_inc(turned, 1)

                def scores(n):
                    pe.wait_ge(t_split, n + 1)
                    if n:
                        pe.wait_ge(sc_done, PAIRS * n)
                    for c in range(DC):
                        for r in range(PAIRS):
                            rows = slice(32 * r, 32 * (r + 1))
                            if c == 0 and r == PAIRS - 1 and n:
                                pe.wait_ge(o_done, n)
                            last = product(nc, ps[:, SCORE_BANKS[r], c * 2 * P:(c + 1) * 2 * P], k_h[rows, n % 2, c, :],
                                           k_l[rows, n % 2, c, :], qp_h[rows, n % 2, c, :, :].rearrange("p j t -> p (j t)"),
                                           qp_l[rows, n % 2, c, :, :].rearrange("p j t -> p (j t)"), True, True)
                            if c == DC - 1:
                                last.then_inc(sc_full, 1)

                def outputs(n):
                    pe.wait_ge(kd_done, n + 1)
                    pe.wait_ge(state_done, n + 1)
                    if n:
                        pe.wait_ge(inter_done, n)
                    for c in range(DC):
                        nc.tensor.matmul(ps[:, 3, c * P:(c + 1) * P], kd[:, n % 4, c * P:(c + 1) * P],
                                         v[:, n, c * P:(c + 1) * P], start=True, stop=True)
                    for c in range(DC):
                        nc.tensor.matmul(ps[:, 3, D + c * P:D + (c + 1) * P], q_t[:, n % 4, c, :], state[:, c, :],
                                         start=True, stop=True)
                    pe.wait_ge(sc_done, PAIRS * (n + 1))
                    for h in range(H1):
                        last = nc.tensor.matmul(ps[:, 4, h * HD:(h + 1) * HD], sc[:, n % 2, h, :],
                                                v[:, n, h * HD:(h + 1) * HD], start=True, stop=True)
                    last.then_inc(out_full, 1)

                pe.wait_ge(w_split, 1)
                for n in range(STEPS):
                    if n < TT:
                        projections(n)
                    if 0 <= n - 1 < TT:
                        transposes(n - 1)
                    if n == TT:
                        pe.wait_ge(act_done, TT)
                        pe.wait_ge(v_done, TT)
                        for i in range(TT):
                            last = nc.tensor.transpose(ps[0:HD, i // 4, (i % 4) * P:(i % 4 + 1) * P], g1[:, i, :], net.ident[:, :])
                        last.then_inc(g1_turned, 1)
                    if n - 3 >= 0:
                        outputs(n - 3)
                    if 0 <= n - 2 < TT:
                        scores(n - 2)
                    if n >= TT:
                        for b in range(2) if n < STEPS - 1 else ():
                            k = 2 * (n - TT) + b
                            pe.wait_ge(g1_copied, 2)
                            if k >= 2:
                                pe.wait_ge(gate_done, k - 1)
                            for i in (2 * k, 2 * k + 1):
                                last = nc.tensor.matmul(ps[:, k % 2, (i % 2) * D:(i % 2 + 1) * D], g1_t[:, i * P:(i + 1) * P],
                                                        wg2[:, :], start=True, stop=True)
                            last.then_inc(gate_full, 1)
                for half in range(2):
                    pe.wait_ge(weighted, half + 1)
                    for c in range(DC):
                        for k in range(HALF):
                            i = half * HALF + k
                            last = nc.tensor.transpose(ps[:, 4 + 2 * half + c, k * P:(k + 1) * P], o[:, i, c * P:(c + 1) * P],
                                                       net.ident[:, :])
                        last.then_inc(o_turned, 1)
                for b in range(NB):
                    cols = slice(b * BANK, (b + 1) * BANK)
                    pe.wait_ge(o_split, DC * (b + 1))
                    for m in range(DC):
                        for c in range(DC):
                            last = product(nc, ps[:, 2 * b + m, :], wo_h[:, c, m * P:(m + 1) * P], wo_l[:, c, m * P:(m + 1) * P],
                                           o_h[:, c, cols], o_l[:, c, cols], c == 0, c == DC - 1)
                        last.then_inc(y_full, 1)

            @block.scalar
            def _(act_e):
                act_e.wait_ge(w_loaded, 32)
                nc.scalar.activation(w_h[:, :, :], w[:, :, :], ACT.Copy).then_inc(w_high, 1)
                nc.scalar.activation(wo_h[:, :, :], wo[:, :, :], ACT.Copy).then_inc(w_high, 1)
                act_e.wait_ge(consts, 160)
                for n in range(TT + 1):
                    if n < TT:
                        act_e.wait_ge(projected, n + 1)
                        if n >= 2:
                            act_e.wait_ge(rotated, n - 1)
                        nc.scalar.activation(act[:, n % 2, :], ps[:, 0, :], ACT.Silu).then_inc(act_done, 1)
                        nc.scalar.activation(g1[:, n, :], ps[:, 1, D:VG], ACT.Copy)
                        nc.scalar.activation(v[:, n, :], ps[:, 1, 0:D], ACT.Copy).then_inc(v_done, 1)
                    i = n - 1
                    if i >= 0:
                        act_e.wait_ge(turned, i + 1)
                        if i >= 2:
                            act_e.wait_ge(sc_full, PAIRS * (i - 1))
                        if i >= 4:
                            act_e.wait_ge(out_full, i - 3)
                        q_ps = ps[:, 2, 0:D].rearrange("p (c t) -> p c t", c=DC)
                        nc.scalar.activation(q_t[:, i % 4, :, :], q_ps, ACT.Copy)
                        for j in range(2):
                            nc.scalar.activation(qp_h[:, i % 2, :, j, :], q_ps, ACT.Copy, scale=in_pair[:, j:j + 1])
                        nc.scalar.activation(k_h[:, i % 2, :, :], ps[:, 2, D:].rearrange("p (c t) -> p c t", c=DC),
                                             ACT.Copy).then_inc(t_high, 1)
                act_e.wait_ge(g1_turned, 1)
                for b in range(2):
                    nc.scalar.activation(g1_t[:, b * BANK:(b + 1) * BANK], ps[0:HD, b, :], ACT.Copy).then_inc(g1_copied, 1)
                for k in range(TT // 2):
                    act_e.wait_ge(gate_full, k + 1)
                    nc.scalar.activation(gate[:, 2 * k:2 * k + 2, :], ps[:, k % 2, :].rearrange("p (i d) -> p i d", i=2),
                                         ACT.Sigmoid).then_inc(gate_done, 1)
                for half in range(2):
                    for c in range(DC):
                        act_e.wait_ge(o_turned, DC * half + c + 1)
                        nc.scalar.activation(o_h[:, c, half * BANK:(half + 1) * BANK], ps[:, 4 + 2 * half + c, :],
                                             ACT.Copy).then_inc(o_high, 1)
                for n in range(NB * DC):
                    if n % DC == 0:
                        act_e.wait_ge(y_full, n + 1)
                        nc.scalar.activation(net.delta[:, 0, (n // DC) * BANK:(n // DC + 1) * BANK], ps[:, n, :],
                                             ACT.Copy).then_inc(y_copied, 1)

            @block.vector
            def _(dve):
                dve.wait_ge(w_high, 1)
                nc.vector.tensor_tensor(w_l[:, :, :], w[:, :, :], w_h[:, :, :].bitcast(F32), ALU.subtract).then_inc(w_split, 1)
                dve.wait_ge(w_high, 2)
                nc.vector.tensor_tensor(wo_l[:, :, :], wo[:, :, :], wo_h[:, :, :].bitcast(F32), ALU.subtract).then_inc(w_split, 1)
                dve.wait_ge(consts, 160)
                for n in range(STEPS):
                    if n < TT:
                        dve.wait_ge(act_done, n + 1)
                        wide = lambda ap: ap.rearrange("p (h e) -> p h e", e=HD)
                        nc.vector.tensor_tensor(wide(by_cos[:, n % 2, :]), wide(act[:, n % 2, :]),
                                                cos[:, n, :].unsqueeze(1).broadcast_to([P, 2 * H1, HD]), ALU.mult).then_inc(cos_done, 1)
                        dve.wait_ge(cos_done, n + 1)
                        dve.wait_ge(sin_done, 2 * n + 2)
                        if n >= 2:
                            dve.wait_ge(turned, n - 1)
                            dve.wait_ge(kd_done, n - 1)
                        nc.vector.tensor_tensor(rot[:, n % 2, :], by_cos[:, n % 2, :], by_sin[:, n % 2, :], ALU.add).then_inc(rotated, 1)
                    i = n - 1
                    if 0 <= i < TT:
                        dve.wait_ge(t_high, i + 1)
                        q_ps = ps[:, 2, 0:D].rearrange("p (c t) -> p c t", c=DC)
                        for j in range(2):
                            nc.vector.scalar_tensor_tensor(qp_l[:, i % 2, :, j, :], q_ps, in_pair[:, j:j + 1],
                                                           qp_h[:, i % 2, :, j, :].bitcast(F32), ALU.mult, ALU.subtract)
                        nc.vector.tensor_tensor(k_l[:, i % 2, :, :], ps[:, 2, D:].rearrange("p (c t) -> p c t", c=DC),
                                                k_h[:, i % 2, :, :].bitcast(F32), ALU.subtract).then_inc(t_split, 1)
                    i = n - 3
                    if i >= 0:
                        dve.wait_ge(out_full, i + 1)
                        nc.vector.tensor_tensor(heads(inter[:, i % 2, :]), heads(ps[:, 3, D:]),
                                                decay_q[:, :].unsqueeze(2).broadcast_to([P, H1, HD]), ALU.mult).then_inc(chain, 1)
                        nc.vector.tensor_tensor(kv[:, :, :], ps[:, 3, 0:D].rearrange("p (c t) -> p c t", c=DC),
                                                same_head[:, :].unsqueeze(1).broadcast_to([P, DC, P]), ALU.mult).then_inc(inter_done, 1)
                        dve.wait_ge(chain, i + 1)
                        nc.vector.tensor_tensor(o[:, i, :], inter[:, i % 2, :], ps[:, 4, 0:D], ALU.add).then_inc(o_done, 1)
                        dve.wait_ge(inter_done, i + 1)
                        for c in range(DC):
                            last = nc.vector.scalar_tensor_tensor(state[:, c, :], state[:, c, :], lam_c[:, c:c + 1], kv[:, c, :],
                                                                  ALU.mult, ALU.add)
                        last.then_inc(state_done, 1)
                        dve.wait_ge(state_done, i + 2)
                    i = n - 2
                    if 0 <= i < TT:
                        for r in range(PAIRS):
                            dve.wait_ge(sc_full, PAIRS * i + r + 1)
                            nc.vector.tensor_tensor(of_pair(sc[:, i % 2, :, :], r), ps[:, SCORE_BANKS[r], :].rearrange("p (c x) -> p c x", c=DC),
                                                    of_pair(decay[:, :, :], r), ALU.mult).then_inc(sc_done, 1)
                for half in range(2):
                    part = slice(half * HALF, (half + 1) * HALF)
                    dve.wait_ge(gate_done, HALF // 2 * (half + 1))
                    dve.wait_ge(o_done, TT)
                    nc.vector.tensor_tensor(o[:, part, :], o[:, part, :], gate[:, part, :], ALU.mult).then_inc(gated, 1)
                links = TT
                for half in range(2):
                    part = slice(half * HALF, (half + 1) * HALF)
                    dve.wait_ge(squares, half + 1)
                    nc.vector.tensor_reduce(ms[:, part, :], sq[:, part, :].rearrange("p i (h e) -> p i h e", e=HD), AX.X, ALU.add)\
                        .then_inc(chain, 1)
                    dve.wait_ge(chain, links + 1)
                    nc.vector.tensor_scalar(ms[:, part, :], ms[:, part, :], 1.0 / HD, None, ALU.mult).then_inc(chain, 1)
                    dve.wait_ge(chain, links + 2)
                    flat = lambda ap: ap.rearrange("p i h -> p (i h)")
                    links = inverse_root(nc, dve, flat(rms[:, part, :]), flat(ms[:, part, :]), RMS_EPS,
                                         root[:, 0, half * HALF * H1:(half + 1) * HALF * H1],
                                         root[:, 1, half * HALF * H1:(half + 1) * HALF * H1], chain, links + 2)
                    dve.wait_ge(chain, links)
                    by_head = lambda ap: ap.rearrange("p i (h e) -> p (i h) e", e=HD)
                    nc.vector.tensor_tensor(by_head(o[:, part, :]), by_head(o[:, part, :]),
                                            flat(rms[:, part, :]).unsqueeze(2).broadcast_to([P, HALF * H1, HD]), ALU.mult).then_inc(chain, 1)
                    links += 1
                    dve.wait_ge(chain, links)
                    nc.vector.tensor_tensor(o[:, part, :], o[:, part, :], weight[:, :].unsqueeze(1).broadcast_to([P, HALF, D]),
                                            ALU.mult).then_inc(weighted, 1)
                for half in range(2):
                    for c in range(DC):
                        cols = slice(half * BANK, (half + 1) * BANK)
                        dve.wait_ge(o_high, DC * half + c + 1)
                        nc.vector.tensor_tensor(o_l[:, c, cols], ps[:, 4 + 2 * half + c, :], o_h[:, c, cols].bitcast(F32),
                                                ALU.subtract).then_inc(o_split, 1)
                for n in range(NB * DC):
                    if n % DC == 1:
                        dve.wait_ge(y_full, n + 1)
                        nc.vector.tensor_copy(net.delta[:, 1, (n // DC) * BANK:(n // DC + 1) * BANK], ps[:, n, :]).then_inc(y_copied, 1)
                dve.wait_ge(y_copied, NB * DC)


EXP1, F1, TOP1 = 32, 176, 6
SHARED1 = 2 * F1
CAPACITY = 2 * (T * TOP1 // EXP1)
TILES1 = EXP1 * F1 // P
GRAIN = 16
SH1 = -(-SHARED1 // P)
SHARED_TILES = [min(P, SHARED1 - k * P) for k in range(SH1)]


def silu_experts_phase(nc, net):
    BODY, RAW, RING, WRING = 4, 2, 2, 4
    AHEAD = 2
    GATE, UP, DOWN, W = 0, DC * P, 2 * DC * P, 2 * DC * P + D
    SG, SU, SD, SW = 0, DC * SHARED1, 2 * DC * SHARED1, 2 * DC * SHARED1 + (SH1 - 1) * D
    TAIL = SHARED_TILES[-1]
    SENT = 8 - TOP1
    assert TILES1 % BODY == 0
    with ExitStack() as mem:
        sb = lambda n, s, d=F32: mem.enter_context(nc.sbuf_tensor(f"f1_{n}", s, d))
        sem = lambda n: net.ctx.enter_context(nc.semaphore(f"f1_{n}"))
        ps, xn, xn_h, xn_l = net.ps, net.xn, net.xn_h, net.xn_l
        router, before = sb("router", [P, DC, EXP1]), sb("before", [P, P])
        before_b, ones_b = sb("before_b", [P, P], BF16), sb("ones_b", [P, P], BF16)
        sw, sw_h, sw_l = sb("sw", [P, SW]), sb("sw_h", [P, SW], F32R), sb("sw_l", [P, SW], F32R)
        st, st_h, st_l = sb("st", [TAIL, D]), sb("st_h", [TAIL, D], F32R), sb("st_l", [TAIL, D], F32R)
        e_raw = sb("e_raw", [P, RAW, W])
        e_h, e_l = sb("e_h", [P, WRING, W], F32R), sb("e_l", [P, WRING, W], F32R)
        one = sb("one", [P, 1])
        silu, act = sb("silu", [P, RING, T]), sb("act", [P, RING, T])
        a_h, a_l = sb("a_h", [P, RING, T], F32R), sb("a_l", [P, RING, T], F32R)
        s_h, s_l = sb("s_h", [P, SH1, T], F32R), sb("s_l", [P, SH1, T], F32R)
        cw_row = sb("cw_row", [P, RING, T])
        logit = sb("logit", [P, TT, EXP1 + SENT])
        score, found = sb("score", [P, TT, EXP1]), sb("found", [P, TT, EXP1 + SENT])
        best, take = sb("best", [P, TT, 8]), sb("take", [P, TT, 8])
        total, cw = sb("total", [P, TT]), sb("cw", [P, TT, EXP1])
        chosen = sb("chosen", [P, TT, EXP1], BF16)
        cw_t = sb("cw_t", [EXP1, T])
        grains = net.cw_grains

        consts, s_loaded = sem("consts"), sem("s_loaded")
        s_high, s_split = sem("s_high"), sem("s_split")
        logits, scored, exped, marked, ranked = sem("logits"), sem("scored"), sem("exped"), sem("marked"), sem("ranked")
        routed, cw_turned, cw_copied, cw_stored = sem("routed"), sem("cw_turned"), sem("cw_copied"), sem("cw_stored")
        e_loaded = [sem(f"e_loaded{r}") for r in range(RAW)]
        row_loaded = [sem(f"row_loaded{r}") for r in range(RING)]
        e_high, e_split = sem("e_high"), sem("e_split")
        gate_full, up_full, silued, timed, weighed = sem("gate_full"), sem("up_full"), sem("silued"), sem("timed"), sem("weighed")
        act_high, act_split, down_done = sem("act_high"), sem("act_split"), sem("down_done")
        y_copied, chain = sem("y_copied"), sem("chain")

        def blocks(ap):
            return ap.rearrange("p (n t) -> p n t", n=NB)

        def steps(eng, loop_end, last, step):
            for n in range(BODY):
                step(0, n)
            with eng.Fori(1, loop_end) as it:
                for r in range(BODY):
                    step(it, r)
            for n in range(loop_end * BODY, last):
                step(*divmod(n, BODY))

        def known(it, r, low, high=TILES1 + BODY):
            return not isinstance(it, int) or low <= it * BODY + r < high

        with nc.Block() as block:

            @block.sync
            def _(sp):
                sp.dma_start(router[:, :, :], net.dram["router"]).then_inc(consts, 16)
                sp.dma_start(before[:, :], net.dram["before"]).then_inc(consts, 16)
                sp.dma_start(sw[:, SG:SU], net.dram["wsg"]).then_inc(s_loaded, 16)
                sp.dma_start(sw[:, SU:SD], net.dram["wsu"]).then_inc(s_loaded, 16)
                sp.dma_start(sw[:, SD:SW].rearrange("p (k d) -> p k d", d=D),
                             net.dram["wsd"][0:(SH1 - 1) * P, :].rearrange("(k p) d -> p k d", p=P)).then_inc(s_loaded, 16)
                sp.dma_start(st[:, :], net.dram["wsd"][(SH1 - 1) * P:SHARED1, :]).then_inc(s_loaded, 16)

                def load_weights(it, r):
                    n = it * BODY + r
                    if known(it, r, RAW):
                        sp.wait_ge(e_split, n - RAW + 1)
                    sp.dma_start(e_raw[:, r % RAW, :], net.dram["we1"][n]).then_inc(e_loaded[r % RAW], 16)

                def load_row(it, r):
                    n = it * BODY + r
                    if known(it, r, RING):
                        sp.wait_ge(weighed, n - RING + 1)
                    sp.dma_start(cw_row[:, r % RING, :],
                                 grains[n].unsqueeze(1).broadcast_to([P // GRAIN, GRAIN, T])).then_inc(row_loaded[r % RING], 16)

                for r in range(RAW):
                    load_weights(0, r)
                sp.wait_ge(cw_copied, 1)
                sp.dma_start(grains.rearrange("a b t -> (a b) t").rearrange("(e g) t -> e g t", e=EXP1),
                             cw_t[:, :].unsqueeze(1).broadcast_to([EXP1, F1 // GRAIN, T])).then_inc(cw_stored, 16)
                sp.wait_ge(cw_stored, 16)

                def step(it, r):
                    load_row(it, r)
                    if known(it, r, 0, TILES1 - RAW):
                        load_weights(it, r + RAW)

                steps(sp, TILES1 // BODY - 1, TILES1, step)

            @block.tensor
            def _(pe):
                pe.wait_ge(consts, 35)
                for i in range(TT):
                    for c in range(DC):
                        last = nc.tensor.matmul(ps[:, 7, i * EXP1:(i + 1) * EXP1], xn[:, c, i * P:(i + 1) * P],
                                                router[:, c, :], start=c == 0, stop=c == DC - 1)
                last.then_inc(logits, 1)

                def project(bank, rows, weight, full):
                    for b in range(NB):
                        cols = slice(b * BANK, (b + 1) * BANK)
                        for c in range(DC):
                            last = product(nc, ps[0:rows, bank + b, :], *weight(c), xn_h[:, c, cols], xn_l[:, c, cols],
                                           c == 0, c == DC - 1)
                    last.then_inc(full, 1)

                def down(weight, rows, h, l, first, final):
                    for m in range(DC):
                        for b in range(NB):
                            cols = slice(b * BANK, (b + 1) * BANK)
                            wt = weight(m)
                            last = product(nc, ps[:, 4 + 2 * m + b, :], *wt, h[0:rows, cols], l[0:rows, cols], first, final)
                    last.then_inc(down_done, 1)

                pe.wait_ge(s_split, 2)
                for k, rows in enumerate(SHARED_TILES):
                    def piece(base):
                        def weight(c):
                            part = slice(base + c * SHARED1 + k * P, base + c * SHARED1 + k * P + rows)
                            return sw_h[:, part], sw_l[:, part]
                        return weight
                    if k:
                        pe.wait_ge(silued, k)
                    project(0, rows, piece(SG), gate_full)
                    if k:
                        pe.wait_ge(timed, k)
                    project(2, rows, piece(SU), up_full)
                pe.wait_ge(marked, 1)
                for i in range(TT):
                    for k in range(i + 1):
                        last = nc.tensor.matmul(ps[:, 6, i * EXP1:(i + 1) * EXP1], before_b[:, :] if k == i else ones_b[:, :],
                                                chosen[:, k, :], start=k == 0, stop=k == i)
                last.then_inc(ranked, 1)
                pe.wait_ge(routed, 1)
                for i in range(TT):
                    last = nc.tensor.transpose(ps[0:EXP1, 4 + i // 4, (i % 4) * P:(i % 4 + 1) * P], cw[:, i, :], net.ident[:, :])
                last.then_inc(cw_turned, 1)
                pe.wait_ge(cw_copied, 1)
                for k, rows in enumerate(SHARED_TILES):
                    pe.wait_ge(act_split, k + 1)
                    if k < SH1 - 1:
                        weight = lambda m: (sw_h[:, SD + k * D + m * P:SD + k * D + (m + 1) * P],
                                            sw_l[:, SD + k * D + m * P:SD + k * D + (m + 1) * P])
                    else:
                        weight = lambda m: (st_h[:, m * P:(m + 1) * P], st_l[:, m * P:(m + 1) * P])
                    down(weight, rows, s_h[:, k, :], s_l[:, k, :], k == 0, False)

                def step(it, r):
                    n = it * BODY + r

                    def piece(slot, base):
                        return lambda c: (e_h[:, slot, base + c * P:base + (c + 1) * P],
                                          e_l[:, slot, base + c * P:base + (c + 1) * P])

                    if known(it, r, 0, TILES1):
                        pe.wait_ge(e_split, n + 1)
                        pe.wait_ge(silued, n + SH1)
                        project(0, P, piece(r % WRING, GATE), gate_full)
                        pe.wait_ge(timed, n + SH1)
                        project(2, P, piece(r % WRING, UP), up_full)
                    if known(it, r, 1):
                        m = (r - 1) % BODY
                        pe.wait_ge(act_split, n + SH1)
                        final = isinstance(it, int) and n == TILES1
                        down(piece(m % WRING, DOWN), P, a_h[:, m % RING, :], a_l[:, m % RING, :], False, final)

                steps(pe, TILES1 // BODY, TILES1 + 1, step)

            @block.scalar
            def _(act_e):
                act_e.wait_ge(s_loaded, 64)
                nc.scalar.activation(sw_h[:, :], sw[:, :], ACT.Copy).then_inc(s_high, 1)
                nc.scalar.activation(st_h[:, :], st[:, :], ACT.Copy).then_inc(s_high, 1)
                act_e.wait_ge(scored, 1)
                nc.scalar.activation(score[:, :, :], score[:, :, :], ACT.Exp).then_inc(exped, 1)

                def silu_gate(n, k, rows):
                    act_e.wait_ge(gate_full, n + 1)
                    if not isinstance(n, int) or n >= RING:
                        act_e.wait_ge(timed, n - RING + 1)
                    nc.scalar.activation(blocks(silu[0:rows, k % RING, :]), ps[0:rows, 0:2, :], ACT.Silu).then_inc(silued, 1)

                for k, rows in enumerate(SHARED_TILES):
                    silu_gate(k, k, rows)
                    act_e.wait_ge(timed, k + 1)
                    nc.scalar.activation(s_h[0:rows, k, :], act[0:rows, k % RING, :], ACT.Copy).then_inc(act_high, 1)

                def high_weights(it, r):
                    act_e.wait_ge(e_loaded[r % RAW], 16 * (it * (BODY // RAW) + r // RAW) + 16)
                    if known(it, r, WRING):
                        act_e.wait_ge(down_done, it * BODY + (r - WRING + 1 + SH1))
                    nc.scalar.activation(e_h[:, r % WRING, :], e_raw[:, r % RAW, :], ACT.Copy).then_inc(e_high, 1)

                for r in range(AHEAD):
                    high_weights(0, r)

                def step(it, r):
                    n = it * BODY + r
                    if known(it, r, 1):
                        m = (r - 1) % RING
                        act_e.wait_ge(weighed, n)
                        if known(it, r, 1 + RING):
                            act_e.wait_ge(down_done, n - RING + SH1)
                        nc.scalar.activation(a_h[:, m, :], act[:, m, :], ACT.Copy).then_inc(act_high, 1)
                    if known(it, r, 0, TILES1):
                        silu_gate(n + SH1, r, P)
                    if known(it, r, 0, TILES1 - AHEAD):
                        high_weights(it, r + AHEAD)

                steps(act_e, TILES1 // BODY - 1, TILES1 + 1, step)
                act_e.wait_ge(down_done, SH1 + TILES1)
                nc.scalar.activation(blocks(net.delta[:, 0, :]), ps[:, 4:6, :], ACT.Copy).then_inc(y_copied, 1)

            @block.gpsimd
            def _(pool):
                nc.gpsimd.memset(logit[:, :, EXP1:], BIG).then_inc(consts, 1)
                nc.gpsimd.memset(take[:, :, TOP1:], BIG).then_inc(consts, 1)
                nc.gpsimd.memset(ones_b[:, :], 1.0).then_inc(consts, 1)

                def low_weights(it, r):
                    pool.wait_ge(e_high, it * BODY + r + 1)
                    nc.gpsimd.tensor_tensor(e_l[:, r % WRING, :], e_raw[:, r % RAW, :], e_h[:, r % WRING, :].bitcast(F32),
                                            ALU.subtract).then_inc(e_split, 1)

                for r in range(AHEAD):
                    low_weights(0, r)

                def step(it, r):
                    n = it * BODY + r
                    if known(it, r, 0, TILES1 - AHEAD):
                        low_weights(it, r + AHEAD)
                    if known(it, r, 0, TILES1):
                        pool.wait_ge(row_loaded[r % RING], 16 * (it * (BODY // RING) + r // RING) + 16)
                        pool.wait_ge(timed, n + SH1 + 1)
                        nc.gpsimd.tensor_tensor(act[:, r % RING, :], act[:, r % RING, :], cw_row[:, r % RING, :],
                                                ALU.mult).then_inc(weighed, 1)

                steps(pool, TILES1 // BODY - 1, TILES1, step)

            @block.vector
            def _(dve):
                links = [0]

                def link(ins):
                    ins.then_inc(chain, 1)
                    links[0] += 1
                    dve.wait_ge(chain, links[0])

                def times(n, k, rows):
                    dve.wait_ge(up_full, n + 1)
                    dve.wait_ge(silued, n + 1)
                    if not isinstance(n, int) or n >= RING:
                        dve.wait_ge(act_split, n - RING + 1)
                    nc.vector.tensor_tensor(blocks(act[0:rows, k % RING, :]), ps[0:rows, 2:4, :], blocks(silu[0:rows, k % RING, :]),
                                            ALU.mult).then_inc(timed, 1)

                def split_shared(k, rows):
                    dve.wait_ge(act_high, k + 1)
                    nc.vector.tensor_tensor(s_l[0:rows, k, :], act[0:rows, k % RING, :], s_h[0:rows, k, :].bitcast(F32),
                                            ALU.subtract).then_inc(act_split, 1)

                dve.wait_ge(s_high, 2)
                nc.vector.tensor_tensor(sw_l[:, :], sw[:, :], sw_h[:, :].bitcast(F32), ALU.subtract).then_inc(s_split, 1)
                nc.vector.tensor_tensor(st_l[:, :], st[:, :], st_h[:, :].bitcast(F32), ALU.subtract).then_inc(s_split, 1)
                dve.wait_ge(consts, 35)
                dve.wait_ge(logits, 1)
                nc.vector.tensor_copy(before_b[:, :], before[:, :])
                link(nc.vector.tensor_copy(logit[:, :, 0:EXP1], ps[:, 7, 0:TT * EXP1].rearrange("p (i e) -> p i e", e=EXP1)))
                for i in range(TT):
                    last = nc.vector.max(best[:, i, :], logit[:, i, 0:EXP1])
                link(last)
                nc.vector.tensor_tensor(score[:, :, :], logit[:, :, 0:EXP1], best[:, :, 0:1].broadcast_to([P, TT, EXP1]),
                                        ALU.subtract).then_inc(scored, 1)
                link(nc.vector.tensor_copy(take[:, :, 0:TOP1], best[:, :, 0:TOP1]))
                for i in range(TT):
                    last = nc.vector.match_replace(found[:, i, :], take[:, i, :], logit[:, i, :], TAKEN)
                link(last)
                nc.vector.tensor_scalar(chosen[:, :, :], found[:, :, 0:EXP1], TAKEN, None, ALU.is_equal).then_inc(marked, 1)
                dve.wait_ge(exped, 1)
                link(nc.vector.tensor_reduce(total[:, :], score[:, :, :], AX.X, ALU.add))
                link(nc.vector.reciprocal(total[:, :], total[:, :]))
                link(nc.vector.tensor_tensor(score[:, :, :], score[:, :, :], total[:, :].unsqueeze(2).broadcast_to([P, TT, EXP1]),
                                             ALU.mult))
                times(0, 0, SHARED_TILES[0])
                link(nc.vector.scalar_tensor_tensor(cw[:, :, :], found[:, :, 0:EXP1], TAKEN, score[:, :, :], ALU.is_equal, ALU.mult))
                link(nc.vector.tensor_reduce(total[:, :], cw[:, :, :], AX.X, ALU.add))
                link(nc.vector.tensor_scalar(total[:, :], total[:, :], 1e-20, None, ALU.add))
                link(nc.vector.reciprocal(total[:, :], total[:, :]))
                split_shared(0, SHARED_TILES[0])
                link(nc.vector.tensor_tensor(cw[:, :, :], cw[:, :, :], total[:, :].unsqueeze(2).broadcast_to([P, TT, EXP1]),
                                             ALU.mult))
                for k in range(1, SH1):
                    times(k, k, SHARED_TILES[k])
                    split_shared(k, SHARED_TILES[k])
                dve.wait_ge(ranked, 1)
                nc.vector.scalar_tensor_tensor(cw[:, :, :], ps[:, 6, 0:TT * EXP1].rearrange("p (i e) -> p i e", e=EXP1),
                                               float(CAPACITY), cw[:, :, :], ALU.is_lt, ALU.mult).then_inc(routed, 1)
                dve.wait_ge(cw_turned, 1)
                nc.vector.tensor_copy(blocks(cw_t[:, :]), ps[0:EXP1, 4:6, :]).then_inc(cw_copied, 1)

                def step(it, r):
                    n = it * BODY + r
                    if known(it, r, 1):
                        m = (r - 1) % RING
                        dve.wait_ge(act_high, n + SH1)
                        nc.vector.tensor_tensor(a_l[:, m, :], act[:, m, :], a_h[:, m, :].bitcast(F32),
                                                ALU.subtract).then_inc(act_split, 1)
                    if known(it, r, 0, TILES1):
                        times(n + SH1, r, P)

                steps(dve, TILES1 // BODY, TILES1 + 1, step)
                dve.wait_ge(down_done, SH1 + TILES1)
                nc.vector.tensor_copy(blocks(net.delta[:, 1, :]), ps[:, 6:8, :]).then_inc(y_copied, 1)
                dve.wait_ge(y_copied, 2)


def program(nc, dram, out, upto=99):
    net = Net()
    net.dram = dram
    with ExitStack() as ctx:
        net.ctx = ctx
        sb = lambda n, s, d=F32: ctx.enter_context(nc.sbuf_tensor(n, s, d))
        net.ps = ctx.enter_context(nc.psum_tensor("ps", [P, 8, BANK], F32))
        net.x = sb("x", [P, TT, D])
        net.delta = sb("delta", [P, DC, T])
        net.xn_h, net.xn_l = sb("xn_h", [P, DC, T], F32R), sb("xn_l", [P, DC, T], F32R)
        net.ident = sb("ident", [P, P])
        net.cw_dram = [nc.dram_tensor(f"cw{n}", (EXP0, T), F32, kind="Internal").ap() for n in range(1)]
        net.cw_grains = nc.dram_tensor("cw_grains", (TILES1, P // GRAIN, T), F32, kind="Internal").ap()
        net.norm_sems = [ctx.enter_context(nc.semaphore(f"norm_{n}")) for n in (
            "loaded", "delta_turned", "x_added", "biased", "stats_done", "moments_done", "rstd_done", "xc_done",
            "xc_turned", "high_done", "parts_done", "full_done", "stored")]
        net.norm_counts = {s.name: 0 for s in net.norm_sems}
        norm_phase(nc, net, "n0", False, None, True, False, None)
        softmax_attention_phase(nc, net)
        net.xn = sb("xn", [P, DC, T])
        norm_phase(nc, net, "n1", True, dram["bo"], True, True, None)
        squared_relu_experts_phase(nc, net)
        norm_phase(nc, net, "n2", True, None, True, False, None)
        linear_attention_phase(nc, net)
        norm_phase(nc, net, "n3", True, None, True, True, None)
        silu_experts_phase(nc, net)
        norm_phase(nc, net, "n4", True, None, False, False, out)


def kernel(**inputs):
    import numpy as _np
    import concourse.bacc as _bacc
    from concourse import mybir as _mybir
    from concourse.bass_utils import run_bass_kernel_spmd as _run

    def get(name):
        return _np.asarray(inputs[name])

    def grouped(w, groups):
        return w.reshape(DC, P, groups, -1).transpose(2, 1, 0, 3)

    def tiled(w):
        return w.reshape(-1, P, w.shape[1]).transpose(1, 0, 2)

    def flat(w):
        return tiled(w).reshape(P, -1)

    def by_feature(w):
        w = w.transpose(1, 0, 2).reshape(DC, P, TILES1, P)
        return w.transpose(2, 1, 0, 3).reshape(TILES1, P, DC * P)

    host = {
        "x": get("L0_attn_inputs_q").reshape(T, D),
        "ident": _np.eye(P, dtype=_np.float32),
        "bq": get("L0_attn_bq").reshape(HEADS, DH).T, "bk": get("L0_attn_bk").reshape(KV, DH).T, "bv": get("L0_attn_bv"), "bo": get("L0_attn_bo"),
        "wq": grouped(get("L0_attn_wq"), KV), "wk": grouped(get("L0_attn_wk"), KV), "wv": grouped(get("L0_attn_wv"), KV),
        "wo": get("L0_attn_wo").reshape(KV, PER, DH, D).transpose(0, 2, 1, 3),
        "gate0": tiled(get("L0_ffn_gate_w").T), "gate_bias": get("L0_ffn_gate_bias"),
        "fc1": flat(get("L0_ffn_fc1_w").T), "fc2": flat(get("L0_ffn_fc2_w").T),
        "sup0": flat(get("L0_ffn_shared_up_w").T), "sdn0": flat(get("L0_ffn_shared_down_w").T),
        "we0": _np.stack([get("L0_ffn_w1").transpose(0, 2, 1), get("L0_ffn_w2").transpose(0, 2, 1)], 2),
        "w1a": tiled(_np.concatenate([get("L1_attn_Wq"), get("L1_attn_Wk"), get("L1_attn_Wv"), get("L1_attn_Wg1")], 1)),
        "wg2": get("L1_attn_Wg2"), "wo1": tiled(get("L1_attn_Wo")), "norm_weight": get("L1_attn_norm_weight"),
        **{k: a.astype(_np.float32) for k, a in decay_tables().items()},
        "router": tiled(get("L1_ffn_wg_router").T), "before": _np.triu(_np.ones((P, P), _np.float32), 1),
        "wsg": flat(get("L1_ffn_ws_gate")), "wsu": flat(get("L1_ffn_ws_up")), "wsd": get("L1_ffn_ws_down"),
        "we1": _np.concatenate([by_feature(get("L1_ffn_w_gate")), by_feature(get("L1_ffn_w_up")),
                                get("L1_ffn_w_down").reshape(TILES1, P, D)], 2),
    }
    nc = _bacc.Bacc("TRN2", target_bir_lowering=False, num_devices=1)
    arrays, dram = {}, {}
    for name, a in host.items():
        a = _np.ascontiguousarray(a)
        arrays[f"in_{name}"] = a
        dram[name] = nc.dram_tensor(f"in_{name}", a.shape, _mybir.dt.from_np(a.dtype), kind="ExternalInput").ap()
    out = nc.dram_tensor("out_x", (T, D), F32, kind="ExternalOutput").ap()
    program(nc, dram, out)
    r = _run(nc, [arrays], core_ids=[0])
    return r.results[0]["out_x"].reshape(1, T, D)
```

```python
import numpy as np

import concourse.bass as bass
from concourse import mybir
from contextlib import ExitStack

F32 = mybir.dt.float32
F32R = mybir.dt.float32r
I32 = mybir.dt.int32
BF16 = mybir.dt.bfloat16
ALU = mybir.AluOpType
ACT = mybir.ActivationFunctionType
AX = mybir.AxisListType

P = 128
BANK = 512
T, D = 1024, 256
TT, DC = T // P, D // P
NB = T // BANK
LN_EPS = 1e-5


class Net:
    pass


def product(nc, out, lhs_h, lhs_l, rhs_h, rhs_l, start, stop):
    nc.tensor.matmul(out, lhs_h, rhs_h, start=start, stop=False)
    nc.tensor.matmul(out, lhs_h, rhs_l, start=False, stop=False)
    return nc.tensor.matmul(out, lhs_l, rhs_h, start=False, stop=stop)


def inverse_root(nc, dve, out, var, eps, a, s, done, n):
    nc.vector.tensor_scalar(a, var, eps, None, ALU.add).then_inc(done, 1)
    dve.wait_ge(done, n + 1)
    nc.vector.tensor_scalar(s.bitcast(I32), a.bitcast(I32), 1, None, ALU.logical_shift_right).then_inc(done, 1)
    dve.wait_ge(done, n + 2)
    nc.vector.tensor_scalar(out.bitcast(I32), s.bitcast(I32), -1.0, float(0x5F3759DF), ALU.mult, ALU.add).then_inc(done, 1)
    n += 3
    for _ in range(3):
        dve.wait_ge(done, n)
        nc.vector.scalar_tensor_tensor(s, out, -0.5, out, ALU.mult, ALU.mult).then_inc(done, 1)
        dve.wait_ge(done, n + 1)
        nc.vector.tensor_tensor(s, s, a, ALU.mult).then_inc(done, 1)
        dve.wait_ge(done, n + 2)
        nc.vector.scalar_tensor_tensor(out, s, 1.5, out, ALU.add, ALU.mult).then_inc(done, 1)
        n += 3
    return n


class Norm:

    def __init__(self, nc, net, tag, mem, add_delta, keep_full, xc=None):
        sb = lambda n, s, d=F32: mem.enter_context(nc.sbuf_tensor(f"{tag}_{n}", s, d))
        self.nc, self.net, self.add_delta, self.keep_full = nc, net, add_delta, keep_full
        self.xc = sb("xc", [P, TT, D]) if xc is None else xc
        self.stats = sb("stats", [P, TT, 6])
        self.moments = sb("moments", [P, TT, 2])
        self.rstd, self.root = sb("rstd", [P, TT]), sb("root", [P, 2, TT])
        self.base = dict(net.norm_counts)
        totals = {"loaded": 32 * (not add_delta), "delta_turned": PAIRS * add_delta, "x_added": PAIRS * add_delta,
                  "stats_done": TT, "moments_done": TT, "rstd_done": 24, "xc_done": TT, "xc_turned": NB,
                  "high_done": NB * DC, "parts_done": NB * DC, "full_done": NB * DC * keep_full}
        for name, count in totals.items():
            net.norm_counts[name] += int(count)

    def wait(self, eng, name, n):
        eng.wait_ge(self.net.norm_sems[name], self.base[name] + n)

    def wait_parts(self, eng):
        self.wait(eng, "parts_done", NB * DC)

    def wait_full(self, eng):
        self.wait(eng, "full_done", NB * DC)

    def sync(self, sp):
        if not self.add_delta:
            sems, net = self.net.norm_sems, self.net
            sp.dma_start(net.x[:, :, :], net.dram["x"].rearrange("(i p) d -> p i d", p=P)).then_inc(sems["loaded"], 16)
            sp.dma_start(net.ident[:, :], net.dram["ident"]).then_inc(sems["loaded"], 16)

    def tensor(self, pe):
        nc, net, sems = self.nc, self.net, self.net.norm_sems
        if self.add_delta:
            turn_delta(nc, net)
        else:
            self.wait(pe, "loaded", 32)
        for n in range(NB):
            for k in range(4):
                self.wait(pe, "xc_done", 4 * n + k + 1)
                for c in range(DC):
                    last = nc.tensor.transpose(net.ps[:, 4 + 2 * n + c, k * P:(k + 1) * P],
                                               self.xc[:, 4 * n + k, c * P:(c + 1) * P], net.ident[:, :])
            last.then_inc(sems["xc_turned"], 1)

    def vector(self, dve):
        nc, net, sems, x = self.nc, self.net, self.net.norm_sems, self.net.x
        half = TT // 2
        if not self.add_delta:
            self.wait(dve, "loaded", 32)
        n_rstd = self.base["rstd_done"]
        for n in range(2):
            if self.add_delta:
                for j in range(n * PAIRS // 2, (n + 1) * PAIRS // 2):
                    self.wait(dve, "delta_turned", j + 1)
                    add_delta(nc, net, j).then_inc(sems["x_added"], 1)
            for i in range(n * half, (n + 1) * half):
                if self.add_delta:
                    self.wait(dve, "x_added", i // 2 + 1)
                nc.vector.bn_stats(self.stats[:, i, :], x[:, i, :]).then_inc(sems["stats_done"], 1)
            for i in range(n * half, (n + 1) * half):
                self.wait(dve, "stats_done", i + 1)
                nc.vector.bn_aggr(self.moments[:, i, :], self.stats[:, i, :]).then_inc(sems["moments_done"], 1)
            self.wait(dve, "moments_done", (n + 1) * half)
            part = slice(n * half, (n + 1) * half)
            n_rstd = inverse_root(nc, dve, self.rstd[:, part], self.moments[:, part, 1], LN_EPS, self.root[:, 0, part],
                                  self.root[:, 1, part], sems["rstd_done"], n_rstd)
            dve.wait_ge(sems["rstd_done"], n_rstd)
            for i in range(n * half, (n + 1) * half):
                nc.vector.tensor_scalar(self.xc[:, i, :], x[:, i, :], self.moments[:, i, 0:1], self.rstd[:, i:i + 1],
                                        ALU.subtract, ALU.mult).then_inc(sems["xc_done"], 1)
        for n in range(NB):
            for c in range(DC):
                cols = slice(n * BANK, (n + 1) * BANK)
                self.wait(dve, "high_done", DC * n + c + 1)
                nc.vector.tensor_tensor(net.xn_l[:, c, cols], net.ps[:, 4 + 2 * n + c, :], net.xn_h[:, c, cols].bitcast(F32),
                                        ALU.subtract).then_inc(sems["parts_done"], 1)

    def scalar(self, act):
        nc, net, sems = self.nc, self.net, self.net.norm_sems
        for n in range(NB):
            self.wait(act, "xc_turned", n + 1)
            for c in range(DC):
                cols = slice(n * BANK, (n + 1) * BANK)
                if self.keep_full:
                    nc.scalar.activation(net.xn[:, c, cols], net.ps[:, 4 + 2 * n + c, :], ACT.Copy).then_inc(sems["full_done"], 1)
                nc.scalar.activation(net.xn_h[:, c, cols], net.ps[:, 4 + 2 * n + c, :], ACT.Copy).then_inc(sems["high_done"], 1)


PAIRS = TT // 2
NORM_SEMS = ("loaded", "delta_turned", "x_added", "stats_done", "moments_done", "rstd_done", "xc_done", "xc_turned",
             "high_done", "parts_done", "full_done", "stored")


def turn_delta(nc, net):
    for j in range(PAIRS):
        for i in (2 * j, 2 * j + 1):
            for c in range(DC):
                last = nc.tensor.transpose(net.ps[:, j, (i % 2) * D + c * P:(i % 2) * D + (c + 1) * P],
                                           net.delta[:, c, i * P:(i + 1) * P], net.ident[:, :])
        last.then_inc(net.norm_sems["delta_turned"], 1)


def add_delta(nc, net, j):
    pair = net.x[:, 2 * j:2 * j + 2, :]
    return nc.vector.tensor_tensor(pair, pair, net.ps[:, j, :].rearrange("p (k d) -> p k d", k=2), ALU.add)


def output_phase(nc, net, out):
    sems, base = net.norm_sems, dict(net.norm_counts)
    with nc.Block() as block:

        @block.tensor
        def _(pe):
            turn_delta(nc, net)

        @block.vector
        def _(dve):
            for j in range(PAIRS):
                dve.wait_ge(sems["delta_turned"], base["delta_turned"] + j + 1)
                add_delta(nc, net, j).then_inc(sems["x_added"], 1)

        @block.sync
        def _(sp):
            for j in range(PAIRS):
                sp.wait_ge(sems["x_added"], base["x_added"] + j + 1)
                sp.dma_start(out.rearrange("(i p) d -> p i d", p=P)[:, 2 * j:2 * j + 2, :],
                             net.x[:, 2 * j:2 * j + 2, :]).then_inc(sems["stored"], 16)
            sp.wait_ge(sems["stored"], base["stored"] + 16 * PAIRS)


HEADS, KV, DH = 16, 4, 128
PER = HEADS // KV
Q_SCALE = float(1.0 / np.sqrt(DH))


def softmax_attention_phase(nc, net):
    UNITS = PER * NB
    KT = TT
    STEPS = UNITS * KT
    TILES = UNITS * 4
    RING = 8
    LEAD = 12
    GW = PER * DH
    PROJ = PER + 1

    opening = [("k",), ("q", 0), ("v",), ("s", 0), ("s", 1), ("vs",)] + [("s", s) for s in range(2, LEAD)] + [("t", 0)]
    steady = []
    for s in range(LEAD, STEPS):
        if s % 2 == 0 and (s // 2 + 2) % TT == 0:
            steady.append(("q", (s // 2 + 2) // TT))
        steady += [("t", s - LEAD + 1), ("s", s), ("p", s - LEAD)]
    at = STEPS - LEAD
    change = [("k",)]
    ahead = [[], [], [], [0], [1], [2], [3], [4, 5], [6], [7], [8, 9]]
    for n in range(LEAD - 1):
        change += [("v",)] if n == 2 else []
        change += [("t", at + n + 1)] + [("s", s) for s in ahead[n]] + [("p", at + n)]
    change += [("p", STEPS - 1), ("vs",), ("s", 10), ("s", 11), ("y", 0), ("t", 0), ("y", 1)]
    closing = []
    for n in range(LEAD - 1):
        closing += [("t", at + n + 1), ("p", at + n)]
    closing += [("p", STEPS - 1), ("y", 0), ("y", 1)]

    def jobs_of(events):
        return [e for e in events if e[0] in "kvqy" or (e[0] == "s" and e[1] % 2 == 0)]

    first, lap = len(jobs_of(opening)), len(jobs_of(steady + change))
    assert lap % 2 == 0

    with ExitStack() as mem:
        sb = lambda n, s, d=F32: mem.enter_context(nc.sbuf_tensor(f"at_{n}", s, d))
        sem = lambda n: net.ctx.enter_context(nc.semaphore(f"at_{n}"))
        norm = Norm(nc, net, "n0", mem, False, False)
        ps, xn_h, xn_l = net.ps, net.xn_h, net.xn_l
        wq_raw, wkv_raw, wo_raw = sb("wq_raw", [P, DC, GW]), sb("wkv_raw", [P, 2, DC, DH]), sb("wo_raw", [P, PER, D])
        wq_h, wq_l = sb("wq_h", [P, DC, GW], F32R), sb("wq_l", [P, DC, GW], F32R)
        wkv_h, wkv_l = sb("wkv_h", [P, 2, DC, DH], F32R), sb("wkv_l", [P, 2, DC, DH], F32R)
        wo_h, wo_l = sb("wo_h", [P, PER, D], F32R), sb("wo_l", [P, PER, D], F32R)
        one = sb("one", [P, 1])
        bq, bk = sb("bq", [P, HEADS]), sb("bk", [P, KV])
        bv, bo = sb("bv", [P, KV * DH]), sb("bo", [P, D])
        proj = sb("proj", [P, T])
        v_full = sb("v_full", [P, T])
        q_h, q_l = sb("q_h", [P, 2, T], F32R), sb("q_l", [P, 2, T], F32R)
        k_h, k_l = sb("k_h", [P, T], F32R), sb("k_l", [P, T], F32R)
        v_h, v_l = sb("v_h", [P, T], F32R), sb("v_l", [P, T], F32R)
        prob = sb("prob", [P, RING, T])
        pt_h, pt_l = sb("pt_h", [P, 2, BANK], F32R), sb("pt_l", [P, 2, BANK], F32R)
        o_h, o_l = sb("o_h", [P, PER, T], F32R), sb("o_l", [P, PER, T], F32R)
        neg_max, row_sum, inv_sum = sb("neg_max", [P, TILES]), sb("row_sum", [P, TILES]), sb("inv_sum", [P, TILES])

        consts, ready = sem("consts"), sem("ready")
        wq_loaded, wkv_loaded, wo_loaded = sem("wq_loaded"), sem("wkv_loaded"), sem("wo_loaded")
        w_high, wq_split, wkv_split, wo_split = sem("w_high"), sem("wq_split"), sem("wkv_split"), sem("wo_split")
        bq_scaled = sem("bq_scaled")
        proj_full, proj_read = sem("proj_full"), sem("proj_read")
        proj_high, proj_split = sem("proj_high"), sem("proj_split")
        values_full, v_added, v_high, v_split = sem("values_full"), sem("v_added"), sem("v_high"), sem("v_split")
        s_full, maxed, exped, inverted, normed = sem("s_full"), sem("maxed"), sem("exped"), sem("inverted"), sem("normed")
        pt_full, pt_high, pt_split, pv_done = sem("pt_full"), sem("pt_high"), sem("pt_split"), sem("pv_done")
        o_high, o_split, y_full, y_added = sem("o_high"), sem("o_split"), sem("y_full"), sem("y_added")

        LIFT = KT + 1
        lifted = {"pe": (pt_full, pv_done), "dve": (pt_split, o_split, y_added)}

        def slot(n):
            return ps[:, 2 * (n % 2):2 * (n % 2) + 2, :]

        def turned(j):
            return ps[:, 4 + j % 2, :]

        def o_bank(u):
            return ps[:, 6 + u % 2, :]

        def halves(ap):
            return ap.rearrange("p (n t) -> p n t", n=NB)

        def proj_count(g, e):
            if e[0] == "k":
                return 2 + PROJ * (g + 1) if not (isinstance(g, int) and g < 0) else 1
            return 2 + PROJ * g + e[1] if not (isinstance(g, int) and g < 0) else 2

        def read_of(g, e, nxt):
            own = g + 1 if nxt else g
            if e[0] in "kq":
                return proj_read, proj_count(g, e)
            if e[0] == "v":
                return v_added, own + 1
            if e[0] == "s":
                return exped, own * TILES + e[1] // 2 + 1
            return y_added, LIFT + DC * own + e[1] + 1

        def laps(eng, run):
            run(-1, opening, 0)
            with eng.Fori(0, KV - 1) as g:
                run(g, steady + change, first)
            run(KV - 1, [e for e in steady if e != ("q", PER)] + closing, first)

        def belongs_next(events, n):
            if events is opening:
                return True
            e = events[n]
            return ("k",) in events[:n] and e[0] in "vs" or e[0] == "k" or (e[0] == "t" and e[1] == 0)

        with nc.Block() as block:

            @block.sync
            def _(sp):
                def load(g, *what):
                    if "q" in what:
                        sp.dma_start(wq_raw[:, :, :], net.dram["wq"][g]).then_inc(wq_loaded, 16)
                    if "kv" in what:
                        sp.dma_start(wkv_raw[:, 0, :, :], net.dram["wk"][g]).then_inc(wkv_loaded, 16)
                        sp.dma_start(wkv_raw[:, 1, :, :], net.dram["wv"][g]).then_inc(wkv_loaded, 16)

                norm.sync(sp)
                load(0, "kv", "q")
                sp.dma_start(bq[:, :], net.dram["bq"]).then_inc(consts, 16)
                sp.dma_start(bk[:, :], net.dram["bk"]).then_inc(consts, 16)
                sp.dma_start(bv[:, :], net.dram["bv"].partition_broadcast(P)).then_inc(consts, 16)
                sp.dma_start(bo[:, :], net.dram["bo"].partition_broadcast(P)).then_inc(consts, 16)
                with sp.Fori(0, KV - 1) as g:
                    sp.wait_ge(wo_split, 1 + 4 * g)
                    sp.dma_start(wo_raw[:, :, :], net.dram["wo"][g]).then_inc(wo_loaded, 16)
                    sp.wait_ge(wkv_split, g + 1)
                    load(g + 1, "kv")
                    sp.wait_ge(wq_split, 2 * (g + 1))
                    load(g + 1, "q")
                sp.wait_ge(wo_split, 1 + 4 * (KV - 1))
                sp.dma_start(wo_raw[:, :, :], net.dram["wo"][KV - 1]).then_inc(wo_loaded, 16)

            @block.gpsimd
            def _(pool):
                def split(hi, lo, raw, highs, done):
                    shape = list(raw.shape)
                    o = one[:, :]
                    while len(o.shape) < len(shape):
                        o = o.unsqueeze(1)
                    nc.gpsimd.tensor_tensor(hi, raw, o.broadcast_to(shape), ALU.mult).then_inc(w_high, 1)
                    pool.wait_ge(w_high, highs)
                    nc.gpsimd.tensor_tensor(lo, raw, hi.bitcast(F32), ALU.subtract).then_inc(done, 1)

                def split_wkv(g, highs):
                    pool.wait_ge(wkv_loaded, 32 * (g + 1))
                    split(wkv_h[:, :, :, :], wkv_l[:, :, :, :], wkv_raw[:, :, :, :], highs, wkv_split)

                def split_wq(g, c, highs):
                    pool.wait_ge(wq_loaded, 16 * (g + 1))
                    split(wq_h[:, c, :], wq_l[:, c, :], wq_raw[:, c, :], highs, wq_split)

                def split_wo(g, k, highs):
                    pool.wait_ge(wo_loaded, 16 * (g + 1))
                    split(wo_h[:, k, :], wo_l[:, k, :], wo_raw[:, k, :], highs, wo_split)

                def normalise(count, t):
                    pool.wait_ge(inverted, count)
                    nc.gpsimd.tensor_tensor(prob[:, t % RING, :], prob[:, t % RING, :],
                                            inv_sum[:, t:t + 1].broadcast_to([P, T]), ALU.mult).then_inc(normed, 1)

                HIGHS = 1 + DC + PER

                def group(g, tiles):
                    for t in tiles:
                        normalise(g * TILES + t + 1, t % TILES)
                        base = HIGHS * g + 1 + DC
                        if 7 <= t < 7 + PER:
                            if t == 7:
                                pool.wait_ge(y_added, LIFT + DC * g)
                            split_wo(g, t - 7, base + t - 6)
                        if TILES in tiles:
                            if t == 13:
                                pool.wait_ge(v_split, g + 1)
                                split_wkv(g + 1, base + PER + 1)
                            if t in (22, 24):
                                pool.wait_ge(proj_full, proj_count(g, ("q", PER - 1)))
                                split_wq(g + 1, (t - 22) // 2, base + PER + 1 + (t - 20) // 2)
                        elif t == 16:
                            norm.wait(pool, "xc_done", TT)
                            pool.wait_ge(consts, 64)
                            nc.gpsimd.tensor_tensor(net.x[:, :, :], net.x[:, :, :],
                                                    bo[:, :].unsqueeze(1).broadcast_to([P, TT, D]), ALU.add)

                nc.gpsimd.memset(one[:, :], 1.0).then_inc(ready, 1)
                nc.gpsimd.memset(net.delta[:, :, :], 0.0).then_inc(ready, 1)
                pool.sem_inc(wo_split, 1)
                pool.wait_ge(ready, 2)
                split_wkv(0, 1)
                for c in range(DC):
                    split_wq(0, c, 2 + c)
                for t in range(LEAD // 2):
                    normalise(t + 1, t)
                with pool.Fori(0, KV - 1) as g:
                    group(g, range(LEAD // 2, TILES + LEAD // 2))
                group(KV - 1, range(LEAD // 2, TILES))

            @block.tensor
            def _(pe):
                def run(g, events, start):
                    jobs = jobs_of(events)
                    spots = [n for n, e in enumerate(events) if e in jobs and (e[0] in "kvqy" or e[1] % 2 == 0)]
                    before = jobs_of(steady + change)[-2:]
                    n = start - 1

                    def begin(place):
                        k = spots.index(place)
                        if k >= 2:
                            q = spots[k - 2]
                            sem_, count = read_of(g, events[q], belongs_next(events, q))
                        elif start == 0:
                            return
                        elif isinstance(g, int):
                            sem_, count = read_of(g - 1, before[k], False)
                        else:
                            sem_, count = read_before(g, k)
                        pe.wait_ge(sem_, count)

                    def read_before(g, k):
                        return y_added, LIFT + DC * g - DC + k + 1

                    if start and not (isinstance(g, int)):
                        pe.wait_ge(exped, TILES * g + LEAD // 2)

                    for place, e in enumerate(events):
                        nxt = belongs_next(events, place)
                        own = g + 1 if nxt else g
                        if place in spots:
                            begin(place)
                            n += 1
                        if e[0] in "kq":
                            if e[0] == "k":
                                pe.wait_ge(wkv_split, g + 2)
                            elif start == 0 or e[1] == PER:
                                pe.wait_ge(wq_split, DC * (g + 2))
                            for b in range(NB):
                                cols = slice(b * BANK, (b + 1) * BANK)
                                for c in range(DC):
                                    hh = slice(e[1] % PER * DH, (e[1] % PER + 1) * DH) if e[0] == "q" else None
                                    wt = (wkv_h[:, 0, c, :], wkv_l[:, 0, c, :]) if e[0] == "k" else \
                                        (wq_h[:, c, hh], wq_l[:, c, hh])
                                    last = product(nc, slot(n)[:, b, :], *wt, xn_h[:, c, cols], xn_l[:, c, cols],
                                                   c == 0, c == DC - 1)
                            last.then_inc(proj_full, 1)
                        if e[0] == "v":
                            for i in range(TT):
                                toks = slice(i * P, (i + 1) * P)
                                for c in range(DC):
                                    last = product(nc, slot(n)[:, i // 4, (i % 4) * P:(i % 4 + 1) * P], xn_h[:, c, toks],
                                                   xn_l[:, c, toks], wkv_h[:, 1, c, :], wkv_l[:, 1, c, :], c == 0, c == DC - 1)
                            last.then_inc(values_full, 1)
                        if e[0] == "s":
                            t, b = divmod(e[1], 2)
                            hh, i = divmod(t, TT)
                            if e[1] % (2 * TT) == 0:
                                pe.wait_ge(proj_split, 2 + PROJ * own + hh)
                            keys = slice(b * BANK, (b + 1) * BANK)
                            last = product(nc, slot(n)[:, b, :], q_h[:, hh % 2, i * P:(i + 1) * P],
                                           q_l[:, hh % 2, i * P:(i + 1) * P], k_h[:, keys], k_l[:, keys], True, True)
                            if b == 1:
                                last.then_inc(s_full, 1)
                        if e[0] == "t":
                            u, kt = divmod(e[1], KT)
                            if kt == 0:
                                pe.wait_ge(normed, own * TILES + 4 * u + 4)
                            pe.wait_ge(pt_split, LIFT + own * STEPS + e[1] - 1)
                            for i in range(4):
                                last = nc.tensor.transpose(turned(e[1])[:, i * P:(i + 1) * P],
                                                           prob[:, (4 * u + i) % RING, kt * P:(kt + 1) * P], net.ident[:, :])
                            last.then_inc(pt_full, 1)
                        if e[0] == "p":
                            u, kt = divmod(e[1], KT)
                            if e[1] == 0:
                                pe.wait_ge(v_split, g + 1)
                            if kt == 0:
                                pe.wait_ge(o_split, LIFT + g * UNITS + u - 1)
                            pe.wait_ge(pt_split, LIFT + g * STEPS + e[1] + 1)
                            keys = slice(kt * P, (kt + 1) * P)
                            product(nc, o_bank(u), v_h[:, keys], v_l[:, keys], pt_h[:, e[1] % 2, :], pt_l[:, e[1] % 2, :],
                                    kt == 0, kt == KT - 1).then_inc(pv_done, 1)
                        if e[0] == "y":
                            if e[1] == 0:
                                pe.wait_ge(wo_split, 1 + 4 * (g + 1))
                                pe.wait_ge(o_split, LIFT + UNITS * (g + 1))
                            for b in range(NB):
                                cols = slice(b * BANK, (b + 1) * BANK)
                                for hh in range(PER):
                                    part = slice(e[1] * P, (e[1] + 1) * P)
                                    last = product(nc, slot(n)[:, b, :], wo_h[:, hh, part], wo_l[:, hh, part],
                                                   o_h[:, hh, cols], o_l[:, hh, cols], hh == 0, hh == PER - 1)
                            last.then_inc(y_full, 1)

                for s in lifted["pe"]:
                    pe.sem_inc(s, LIFT)
                norm.tensor(pe)
                norm.wait_parts(pe)
                laps(pe, run)

            @block.scalar
            def _(act):
                def run(g, events, start):
                    waiting = []
                    later = []
                    n = start - 1

                    def highs(least):
                        while later and later[0][1] >= least:
                            e, _ = later.pop(0)
                            to = k_h[:, :] if e[0] == "k" else q_h[:, e[1] % 2, :]
                            act.wait_ge(proj_read, proj_count(g, e))
                            nc.scalar.activation(to, proj[:, :], ACT.Copy).then_inc(proj_high, 1)

                    def exps():
                        for own, t, k in waiting:
                            act.wait_ge(maxed, own * TILES + t + 1)
                            u = t // 4
                            act.wait_ge(pt_full, LIFT + own * STEPS + KT * (u - 1))
                            nc.scalar.activation(halves(prob[:, t % RING, :]), slot(k), ACT.Exp, bias=neg_max[:, t:t + 1],
                                                 accum_out=row_sum[:, t:t + 1]).then_inc(exped, 1)
                        waiting.clear()

                    for place, e in enumerate(events):
                        own = g + 1 if belongs_next(events, place) else g
                        if e in jobs_of([e]):
                            n += 1
                        if e[0] in "kq":
                            exps()
                            count = proj_count(g, e)
                            act.wait_ge(proj_full, count)
                            if not (isinstance(g, int) and count == 1):
                                act.wait_ge(proj_split, count - 1)
                            if e[0] == "k":
                                ins = nc.scalar.activation(halves(proj[:, :]), slot(n), ACT.Identity,
                                                           bias=bk[:, bass.ds(g + 1, 1)])
                            else:
                                h = 0 if start == 0 else g * PER + e[1]
                                ins = nc.scalar.activation(halves(proj[:, :]), slot(n), ACT.Identity,
                                                           bias=bq[:, bass.ds(h, 1)], scale=Q_SCALE)
                            ins.then_inc(proj_read, 1)
                            later.append([e, 0])
                            highs(0 if start == 0 else 1)
                        if e[0] == "s" and e[1] % 2 == 1:
                            exps()
                            waiting.append((own, e[1] // 2, n))
                        if e[0] == "t":
                            act.wait_ge(pt_full, LIFT + own * STEPS + e[1] + 1)
                            act.wait_ge(pv_done, LIFT + own * STEPS + e[1] - 1)
                            nc.scalar.activation(pt_h[:, e[1] % 2, :], turned(e[1]), ACT.Copy).then_inc(pt_high, 1)
                            exps()
                            for w in later:
                                w[1] += 1
                            highs(2)
                        if e[0] == "p" and e[1] % KT == KT - 1:
                            u = e[1] // KT
                            if u == 0:
                                act.wait_ge(y_added, LIFT + DC * g)
                            act.wait_ge(pv_done, LIFT + g * STEPS + e[1] + 1)
                            nc.scalar.activation(o_h[:, u // NB, (u % NB) * BANK:(u % NB + 1) * BANK], o_bank(u),
                                                 ACT.Copy).then_inc(o_high, 1)
                    exps()
                    highs(0)

                norm.scalar(act)
                act.wait_ge(bq_scaled, 1)
                act.wait_ge(consts, 64)
                laps(act, run)

            @block.vector
            def _(dve):
                def run(g, events, start):
                    n = start - 1
                    waiting = []
                    later = []

                    def inverts(least):
                        while waiting and waiting[0][2] >= least:
                            own, t, _ = waiting.pop(0)
                            dve.wait_ge(exped, own * TILES + t + 1)
                            nc.vector.reciprocal(inv_sum[:, t:t + 1], row_sum[:, t:t + 1]).then_inc(inverted, 1)

                    def lows(least):
                        while later and later[0][1] >= least:
                            e, _ = later.pop(0)
                            dve.wait_ge(proj_high, proj_count(g, e))
                            hi, lo = (k_h[:, :], k_l[:, :]) if e[0] == "k" else (q_h[:, e[1] % 2, :], q_l[:, e[1] % 2, :])
                            nc.vector.tensor_tensor(lo, proj[:, :], hi.bitcast(F32), ALU.subtract).then_inc(proj_split, 1)

                    for place, e in enumerate(events):
                        own = g + 1 if belongs_next(events, place) else g
                        if e in jobs_of([e]):
                            n += 1
                        if e[0] in "kq":
                            later.append([e, 0])
                            lows(0 if start == 0 else 1)
                        if e[0] == "v":
                            dve.wait_ge(values_full, own + 1)
                            if start:
                                dve.wait_ge(v_split, g + 1)
                            nc.vector.tensor_tensor(v_full[:, :].rearrange("p (i d) -> p i d", d=DH),
                                                    slot(n).rearrange("p n (i d) -> p (n i) d", d=DH),
                                                    bv[:, bass.ds(own * DH, DH)].unsqueeze(1).broadcast_to([P, TT, DH]),
                                                    ALU.add).then_inc(v_added, 1)
                        if e[0] == "vs":
                            if start:
                                dve.wait_ge(pv_done, LIFT + STEPS * (g + 1))
                            dve.wait_ge(v_added, own + 1)
                            nc.vector.tensor_copy(v_h[:, :], v_full[:, :]).then_inc(v_high, 1)
                            dve.wait_ge(v_high, own + 1)
                            nc.vector.tensor_tensor(v_l[:, :], v_full[:, :], v_h[:, :].bitcast(F32), ALU.subtract)\
                                .then_inc(v_split, 1)
                        if e[0] == "s" and e[1] % 2 == 1:
                            t = e[1] // 2
                            dve.wait_ge(s_full, own * TILES + t + 1)
                            nc.vector.tensor_reduce(neg_max[:, t:t + 1], slot(n), AX.XY, ALU.max, negate=True).then_inc(maxed, 1)
                            inverts(0)
                            waiting.append([own, t, 0])
                        if e[0] == "t":
                            for w in waiting:
                                w[2] += 1
                            inverts(2)
                            dve.wait_ge(pt_high, own * STEPS + e[1] + 1)
                            nc.vector.tensor_tensor(pt_l[:, e[1] % 2, :], turned(e[1]), pt_h[:, e[1] % 2, :].bitcast(F32),
                                                    ALU.subtract).then_inc(pt_split, 1)
                            for w in later:
                                w[1] += 1
                            lows(3)
                        if e[0] == "p" and e[1] % KT == KT - 1:
                            u = e[1] // KT
                            dve.wait_ge(o_high, g * UNITS + u + 1)
                            cols = slice((u % NB) * BANK, (u % NB + 1) * BANK)
                            nc.vector.tensor_tensor(o_l[:, u // NB, cols], o_bank(u), o_h[:, u // NB, cols].bitcast(F32),
                                                    ALU.subtract).then_inc(o_split, 1)
                        if e[0] == "y":
                            dve.wait_ge(y_full, DC * g + e[1] + 1)
                            dve.wait_ge(y_added, LIFT + DC * g)
                            nc.vector.tensor_tensor(halves(net.delta[:, e[1], :]), halves(net.delta[:, e[1], :]), slot(n),
                                                    ALU.add).then_inc(y_added, 1)
                    inverts(0)
                    lows(0)

                for s in lifted["dve"]:
                    dve.sem_inc(s, LIFT)
                norm.vector(dve)
                dve.wait_ge(consts, 64)
                nc.vector.tensor_scalar(bq[:, :], bq[:, :], Q_SCALE, None, ALU.mult).then_inc(bq_scaled, 1)
                dve.wait_ge(ready, 2)
                laps(dve, run)
                dve.wait_ge(y_added, LIFT + DC * KV)


EXP0, GROUPS, LAT, INTER, SHARED0 = 32, 4, 128, 128, 512
ROUTED_SCALE = 2.5
SH0 = SHARED0 // P
BIG, TAKEN = 1e30, 3e38


def squared_relu_experts_phase(nc, net):
    BODY, RAW, RING, ROWS = 8, 4, 4, 2
    SPLIT_LAG, DOWN_LAG, AHEAD = 2, 4, 2
    EG = EXP0 // GROUPS
    with ExitStack() as mem:
        sb = lambda n, s, d=F32: mem.enter_context(nc.sbuf_tensor(f"f0_{n}", s, d))
        sem = lambda n: net.ctx.enter_context(nc.semaphore(f"f0_{n}"))
        ps, xn, xn_h, xn_l = net.ps, net.xn, net.xn_h, net.xn_l
        gate, gate_bias = sb("gate", [P, DC, EXP0]), sb("gate_bias", [P, EXP0])
        FC1, UP, DOWN, FC2 = 0, DC * LAT, DC * (LAT + SHARED0), DC * (LAT + SHARED0) + SH0 * D
        PIECES = (("fc1", FC1, UP), ("sup0", UP, DOWN), ("sdn0", DOWN, FC2), ("fc2", FC2, FC2 + D))
        w = sb("w", [P, FC2 + D])
        w_h, w_l = sb("w_h", [P, FC2 + D], F32R), sb("w_l", [P, FC2 + D], F32R)
        e_raw = sb("e_raw", [P, RAW, 2, P])
        e_h, e_l = sb("e_h", [P, BODY, 2, P], F32R), sb("e_l", [P, BODY, 2, P], F32R)
        lat_h, lat_l = sb("lat_h", [P, T], F32R), sb("lat_l", [P, T], F32R)
        relu, act = sb("relu", [P, 2, T]), sb("act", [P, RING, T])
        a_h, a_l = sb("a_h", [P, RING, T], F32R), sb("a_l", [P, RING, T], F32R)
        s_h, s_l = sb("s_h", [P, SH0, T], F32R), sb("s_l", [P, SH0, T], F32R)
        cw_row = sb("cw_row", [P, ROWS, T])
        score, biased = sb("score", [P, TT, EXP0]), sb("biased", [P, TT, EXP0])
        best, found = sb("best", [P, TT, GROUPS, 8]), sb("found", [P, TT, EXP0])
        g_score, g_out = sb("g_score", [P, TT, GROUPS + 6]), sb("g_out", [P, TT, GROUPS + 6])
        g_best, g_take = sb("g_best", [P, TT, 8]), sb("g_take", [P, TT, 8])
        cw, total = sb("cw", [P, TT, EXP0]), sb("total", [P, TT])
        cw_t = sb("cw_t", [EXP0, T])
        cw_dram = net.cw_dram[0]
        norm = Norm(nc, net, "n1", mem, True, True, cw_row[:, :, :].rearrange("p r (k d) -> p (r k) d", d=D))

        consts, w_loaded = sem("consts"), [sem(f"w_loaded_{p[0]}") for p in PIECES]
        w_high, w_split = sem("w_high"), sem("w_split")
        logits, scored, routed = sem("logits"), sem("scored"), sem("routed")
        cw_turned, cw_copied, cw_stored = sem("cw_turned"), sem("cw_copied"), sem("cw_stored")
        e_loaded = [sem(f"e_loaded{r}") for r in range(RAW)]
        row_loaded = [sem(f"row_loaded{r}") for r in range(ROWS)]
        e_high, e_split = sem("e_high"), sem("e_split")
        slot_full = sem("slot_full")
        lat_high, lat_split = sem("lat_high"), sem("lat_split")
        relued, squared, weighed = sem("relued"), sem("squared"), sem("weighed")
        act_high, act_split, down_done = sem("act_high"), sem("act_split"), sem("down_done")
        shared_full, shared_copied = sem("shared_full"), sem("shared_copied")
        y_full, y_added, chain = sem("y_full"), sem("y_added"), sem("chain")

        def slot(n):
            return ps[:, 2 * (n % 2):2 * (n % 2) + 2, :]

        def blocks(ap):
            return ap.rearrange("p (n t) -> p n t", n=NB)

        def steps(eng, loop_end, last, step):
            for n in range(BODY):
                step(0, n)
            with eng.Fori(1, loop_end) as it:
                for r in range(BODY):
                    step(it, r)
            for n in range(loop_end * BODY, last):
                step(*divmod(n, BODY))

        def known(it, r, low, high=EXP0 + BODY):
            return not isinstance(it, int) or low <= it * BODY + r < high

        with nc.Block() as block:

            @block.sync
            def _(sp):
                for k, (name, at, end) in enumerate(PIECES):
                    sp.dma_start(w[:, at:end], net.dram[name]).then_inc(w_loaded[k], 16)
                sp.dma_start(gate[:, :, :], net.dram["gate0"]).then_inc(consts, 16)
                sp.dma_start(gate_bias[:, :], net.dram["gate_bias"].partition_broadcast(P)).then_inc(consts, 16)

                def load_expert(it, r):
                    n = it * BODY + r
                    if known(it, r, RAW):
                        sp.wait_ge(e_split, n - RAW + 1)
                    sp.dma_start(e_raw[:, r % RAW, :, :], net.dram["we0"][n]).then_inc(e_loaded[r % RAW], 16)

                def load_row(it, r):
                    n = it * BODY + r
                    if known(it, r, ROWS):
                        sp.wait_ge(weighed, n - ROWS + 1)
                    sp.dma_start(cw_row[:, r % ROWS, :], cw_dram[n].partition_broadcast(P))\
                        .then_inc(row_loaded[r % ROWS], 16)

                for r in range(RAW):
                    load_expert(0, r)
                sp.wait_ge(cw_copied, 1)
                sp.dma_start(cw_dram, cw_t[:, :]).then_inc(cw_stored, 16)
                sp.wait_ge(cw_stored, 16)

                def step(it, r):
                    load_row(it, r)
                    if known(it, r, 0, EXP0 - RAW):
                        load_expert(it, r + RAW)

                steps(sp, EXP0 // BODY - 1, EXP0, step)

            @block.tensor
            def _(pe):
                norm.tensor(pe)
                pe.wait_ge(consts, 34)
                norm.wait_parts(pe)
                norm.wait_full(pe)
                for i in range(TT):
                    for c in range(DC):
                        last = nc.tensor.matmul(ps[:, 6, i * EXP0:(i + 1) * EXP0], xn[:, c, i * P:(i + 1) * P],
                                                gate[:, c, :], start=c == 0, stop=c == DC - 1)
                last.then_inc(logits, 1)

                def project(n, at, width, k):
                    for b in range(NB):
                        cols = slice(b * BANK, (b + 1) * BANK)
                        for c in range(DC):
                            part = slice(at + c * width + k * P, at + c * width + (k + 1) * P)
                            last = product(nc, slot(n)[:, b, :], w_h[:, part], w_l[:, part], xn_h[:, c, cols],
                                           xn_l[:, c, cols], c == 0, c == DC - 1)
                    last.then_inc(slot_full, 1)

                pe.wait_ge(w_split, 2)
                project(0, FC1, LAT, 0)
                for k in range(SH0):
                    if k == 1:
                        pe.wait_ge(lat_split, 1)
                    if k > 1:
                        pe.wait_ge(squared, k - 1)
                    project(1 + k, UP, SHARED0, k)
                pe.wait_ge(routed, 1)
                for i in range(TT):
                    last = nc.tensor.transpose(ps[0:EXP0, 6 + i // 4, (i % 4) * P:(i % 4 + 1) * P], cw[:, i, :], net.ident[:, :])
                last.then_inc(cw_turned, 1)
                pe.wait_ge(w_split, 4)
                pe.wait_ge(act_split, SH0)
                for m in range(DC):
                    if m == 1:
                        pe.wait_ge(cw_copied, 1)
                    for b in range(NB):
                        cols = slice(b * BANK, (b + 1) * BANK)
                        for k in range(SH0):
                            part = slice(DOWN + k * D + m * P, DOWN + k * D + (m + 1) * P)
                            last = product(nc, ps[:, 4 + 2 * m + b, :], w_h[:, part], w_l[:, part], s_h[:, k, cols],
                                           s_l[:, k, cols], k == 0, k == SH0 - 1)
                    last.then_inc(shared_full, 1)

                def step(it, r):
                    n = it * BODY + r
                    if known(it, r, 0, EXP0):
                        pe.wait_ge(e_split, n + 1)
                        pe.wait_ge(squared, n + SH0 - 1)
                        for b in range(NB):
                            cols = slice(b * BANK, (b + 1) * BANK)
                            last = product(nc, slot(1 + SH0 + r)[:, b, :], e_h[:, r, 0, :], e_l[:, r, 0, :],
                                           lat_h[:, cols], lat_l[:, cols], True, True)
                        last.then_inc(slot_full, 1)
                    if known(it, r, DOWN_LAG):
                        m = (r - DOWN_LAG) % BODY
                        pe.wait_ge(act_split, n - DOWN_LAG + 1 + SH0)
                        first = it == 0 and r == DOWN_LAG if isinstance(it, int) else False
                        final = n == EXP0 - 1 + DOWN_LAG if isinstance(it, int) else False
                        if first:
                            pe.wait_ge(shared_copied, 1)
                        for b in range(NB):
                            cols = slice(b * BANK, (b + 1) * BANK)
                            last = product(nc, ps[:, 4 + b, :], e_h[:, m, 1, :], e_l[:, m, 1, :], a_h[:, m % RING, cols],
                                           a_l[:, m % RING, cols], first, final)
                        last.then_inc(down_done, 1)

                steps(pe, EXP0 // BODY, EXP0 + DOWN_LAG, step)
                pe.wait_ge(squared, SH0 + EXP0)
                pe.wait_ge(lat_split, 2)
                for m in range(DC):
                    for b in range(NB):
                        cols = slice(b * BANK, (b + 1) * BANK)
                        part = slice(FC2 + m * P, FC2 + (m + 1) * P)
                        last = product(nc, ps[:, 2 * m + b, :], w_h[:, part], w_l[:, part], lat_h[:, cols], lat_l[:, cols],
                                       True, True)
                        last.then_inc(y_full, 1)

            @block.scalar
            def _(act_e):
                for k, (_, at, end) in enumerate(PIECES):
                    act_e.wait_ge(w_loaded[k], 16)
                    nc.scalar.activation(w_h[:, at:end], w[:, at:end], ACT.Copy).then_inc(w_high, 1)
                norm.scalar(act_e)
                act_e.wait_ge(logits, 1)
                nc.scalar.activation(score[:, :, :], ps[:, 6, 0:TT * EXP0].rearrange("p (i e) -> p i e", e=EXP0),
                                     ACT.Sigmoid).then_inc(scored, 1)
                act_e.wait_ge(slot_full, 1)
                nc.scalar.activation(blocks(lat_h[:, :]), slot(0), ACT.Copy).then_inc(lat_high, 1)

                def relu_slot(n, k):
                    act_e.wait_ge(slot_full, n + 2)
                    if not isinstance(n, int) or n >= 2:
                        act_e.wait_ge(squared, n - 1)
                    nc.scalar.activation(blocks(relu[:, k % 2, :]), slot(1 + k), ACT.Relu).then_inc(relued, 1)

                def high_weights(it, r):
                    act_e.wait_ge(e_loaded[r % RAW], 16 * (it * (BODY // RAW) + r // RAW) + 16)
                    if known(it, r, BODY):
                        act_e.wait_ge(down_done, it * BODY + (r - BODY + 1))
                    nc.scalar.activation(e_h[:, r % BODY, :, :], e_raw[:, r % RAW, :, :], ACT.Copy).then_inc(e_high, 1)

                for k in range(SH0):
                    relu_slot(k, k)
                    act_e.wait_ge(squared, k + 1)
                    nc.scalar.activation(s_h[:, k, :], act[:, k % RING, :], ACT.Copy).then_inc(act_high, 1)
                for r in range(AHEAD):
                    high_weights(0, r)
                for m in range(DC):
                    act_e.wait_ge(shared_full, m + 1)
                    nc.scalar.activation(blocks(net.delta[:, m, :]), ps[:, 4 + 2 * m:6 + 2 * m, :], ACT.Copy)\
                        .then_inc(shared_copied, 1)

                def step(it, r):
                    n = it * BODY + r
                    if known(it, r, 0, EXP0):
                        relu_slot(n + SH0, r + SH0)
                    if known(it, r, 0, EXP0 - AHEAD):
                        high_weights(it, r + AHEAD)
                    if known(it, r, SPLIT_LAG):
                        m = (r - SPLIT_LAG) % RING
                        act_e.wait_ge(weighed, n - SPLIT_LAG + 1)
                        if known(it, r, SPLIT_LAG + RING):
                            act_e.wait_ge(down_done, n - SPLIT_LAG - RING + 1)
                        nc.scalar.activation(a_h[:, m, :], act[:, m, :], ACT.Copy).then_inc(act_high, 1)

                steps(act_e, EXP0 // BODY - 1, EXP0 + SPLIT_LAG, step)
                act_e.wait_ge(down_done, EXP0)
                nc.scalar.activation(blocks(lat_h[:, :]), ps[:, 4:6, :], ACT.Copy).then_inc(lat_high, 1)

            @block.gpsimd
            def _(pool):
                nc.gpsimd.memset(g_score[:, :, :], -BIG).then_inc(consts, 1)
                nc.gpsimd.memset(g_take[:, :, :], -BIG).then_inc(consts, 1)
                for k, (_, at, end) in enumerate(PIECES):
                    pool.wait_ge(w_high, k + 1)
                    nc.gpsimd.tensor_tensor(w_l[:, at:end], w[:, at:end], w_h[:, at:end].bitcast(F32), ALU.subtract)\
                        .then_inc(w_split, 1)

                def step(it, r):
                    pool.wait_ge(row_loaded[r % ROWS], 16 * (it * (BODY // ROWS) + r // ROWS) + 16)
                    pool.wait_ge(squared, it * BODY + r + SH0 + 1)
                    nc.gpsimd.tensor_tensor(act[:, r % RING, :], act[:, r % RING, :], cw_row[:, r % ROWS, :],
                                            ALU.mult).then_inc(weighed, 1)

                steps(pool, EXP0 // BODY, EXP0, step)

            @block.vector
            def _(dve):
                links = [0]

                def link(ins):
                    ins.then_inc(chain, 1)
                    links[0] += 1
                    dve.wait_ge(chain, links[0])

                norm.vector(dve)
                dve.wait_ge(consts, 34)
                dve.wait_ge(scored, 1)
                link(nc.vector.tensor_tensor(biased[:, :, :], score[:, :, :],
                                             gate_bias[:, :].unsqueeze(1).broadcast_to([P, TT, EXP0]), ALU.add))
                for i in range(TT):
                    for g in range(GROUPS):
                        last = nc.vector.max(best[:, i, g, :], biased[:, i, g * EG:(g + 1) * EG])
                link(last)
                dve.wait_ge(lat_high, 1)
                nc.vector.tensor_tensor(blocks(lat_l[:, :]), slot(0), blocks(lat_h[:, :]).bitcast(F32),
                                        ALU.subtract).then_inc(lat_split, 1)

                def square(n, k):
                    if not isinstance(n, int) or n >= RING:
                        dve.wait_ge(act_split, n - RING + 1)
                    dve.wait_ge(relued, n + 1)
                    nc.vector.scalar_tensor_tensor(blocks(act[:, k % RING, :]), slot(1 + k), 0.0, blocks(relu[:, k % 2, :]),
                                                   ALU.max, ALU.mult).then_inc(squared, 1)

                def split_shared(k):
                    dve.wait_ge(act_high, k + 1)
                    nc.vector.tensor_tensor(s_l[:, k, :], act[:, k % RING, :], s_h[:, k, :].bitcast(F32),
                                            ALU.subtract).then_inc(act_split, 1)

                link(nc.vector.tensor_tensor(g_score[:, :, 0:GROUPS], best[:, :, :, 0], best[:, :, :, 1], ALU.add))
                square(0, 0)
                for i in range(TT):
                    last = nc.vector.max(g_best[:, i, :], g_score[:, i, 0:8])
                link(last)
                link(nc.vector.tensor_copy(g_take[:, :, 0:2], g_best[:, :, 0:2]))
                split_shared(0)
                square(1, 1)
                for i in range(TT):
                    last = nc.vector.match_replace(g_out[:, i, :], g_take[:, i, :], g_score[:, i, :], TAKEN)
                link(last)
                link(nc.vector.tensor_scalar(g_out[:, :, :], g_out[:, :, :], TAKEN, None, ALU.is_equal))
                link(nc.vector.tensor_scalar(g_out[:, :, :], g_out[:, :, :], 1.0, BIG, ALU.subtract, ALU.mult))
                link(nc.vector.tensor_tensor(biased[:, :, :].rearrange("p i (g e) -> p i g e", g=GROUPS),
                                             biased[:, :, :].rearrange("p i (g e) -> p i g e", g=GROUPS),
                                             g_out[:, :, 0:GROUPS].unsqueeze(3).broadcast_to([P, TT, GROUPS, EG]), ALU.add))
                split_shared(1)
                square(2, 2)
                for i in range(TT):
                    last = nc.vector.max(g_best[:, i, :], biased[:, i, :])
                link(last)
                for i in range(TT):
                    last = nc.vector.match_replace(found[:, i, :], g_best[:, i, :], biased[:, i, :], TAKEN)
                link(last)
                link(nc.vector.scalar_tensor_tensor(cw[:, :, :], found[:, :, :], TAKEN, score[:, :, :], ALU.is_equal, ALU.mult))
                link(nc.vector.tensor_reduce(total[:, :], cw[:, :, :], AX.X, ALU.add))
                link(nc.vector.reciprocal(total[:, :], total[:, :]))
                nc.vector.scalar_tensor_tensor(cw[:, :, :], cw[:, :, :], ROUTED_SCALE,
                                               total[:, :].unsqueeze(2).broadcast_to([P, TT, EXP0]), ALU.mult, ALU.mult)\
                    .then_inc(routed, 1)
                split_shared(2)
                square(3, 3)
                split_shared(3)
                dve.wait_ge(cw_turned, 1)
                nc.vector.tensor_copy(blocks(cw_t[:, :]), ps[0:EXP0, 6:8, :]).then_inc(cw_copied, 1)

                def low_weights(it, r):
                    dve.wait_ge(e_high, it * BODY + r + 1)
                    nc.vector.tensor_tensor(e_l[:, r % BODY, :, :], e_raw[:, r % RAW, :, :], e_h[:, r % BODY, :, :].bitcast(F32),
                                            ALU.subtract).then_inc(e_split, 1)

                for r in range(AHEAD):
                    low_weights(0, r)

                def step(it, r):
                    n = it * BODY + r
                    if known(it, r, 0, EXP0):
                        square(n + SH0, r + SH0)
                    if known(it, r, 0, EXP0 - AHEAD):
                        low_weights(it, r + AHEAD)
                    if known(it, r, SPLIT_LAG):
                        m = (r - SPLIT_LAG) % RING
                        dve.wait_ge(act_high, n - SPLIT_LAG + 1 + SH0)
                        nc.vector.tensor_tensor(a_l[:, m, :], act[:, m, :], a_h[:, m, :].bitcast(F32),
                                                ALU.subtract).then_inc(act_split, 1)

                steps(dve, EXP0 // BODY - 1, EXP0 + SPLIT_LAG, step)
                dve.wait_ge(lat_high, 2)
                nc.vector.tensor_tensor(blocks(lat_l[:, :]), ps[:, 4:6, :], blocks(lat_h[:, :]).bitcast(F32),
                                        ALU.subtract).then_inc(lat_split, 1)
                dve.wait_ge(shared_copied, DC)
                for n in range(DC * NB):
                    m, b = divmod(n, NB)
                    dve.wait_ge(y_full, n + 1)
                    part = net.delta[:, m, b * BANK:(b + 1) * BANK]
                    nc.vector.tensor_tensor(part, part, ps[:, n, :], ALU.add).then_inc(y_added, 1)
                dve.wait_ge(y_added, DC * NB)


H1, HD, CHUNK = 16, 16, 128
ROPE_BASE, RMS_EPS = 10000.0, 1e-6


def decay_tables():
    half = HD // 2
    theta = ROPE_BASE ** (-2.0 * np.arange(half, dtype=np.float32) / HD)
    angle = (np.arange(T, dtype=np.float32)[:, None] * theta.astype(np.float32)[None, :]).astype(np.float32)
    cos, sin = np.cos(angle), np.sin(angle)
    by_tile = lambda a: a.reshape(TT, P, -1).transpose(1, 0, 2)
    log_lam = -(2.0 ** (-8.0 * (np.arange(H1, dtype=np.float32) + 1.0) / H1))
    at = np.arange(CHUNK, dtype=np.float32)
    diff = at[None, :] - at[:, None]
    decay = np.where(diff[:, None, :] >= 0, np.exp(np.minimum(log_lam[None, :, None] * diff[:, None, :], 0)), 0)
    head = np.arange(P) // HD
    return {
        "cos": by_tile(np.concatenate([cos, cos], 1)), "sin": by_tile(np.concatenate([-sin, sin], 1)),
        "decay": decay,
        "decay_q": np.exp(log_lam[None, :] * (at[:, None] + 1)),
        "decay_k": np.exp(log_lam[None, :] * (CHUNK - 1 - at[:, None])),
        "lam_c": np.exp(log_lam.reshape(DC, P // HD)[:, head].T * CHUNK),
        "same_head": (head[:, None] == head[None, :]) * 1.0,
        "in_pair": (head[:, None] % 2 == np.arange(2)[None, :]) * 1.0,
    }


def linear_attention_phase(nc, net):
    QK, VG = 2 * D, D + HD
    W = QK + VG
    PAIRS = P // 32
    with ExitStack() as mem:
        sb = lambda n, s, d=F32: mem.enter_context(nc.sbuf_tensor(f"la_{n}", s, d))
        sem = lambda n: net.ctx.enter_context(nc.semaphore(f"la_{n}"))
        ps, xn_h, xn_l = net.ps, net.xn_h, net.xn_l
        w, w_h, w_l = sb("w", [P, DC, W]), sb("w_h", [P, DC, W], F32R), sb("w_l", [P, DC, W], F32R)
        wo, wo_h, wo_l = sb("wo", [P, DC, D]), sb("wo_h", [P, DC, D], F32R), sb("wo_l", [P, DC, D], F32R)
        wg2, weight = sb("wg2", [HD, D]), sb("weight", [P, D])
        cos, sin = sb("cos", [P, TT, HD]), sb("sin", [P, TT, HD])
        decay = sb("decay", [P, H1, CHUNK])
        decay_q, decay_k = sb("decay_q", [P, H1]), sb("decay_k", [P, H1])
        lam_c, same_head, in_pair = sb("lam_c", [P, DC]), sb("same_head", [P, P]), sb("in_pair", [P, 2])
        act = sb("act", [P, 2, QK])
        by_cos, by_sin = sb("by_cos", [P, 2, QK]), sb("by_sin", [P, 2, QK])
        rot = sb("rot", [P, 2, QK])
        v, g1 = sb("v", [P, TT, D]), sb("g1", [P, TT, HD])
        kd = sb("kd", [P, 4, D])
        q_t = sb("q_t", [P, 4, DC, P])
        qp_h, qp_l = sb("qp_h", [P, 2, DC, 2, P], F32R), sb("qp_l", [P, 2, DC, 2, P], F32R)
        k_h, k_l = sb("k_h", [P, 2, DC, P], F32R), sb("k_l", [P, 2, DC, P], F32R)
        sc = sb("sc", [P, 2, H1, CHUNK])
        state, kv = sb("state", [P, DC, P]), sb("kv", [P, DC, P])
        inter = sb("inter", [P, 2, D])
        o, gate, sq = sb("o", [P, TT, D]), sb("gate", [P, TT, D]), sb("sq", [P, TT, D])
        g1_t = sb("g1_t", [HD, T])
        ms, rms, root = sb("ms", [P, TT, H1]), sb("rms", [P, TT, H1]), sb("root", [P, 2, TT * H1])
        o_h, o_l = sb("o_h", [P, DC, T], F32R), sb("o_l", [P, DC, T], F32R)

        w_loaded, consts = sem("w_loaded"), sem("consts")
        w_high, w_split = sem("w_high"), sem("w_split")
        projected, act_done, v_done = sem("projected"), sem("act_done"), sem("v_done")
        cos_done, sin_done, rotated, kd_done = sem("cos_done"), sem("sin_done"), sem("rotated"), sem("kd_done")
        turned, t_high, t_split = sem("turned"), sem("t_high"), sem("t_split")
        sc_full, sc_done = sem("sc_full"), sem("sc_done")
        out_full, kv_masked, state_done = sem("out_full"), sem("kv_masked"), sem("state_done")
        inter_done, o_done = sem("inter_done"), sem("o_done")
        g1_turned, g1_copied, gate_full, gate_done = sem("g1_turned"), sem("g1_copied"), sem("gate_full"), sem("gate_done")
        gated, squares, weighted, chain = sem("gated"), sem("squares"), sem("weighted"), sem("chain")
        o_turned, o_high, o_split = sem("o_turned"), sem("o_high"), sem("o_split")
        y_full, y_copied = sem("y_full"), sem("y_copied")

        norm = Norm(nc, net, "n2", mem, True, False, sq[:, :, :])
        SCORE_BANKS = [5, 6, 7, 4]
        STEPS = TT + 3
        HALF = TT // 2

        def heads(ap):
            return ap.rearrange("p (h e) -> p h e", e=HD)

        def of_pair(ap, r):
            return ap.rearrange("p (c r j) t -> p c r (j t)", c=DC, j=2)[:, :, r, :]

        with nc.Block() as block:

            @block.sync
            def _(sp):
                sp.dma_start(w[:, :, :], net.dram["w1a"]).then_inc(w_loaded, 16)
                sp.dma_start(wo[:, :, :], net.dram["wo1"]).then_inc(w_loaded, 16)
                for to, name in ((cos[:, :, :], "cos"), (sin[:, :, :], "sin"), (decay_k[:, :], "decay_k"),
                                 (in_pair[:, :], "in_pair"), (decay[:, :, :], "decay"), (decay_q[:, :], "decay_q"),
                                 (lam_c[:, :], "lam_c"), (same_head[:, :], "same_head"), (wg2[:, :], "wg2")):
                    sp.dma_start(to, net.dram[name]).then_inc(consts, 16)
                sp.dma_start(weight[:, :], net.dram["norm_weight"].partition_broadcast(P)).then_inc(consts, 16)

            @block.gpsimd
            def _(pool):
                nc.gpsimd.memset(state[:, :, :], 0.0).then_inc(state_done, 1)
                pool.wait_ge(w_high, 1)
                nc.gpsimd.tensor_tensor(w_l[:, :, :], w[:, :, :], w_h[:, :, :].bitcast(F32), ALU.subtract).then_inc(w_split, 1)
                pool.wait_ge(w_high, 2)
                nc.gpsimd.tensor_tensor(wo_l[:, :, :], wo[:, :, :], wo_h[:, :, :].bitcast(F32), ALU.subtract).then_inc(w_split, 1)
                pool.wait_ge(consts, 160)
                for n in range(TT):
                    a = act[:, n % 2, :].rearrange("p (h j e) -> p h j e", j=2, e=HD // 2)
                    b = by_sin[:, n % 2, :].rearrange("p (h j e) -> p h j e", j=2, e=HD // 2)
                    s = sin[:, n, :].rearrange("p (j e) -> p j e", j=2)
                    pool.wait_ge(act_done, n + 1)
                    if n >= 2:
                        pool.wait_ge(rotated, n - 1)
                    for j in range(2):
                        nc.gpsimd.tensor_tensor(b[:, :, j, :], a[:, :, 1 - j, :],
                                                s[:, j, :].unsqueeze(1).broadcast_to([P, 2 * H1, HD // 2]), ALU.mult)\
                            .then_inc(sin_done, 1)
                    pool.wait_ge(rotated, n + 1)
                    if n >= 4:
                        pool.wait_ge(out_full, n - 3)
                    nc.gpsimd.tensor_tensor(heads(kd[:, n % 4, :]), heads(rot[:, n % 2, D:]),
                                            decay_k[:, :].unsqueeze(2).broadcast_to([P, H1, HD]), ALU.mult).then_inc(kd_done, 1)
                for half in range(2):
                    part = slice(half * HALF, (half + 1) * HALF)
                    pool.wait_ge(gated, half + 1)
                    nc.gpsimd.tensor_tensor(sq[:, part, :], o[:, part, :], o[:, part, :], ALU.mult).then_inc(squares, 1)

            @block.tensor
            def _(pe):
                def projections(n):
                    toks = slice(n * P, (n + 1) * P)
                    if n:
                        pe.wait_ge(act_done, n)
                        pe.wait_ge(v_done, n)
                    for bank, cols in ((0, slice(0, QK)), (1, slice(QK, W))):
                        for c in range(DC):
                            last = product(nc, ps[:, bank, 0:cols.stop - cols.start], xn_h[:, c, toks], xn_l[:, c, toks],
                                           w_h[:, c, cols], w_l[:, c, cols], c == 0, c == DC - 1)
                    last.then_inc(projected, 1)

                def transposes(n):
                    pe.wait_ge(rotated, n + 1)
                    if n:
                        pe.wait_ge(t_split, n)
                    for b in range(2 * DC):
                        last = nc.tensor.transpose(ps[:, 2, b * P:(b + 1) * P], rot[:, n % 2, b * P:(b + 1) * P], net.ident[:, :])
                    last.then_inc(turned, 1)

                def scores(n):
                    pe.wait_ge(t_split, n + 1)
                    if n:
                        pe.wait_ge(sc_done, PAIRS * n)
                    for c in range(DC):
                        for r in range(PAIRS):
                            rows = slice(32 * r, 32 * (r + 1))
                            if c == 0 and r == PAIRS - 1 and n:
                                pe.wait_ge(o_done, n)
                            last = product(nc, ps[:, SCORE_BANKS[r], c * 2 * P:(c + 1) * 2 * P], k_h[rows, n % 2, c, :],
                                           k_l[rows, n % 2, c, :], qp_h[rows, n % 2, c, :, :].rearrange("p j t -> p (j t)"),
                                           qp_l[rows, n % 2, c, :, :].rearrange("p j t -> p (j t)"), True, True)
                            if c == DC - 1:
                                last.then_inc(sc_full, 1)

                def outputs(n):
                    pe.wait_ge(kd_done, n + 1)
                    pe.wait_ge(state_done, n + 1)
                    if n:
                        pe.wait_ge(inter_done, n)
                    for c in range(DC):
                        nc.tensor.matmul(ps[:, 3, c * P:(c + 1) * P], kd[:, n % 4, c * P:(c + 1) * P],
                                         v[:, n, c * P:(c + 1) * P], start=True, stop=True)
                    for c in range(DC):
                        nc.tensor.matmul(ps[:, 3, D + c * P:D + (c + 1) * P], q_t[:, n % 4, c, :], state[:, c, :],
                                         start=True, stop=True)
                    pe.wait_ge(sc_done, PAIRS * (n + 1))
                    for h in range(H1):
                        last = nc.tensor.matmul(ps[:, 4, h * HD:(h + 1) * HD], sc[:, n % 2, h, :],
                                                v[:, n, h * HD:(h + 1) * HD], start=True, stop=True)
                    last.then_inc(out_full, 1)

                norm.tensor(pe)
                norm.wait_parts(pe)
                pe.wait_ge(w_split, 1)
                for n in range(STEPS):
                    if n < TT:
                        projections(n)
                    if 0 <= n - 1 < TT:
                        transposes(n - 1)
                    if n == TT:
                        pe.wait_ge(act_done, TT)
                        pe.wait_ge(v_done, TT)
                        for i in range(TT):
                            last = nc.tensor.transpose(ps[0:HD, i // 4, (i % 4) * P:(i % 4 + 1) * P], g1[:, i, :], net.ident[:, :])
                        last.then_inc(g1_turned, 1)
                    if n - 3 >= 0:
                        outputs(n - 3)
                    if 0 <= n - 2 < TT:
                        scores(n - 2)
                    if n >= TT:
                        for b in range(2) if n < STEPS - 1 else ():
                            k = 2 * (n - TT) + b
                            pe.wait_ge(g1_copied, 2)
                            if k >= 2:
                                pe.wait_ge(gate_done, k - 1)
                            for i in (2 * k, 2 * k + 1):
                                last = nc.tensor.matmul(ps[:, k % 2, (i % 2) * D:(i % 2 + 1) * D], g1_t[:, i * P:(i + 1) * P],
                                                        wg2[:, :], start=True, stop=True)
                            last.then_inc(gate_full, 1)
                for half in range(2):
                    pe.wait_ge(weighted, half + 1)
                    for c in range(DC):
                        for k in range(HALF):
                            i = half * HALF + k
                            last = nc.tensor.transpose(ps[:, 4 + 2 * half + c, k * P:(k + 1) * P], o[:, i, c * P:(c + 1) * P],
                                                       net.ident[:, :])
                        last.then_inc(o_turned, 1)
                pe.wait_ge(w_split, 2)
                for b in range(NB):
                    cols = slice(b * BANK, (b + 1) * BANK)
                    pe.wait_ge(o_split, DC * (b + 1))
                    for m in range(DC):
                        for c in range(DC):
                            last = product(nc, ps[:, 2 * b + m, :], wo_h[:, c, m * P:(m + 1) * P], wo_l[:, c, m * P:(m + 1) * P],
                                           o_h[:, c, cols], o_l[:, c, cols], c == 0, c == DC - 1)
                        last.then_inc(y_full, 1)

            @block.scalar
            def _(act_e):
                act_e.wait_ge(w_loaded, 32)
                nc.scalar.activation(w_h[:, :, :], w[:, :, :], ACT.Copy).then_inc(w_high, 1)
                nc.scalar.activation(wo_h[:, :, :], wo[:, :, :], ACT.Copy).then_inc(w_high, 1)
                norm.scalar(act_e)
                act_e.wait_ge(consts, 160)
                for n in range(TT + 1):
                    if n < TT:
                        act_e.wait_ge(projected, n + 1)
                        if n >= 2:
                            act_e.wait_ge(rotated, n - 1)
                        nc.scalar.activation(act[:, n % 2, :], ps[:, 0, :], ACT.Silu).then_inc(act_done, 1)
                        nc.scalar.activation(g1[:, n, :], ps[:, 1, D:VG], ACT.Copy)
                        nc.scalar.activation(v[:, n, :], ps[:, 1, 0:D], ACT.Copy).then_inc(v_done, 1)
                    i = n - 1
                    if i >= 0:
                        act_e.wait_ge(turned, i + 1)
                        if i >= 2:
                            act_e.wait_ge(sc_full, PAIRS * (i - 1))
                        if i >= 4:
                            act_e.wait_ge(out_full, i - 3)
                        q_ps = ps[:, 2, 0:D].rearrange("p (c t) -> p c t", c=DC)
                        nc.scalar.activation(q_t[:, i % 4, :, :], q_ps, ACT.Copy)
                        for j in range(2):
                            nc.scalar.activation(qp_h[:, i % 2, :, j, :], q_ps, ACT.Copy, scale=in_pair[:, j:j + 1])
                        nc.scalar.activation(k_h[:, i % 2, :, :], ps[:, 2, D:].rearrange("p (c t) -> p c t", c=DC),
                                             ACT.Copy).then_inc(t_high, 1)
                act_e.wait_ge(g1_turned, 1)
                for b in range(2):
                    nc.scalar.activation(g1_t[:, b * BANK:(b + 1) * BANK], ps[0:HD, b, :], ACT.Copy).then_inc(g1_copied, 1)
                for k in range(TT // 2):
                    act_e.wait_ge(gate_full, k + 1)
                    nc.scalar.activation(gate[:, 2 * k:2 * k + 2, :], ps[:, k % 2, :].rearrange("p (i d) -> p i d", i=2),
                                         ACT.Sigmoid).then_inc(gate_done, 1)
                for half in range(2):
                    for c in range(DC):
                        act_e.wait_ge(o_turned, DC * half + c + 1)
                        nc.scalar.activation(o_h[:, c, half * BANK:(half + 1) * BANK], ps[:, 4 + 2 * half + c, :],
                                             ACT.Copy).then_inc(o_high, 1)
                for n in range(NB * DC):
                    if n % DC == 0:
                        act_e.wait_ge(y_full, n + 1)
                        nc.scalar.activation(net.delta[:, 0, (n // DC) * BANK:(n // DC + 1) * BANK], ps[:, n, :],
                                             ACT.Copy).then_inc(y_copied, 1)

            @block.vector
            def _(dve):
                norm.vector(dve)
                dve.wait_ge(consts, 160)
                for n in range(STEPS):
                    if n < TT:
                        dve.wait_ge(act_done, n + 1)
                        wide = lambda ap: ap.rearrange("p (h e) -> p h e", e=HD)
                        nc.vector.tensor_tensor(wide(by_cos[:, n % 2, :]), wide(act[:, n % 2, :]),
                                                cos[:, n, :].unsqueeze(1).broadcast_to([P, 2 * H1, HD]), ALU.mult).then_inc(cos_done, 1)
                        dve.wait_ge(cos_done, n + 1)
                        dve.wait_ge(sin_done, 2 * n + 2)
                        if n >= 2:
                            dve.wait_ge(turned, n - 1)
                            dve.wait_ge(kd_done, n - 1)
                        nc.vector.tensor_tensor(rot[:, n % 2, :], by_cos[:, n % 2, :], by_sin[:, n % 2, :], ALU.add).then_inc(rotated, 1)
                    i = n - 1
                    if 0 <= i < TT:
                        dve.wait_ge(t_high, i + 1)
                        q_ps = ps[:, 2, 0:D].rearrange("p (c t) -> p c t", c=DC)
                        for j in range(2):
                            nc.vector.scalar_tensor_tensor(qp_l[:, i % 2, :, j, :], q_ps, in_pair[:, j:j + 1],
                                                           qp_h[:, i % 2, :, j, :].bitcast(F32), ALU.mult, ALU.subtract)
                        nc.vector.tensor_tensor(k_l[:, i % 2, :, :], ps[:, 2, D:].rearrange("p (c t) -> p c t", c=DC),
                                                k_h[:, i % 2, :, :].bitcast(F32), ALU.subtract).then_inc(t_split, 1)
                    i = n - 3
                    if i >= 0:
                        dve.wait_ge(out_full, i + 1)
                        nc.vector.tensor_tensor(heads(inter[:, i % 2, :]), heads(ps[:, 3, D:]),
                                                decay_q[:, :].unsqueeze(2).broadcast_to([P, H1, HD]), ALU.mult).then_inc(chain, 1)
                        nc.vector.tensor_tensor(kv[:, :, :], ps[:, 3, 0:D].rearrange("p (c t) -> p c t", c=DC),
                                                same_head[:, :].unsqueeze(1).broadcast_to([P, DC, P]), ALU.mult).then_inc(inter_done, 1)
                        dve.wait_ge(chain, i + 1)
                        nc.vector.tensor_tensor(o[:, i, :], inter[:, i % 2, :], ps[:, 4, 0:D], ALU.add).then_inc(o_done, 1)
                        dve.wait_ge(inter_done, i + 1)
                        for c in range(DC):
                            last = nc.vector.scalar_tensor_tensor(state[:, c, :], state[:, c, :], lam_c[:, c:c + 1], kv[:, c, :],
                                                                  ALU.mult, ALU.add)
                        last.then_inc(state_done, 1)
                        dve.wait_ge(state_done, i + 2)
                    i = n - 2
                    if 0 <= i < TT:
                        for r in range(PAIRS):
                            dve.wait_ge(sc_full, PAIRS * i + r + 1)
                            nc.vector.tensor_tensor(of_pair(sc[:, i % 2, :, :], r), ps[:, SCORE_BANKS[r], :].rearrange("p (c x) -> p c x", c=DC),
                                                    of_pair(decay[:, :, :], r), ALU.mult).then_inc(sc_done, 1)
                for half in range(2):
                    part = slice(half * HALF, (half + 1) * HALF)
                    dve.wait_ge(gate_done, HALF // 2 * (half + 1))
                    dve.wait_ge(o_done, TT)
                    nc.vector.tensor_tensor(o[:, part, :], o[:, part, :], gate[:, part, :], ALU.mult).then_inc(gated, 1)
                links = TT
                for half in range(2):
                    part = slice(half * HALF, (half + 1) * HALF)
                    dve.wait_ge(squares, half + 1)
                    nc.vector.tensor_reduce(ms[:, part, :], sq[:, part, :].rearrange("p i (h e) -> p i h e", e=HD), AX.X, ALU.add)\
                        .then_inc(chain, 1)
                    dve.wait_ge(chain, links + 1)
                    nc.vector.tensor_scalar(ms[:, part, :], ms[:, part, :], 1.0 / HD, None, ALU.mult).then_inc(chain, 1)
                    dve.wait_ge(chain, links + 2)
                    flat = lambda ap: ap.rearrange("p i h -> p (i h)")
                    links = inverse_root(nc, dve, flat(rms[:, part, :]), flat(ms[:, part, :]), RMS_EPS,
                                         root[:, 0, half * HALF * H1:(half + 1) * HALF * H1],
                                         root[:, 1, half * HALF * H1:(half + 1) * HALF * H1], chain, links + 2)
                    dve.wait_ge(chain, links)
                    by_head = lambda ap: ap.rearrange("p i (h e) -> p (i h) e", e=HD)
                    nc.vector.tensor_tensor(by_head(o[:, part, :]), by_head(o[:, part, :]),
                                            flat(rms[:, part, :]).unsqueeze(2).broadcast_to([P, HALF * H1, HD]), ALU.mult).then_inc(chain, 1)
                    links += 1
                    dve.wait_ge(chain, links)
                    nc.vector.tensor_tensor(o[:, part, :], o[:, part, :], weight[:, :].unsqueeze(1).broadcast_to([P, HALF, D]),
                                            ALU.mult).then_inc(weighted, 1)
                for half in range(2):
                    for c in range(DC):
                        cols = slice(half * BANK, (half + 1) * BANK)
                        dve.wait_ge(o_high, DC * half + c + 1)
                        nc.vector.tensor_tensor(o_l[:, c, cols], ps[:, 4 + 2 * half + c, :], o_h[:, c, cols].bitcast(F32),
                                                ALU.subtract).then_inc(o_split, 1)
                for n in range(NB * DC):
                    if n % DC == 1:
                        dve.wait_ge(y_full, n + 1)
                        nc.vector.tensor_copy(net.delta[:, 1, (n // DC) * BANK:(n // DC + 1) * BANK], ps[:, n, :]).then_inc(y_copied, 1)
                dve.wait_ge(y_copied, NB * DC)


EXP1, F1, TOP1 = 32, 176, 6
SHARED1 = 2 * F1
CAPACITY = 2 * (T * TOP1 // EXP1)
TILES1 = EXP1 * F1 // P
GRAIN = 16
SH1 = -(-SHARED1 // P)
SHARED_TILES = [min(P, SHARED1 - k * P) for k in range(SH1)]


def silu_experts_phase(nc, net):
    BODY, RAW, RING, WRING = 4, 2, 2, 4
    AHEAD = 2
    GATE, UP, DOWN, W = 0, DC * P, 2 * DC * P, 2 * DC * P + D
    SG, SU, SD, SW = 0, DC * SHARED1, 2 * DC * SHARED1, 2 * DC * SHARED1 + (SH1 - 1) * D
    TAIL = SHARED_TILES[-1]
    SENT = 8 - TOP1
    assert TILES1 % BODY == 0
    with ExitStack() as mem:
        sb = lambda n, s, d=F32: mem.enter_context(nc.sbuf_tensor(f"f1_{n}", s, d))
        sem = lambda n: net.ctx.enter_context(nc.semaphore(f"f1_{n}"))
        ps, xn, xn_h, xn_l = net.ps, net.xn, net.xn_h, net.xn_l
        router, before = sb("router", [P, DC, EXP1]), sb("before", [P, P])
        before_b, ones_b = sb("before_b", [P, P], BF16), sb("ones_b", [P, P], BF16)
        sw, sw_h, sw_l = sb("sw", [P, SW]), sb("sw_h", [P, SW], F32R), sb("sw_l", [P, SW], F32R)
        st, st_h, st_l = sb("st", [TAIL, D]), sb("st_h", [TAIL, D], F32R), sb("st_l", [TAIL, D], F32R)
        e_raw = sb("e_raw", [P, RAW, W])
        e_h, e_l = sb("e_h", [P, WRING, W], F32R), sb("e_l", [P, WRING, W], F32R)
        one = sb("one", [P, 1])
        silu, act = sb("silu", [P, RING, T]), sb("act", [P, RING, T])
        a_h, a_l = sb("a_h", [P, RING, T], F32R), sb("a_l", [P, RING, T], F32R)
        s_h, s_l = sb("s_h", [P, SH1, T], F32R), sb("s_l", [P, SH1, T], F32R)
        cw_row = sb("cw_row", [P, RING, T])
        logit = sb("logit", [P, TT, EXP1 + SENT])
        score, found = sb("score", [P, TT, EXP1]), sb("found", [P, TT, EXP1 + SENT])
        best, take = sb("best", [P, TT, 8]), sb("take", [P, TT, 8])
        total, cw = sb("total", [P, TT]), sb("cw", [P, TT, EXP1])
        chosen = sb("chosen", [P, TT, EXP1], BF16)
        cw_t = sb("cw_t", [EXP1, T])
        grains = net.cw_grains

        consts, s_loaded = sem("consts"), sem("s_loaded")
        s_high, s_split = sem("s_high"), sem("s_split")
        logits, scored, exped, marked, ranked = sem("logits"), sem("scored"), sem("exped"), sem("marked"), sem("ranked")
        routed, cw_turned, cw_copied, cw_stored = sem("routed"), sem("cw_turned"), sem("cw_copied"), sem("cw_stored")
        e_loaded = [sem(f"e_loaded{r}") for r in range(RAW)]
        row_loaded = [sem(f"row_loaded{r}") for r in range(RING)]
        e_high, e_split = sem("e_high"), sem("e_split")
        gate_full, up_full, silued, timed, weighed = sem("gate_full"), sem("up_full"), sem("silued"), sem("timed"), sem("weighed")
        act_high, act_split, down_done = sem("act_high"), sem("act_split"), sem("down_done")
        y_copied, chain = sem("y_copied"), sem("chain")

        norm = Norm(nc, net, "n3", mem, True, True, cw_row[:, :, :].rearrange("p r (k d) -> p (r k) d", d=D))

        def blocks(ap):
            return ap.rearrange("p (n t) -> p n t", n=NB)

        def steps(eng, loop_end, last, step):
            for n in range(BODY):
                step(0, n)
            with eng.Fori(1, loop_end) as it:
                for r in range(BODY):
                    step(it, r)
            for n in range(loop_end * BODY, last):
                step(*divmod(n, BODY))

        def known(it, r, low, high=TILES1 + BODY):
            return not isinstance(it, int) or low <= it * BODY + r < high

        with nc.Block() as block:

            @block.sync
            def _(sp):
                sp.dma_start(sw[:, SG:SU], net.dram["wsg"]).then_inc(s_loaded, 16)
                sp.dma_start(sw[:, SU:SD], net.dram["wsu"]).then_inc(s_loaded, 16)
                sp.dma_start(sw[:, SD:SW].rearrange("p (k d) -> p k d", d=D),
                             net.dram["wsd"][0:(SH1 - 1) * P, :].rearrange("(k p) d -> p k d", p=P)).then_inc(s_loaded, 16)
                sp.dma_start(st[:, :], net.dram["wsd"][(SH1 - 1) * P:SHARED1, :]).then_inc(s_loaded, 16)
                sp.dma_start(router[:, :, :], net.dram["router"]).then_inc(consts, 16)
                sp.dma_start(before[:, :], net.dram["before"]).then_inc(consts, 16)

                def load_weights(it, r):
                    n = it * BODY + r
                    if known(it, r, RAW):
                        sp.wait_ge(e_split, n - RAW + 1)
                    sp.dma_start(e_raw[:, r % RAW, :], net.dram["we1"][n]).then_inc(e_loaded[r % RAW], 16)

                def load_row(it, r):
                    n = it * BODY + r
                    if known(it, r, RING):
                        sp.wait_ge(weighed, n - RING + 1)
                    sp.dma_start(cw_row[:, r % RING, :],
                                 grains[n].unsqueeze(1).broadcast_to([P // GRAIN, GRAIN, T])).then_inc(row_loaded[r % RING], 16)

                for r in range(RAW):
                    load_weights(0, r)
                sp.wait_ge(cw_copied, 1)
                sp.dma_start(grains.rearrange("a b t -> (a b) t").rearrange("(e g) t -> e g t", e=EXP1),
                             cw_t[:, :].unsqueeze(1).broadcast_to([EXP1, F1 // GRAIN, T])).then_inc(cw_stored, 16)
                sp.wait_ge(cw_stored, 16)

                def step(it, r):
                    load_row(it, r)
                    if known(it, r, 0, TILES1 - RAW):
                        load_weights(it, r + RAW)

                steps(sp, TILES1 // BODY - 1, TILES1, step)

            @block.tensor
            def _(pe):
                norm.tensor(pe)
                pe.wait_ge(consts, 35)
                norm.wait_parts(pe)
                norm.wait_full(pe)
                for i in range(TT):
                    for c in range(DC):
                        last = nc.tensor.matmul(ps[:, 7, i * EXP1:(i + 1) * EXP1], xn[:, c, i * P:(i + 1) * P],
                                                router[:, c, :], start=c == 0, stop=c == DC - 1)
                last.then_inc(logits, 1)

                def project(bank, rows, weight, full):
                    for b in range(NB):
                        cols = slice(b * BANK, (b + 1) * BANK)
                        for c in range(DC):
                            last = product(nc, ps[0:rows, bank + b, :], *weight(c), xn_h[:, c, cols], xn_l[:, c, cols],
                                           c == 0, c == DC - 1)
                    last.then_inc(full, 1)

                def down(weight, rows, h, l, first, final):
                    for m in range(DC):
                        for b in range(NB):
                            cols = slice(b * BANK, (b + 1) * BANK)
                            wt = weight(m)
                            last = product(nc, ps[:, 4 + 2 * m + b, :], *wt, h[0:rows, cols], l[0:rows, cols], first, final)
                    last.then_inc(down_done, 1)

                pe.wait_ge(s_split, 2)
                for k, rows in enumerate(SHARED_TILES):
                    def piece(base):
                        def weight(c):
                            part = slice(base + c * SHARED1 + k * P, base + c * SHARED1 + k * P + rows)
                            return sw_h[:, part], sw_l[:, part]
                        return weight
                    if k:
                        pe.wait_ge(silued, k)
                    project(0, rows, piece(SG), gate_full)
                    if k:
                        pe.wait_ge(timed, k)
                    project(2, rows, piece(SU), up_full)
                pe.wait_ge(marked, 1)
                for i in range(TT):
                    for k in range(i + 1):
                        last = nc.tensor.matmul(ps[:, 6, i * EXP1:(i + 1) * EXP1], before_b[:, :] if k == i else ones_b[:, :],
                                                chosen[:, k, :], start=k == 0, stop=k == i)
                last.then_inc(ranked, 1)
                pe.wait_ge(routed, 1)
                for i in range(TT):
                    last = nc.tensor.transpose(ps[0:EXP1, 4 + i // 4, (i % 4) * P:(i % 4 + 1) * P], cw[:, i, :], net.ident[:, :])
                last.then_inc(cw_turned, 1)
                pe.wait_ge(cw_copied, 1)
                for k, rows in enumerate(SHARED_TILES):
                    pe.wait_ge(act_split, k + 1)
                    if k < SH1 - 1:
                        weight = lambda m: (sw_h[:, SD + k * D + m * P:SD + k * D + (m + 1) * P],
                                            sw_l[:, SD + k * D + m * P:SD + k * D + (m + 1) * P])
                    else:
                        weight = lambda m: (st_h[:, m * P:(m + 1) * P], st_l[:, m * P:(m + 1) * P])
                    down(weight, rows, s_h[:, k, :], s_l[:, k, :], k == 0, False)

                def step(it, r):
                    n = it * BODY + r

                    def piece(slot, base):
                        return lambda c: (e_h[:, slot, base + c * P:base + (c + 1) * P],
                                          e_l[:, slot, base + c * P:base + (c + 1) * P])

                    if known(it, r, 0, TILES1):
                        pe.wait_ge(e_split, n + 1)
                        pe.wait_ge(silued, n + SH1)
                        project(0, P, piece(r % WRING, GATE), gate_full)
                        pe.wait_ge(timed, n + SH1)
                        project(2, P, piece(r % WRING, UP), up_full)
                    if known(it, r, 1):
                        m = (r - 1) % BODY
                        pe.wait_ge(act_split, n + SH1)
                        final = isinstance(it, int) and n == TILES1
                        down(piece(m % WRING, DOWN), P, a_h[:, m % RING, :], a_l[:, m % RING, :], False, final)

                steps(pe, TILES1 // BODY, TILES1 + 1, step)

            @block.scalar
            def _(act_e):
                act_e.wait_ge(s_loaded, 64)
                nc.scalar.activation(sw_h[:, :], sw[:, :], ACT.Copy).then_inc(s_high, 1)
                nc.scalar.activation(st_h[:, :], st[:, :], ACT.Copy).then_inc(s_high, 1)
                norm.scalar(act_e)
                act_e.wait_ge(scored, 1)
                nc.scalar.activation(score[:, :, :], score[:, :, :], ACT.Exp).then_inc(exped, 1)

                def silu_gate(n, k, rows):
                    act_e.wait_ge(gate_full, n + 1)
                    if not isinstance(n, int) or n >= RING:
                        act_e.wait_ge(timed, n - RING + 1)
                    nc.scalar.activation(blocks(silu[0:rows, k % RING, :]), ps[0:rows, 0:2, :], ACT.Silu).then_inc(silued, 1)

                for k, rows in enumerate(SHARED_TILES):
                    silu_gate(k, k, rows)
                    act_e.wait_ge(timed, k + 1)
                    nc.scalar.activation(s_h[0:rows, k, :], act[0:rows, k % RING, :], ACT.Copy).then_inc(act_high, 1)

                def high_weights(it, r):
                    act_e.wait_ge(e_loaded[r % RAW], 16 * (it * (BODY // RAW) + r // RAW) + 16)
                    if known(it, r, WRING):
                        act_e.wait_ge(down_done, it * BODY + (r - WRING + 1 + SH1))
                    nc.scalar.activation(e_h[:, r % WRING, :], e_raw[:, r % RAW, :], ACT.Copy).then_inc(e_high, 1)

                for r in range(AHEAD):
                    high_weights(0, r)

                def step(it, r):
                    n = it * BODY + r
                    if known(it, r, 1):
                        m = (r - 1) % RING
                        act_e.wait_ge(weighed, n)
                        if known(it, r, 1 + RING):
                            act_e.wait_ge(down_done, n - RING + SH1)
                        nc.scalar.activation(a_h[:, m, :], act[:, m, :], ACT.Copy).then_inc(act_high, 1)
                    if known(it, r, 0, TILES1):
                        silu_gate(n + SH1, r, P)
                    if known(it, r, 0, TILES1 - AHEAD):
                        high_weights(it, r + AHEAD)

                steps(act_e, TILES1 // BODY - 1, TILES1 + 1, step)
                act_e.wait_ge(down_done, SH1 + TILES1)
                nc.scalar.activation(blocks(net.delta[:, 0, :]), ps[:, 4:6, :], ACT.Copy).then_inc(y_copied, 1)

            @block.gpsimd
            def _(pool):
                nc.gpsimd.memset(logit[:, :, EXP1:], BIG).then_inc(consts, 1)
                nc.gpsimd.memset(take[:, :, TOP1:], BIG).then_inc(consts, 1)
                nc.gpsimd.memset(ones_b[:, :], 1.0).then_inc(consts, 1)
                pool.wait_ge(s_high, 2)
                nc.gpsimd.tensor_tensor(sw_l[:, :], sw[:, :], sw_h[:, :].bitcast(F32), ALU.subtract).then_inc(s_split, 1)
                nc.gpsimd.tensor_tensor(st_l[:, :], st[:, :], st_h[:, :].bitcast(F32), ALU.subtract).then_inc(s_split, 1)

                def low_weights(it, r):
                    pool.wait_ge(e_high, it * BODY + r + 1)
                    nc.gpsimd.tensor_tensor(e_l[:, r % WRING, :], e_raw[:, r % RAW, :], e_h[:, r % WRING, :].bitcast(F32),
                                            ALU.subtract).then_inc(e_split, 1)

                for r in range(AHEAD):
                    low_weights(0, r)

                def step(it, r):
                    n = it * BODY + r
                    if known(it, r, 0, TILES1 - AHEAD):
                        low_weights(it, r + AHEAD)
                    if known(it, r, 0, TILES1):
                        pool.wait_ge(row_loaded[r % RING], 16 * (it * (BODY // RING) + r // RING) + 16)
                        pool.wait_ge(timed, n + SH1 + 1)
                        nc.gpsimd.tensor_tensor(act[:, r % RING, :], act[:, r % RING, :], cw_row[:, r % RING, :],
                                                ALU.mult).then_inc(weighed, 1)

                steps(pool, TILES1 // BODY - 1, TILES1, step)

            @block.vector
            def _(dve):
                links = [0]

                def link(ins):
                    ins.then_inc(chain, 1)
                    links[0] += 1
                    dve.wait_ge(chain, links[0])

                def times(n, k, rows):
                    dve.wait_ge(up_full, n + 1)
                    dve.wait_ge(silued, n + 1)
                    if not isinstance(n, int) or n >= RING:
                        dve.wait_ge(act_split, n - RING + 1)
                    nc.vector.tensor_tensor(blocks(act[0:rows, k % RING, :]), ps[0:rows, 2:4, :], blocks(silu[0:rows, k % RING, :]),
                                            ALU.mult).then_inc(timed, 1)

                def split_shared(k, rows):
                    dve.wait_ge(act_high, k + 1)
                    nc.vector.tensor_tensor(s_l[0:rows, k, :], act[0:rows, k % RING, :], s_h[0:rows, k, :].bitcast(F32),
                                            ALU.subtract).then_inc(act_split, 1)

                norm.vector(dve)
                dve.wait_ge(consts, 35)
                dve.wait_ge(logits, 1)
                nc.vector.tensor_copy(before_b[:, :], before[:, :])
                link(nc.vector.tensor_copy(logit[:, :, 0:EXP1], ps[:, 7, 0:TT * EXP1].rearrange("p (i e) -> p i e", e=EXP1)))
                for i in range(TT):
                    last = nc.vector.max(best[:, i, :], logit[:, i, 0:EXP1])
                link(last)
                nc.vector.tensor_tensor(score[:, :, :], logit[:, :, 0:EXP1], best[:, :, 0:1].broadcast_to([P, TT, EXP1]),
                                        ALU.subtract).then_inc(scored, 1)
                link(nc.vector.tensor_copy(take[:, :, 0:TOP1], best[:, :, 0:TOP1]))
                for i in range(TT):
                    last = nc.vector.match_replace(found[:, i, :], take[:, i, :], logit[:, i, :], TAKEN)
                link(last)
                nc.vector.tensor_scalar(chosen[:, :, :], found[:, :, 0:EXP1], TAKEN, None, ALU.is_equal).then_inc(marked, 1)
                dve.wait_ge(exped, 1)
                link(nc.vector.tensor_reduce(total[:, :], score[:, :, :], AX.X, ALU.add))
                link(nc.vector.reciprocal(total[:, :], total[:, :]))
                link(nc.vector.tensor_tensor(score[:, :, :], score[:, :, :], total[:, :].unsqueeze(2).broadcast_to([P, TT, EXP1]),
                                             ALU.mult))
                times(0, 0, SHARED_TILES[0])
                link(nc.vector.scalar_tensor_tensor(cw[:, :, :], found[:, :, 0:EXP1], TAKEN, score[:, :, :], ALU.is_equal, ALU.mult))
                link(nc.vector.tensor_reduce(total[:, :], cw[:, :, :], AX.X, ALU.add))
                link(nc.vector.tensor_scalar(total[:, :], total[:, :], 1e-20, None, ALU.add))
                link(nc.vector.reciprocal(total[:, :], total[:, :]))
                split_shared(0, SHARED_TILES[0])
                link(nc.vector.tensor_tensor(cw[:, :, :], cw[:, :, :], total[:, :].unsqueeze(2).broadcast_to([P, TT, EXP1]),
                                             ALU.mult))
                for k in range(1, SH1):
                    times(k, k, SHARED_TILES[k])
                    split_shared(k, SHARED_TILES[k])
                dve.wait_ge(ranked, 1)
                nc.vector.scalar_tensor_tensor(cw[:, :, :], ps[:, 6, 0:TT * EXP1].rearrange("p (i e) -> p i e", e=EXP1),
                                               float(CAPACITY), cw[:, :, :], ALU.is_lt, ALU.mult).then_inc(routed, 1)
                dve.wait_ge(cw_turned, 1)
                nc.vector.tensor_copy(blocks(cw_t[:, :]), ps[0:EXP1, 4:6, :]).then_inc(cw_copied, 1)

                def step(it, r):
                    n = it * BODY + r
                    if known(it, r, 1):
                        m = (r - 1) % RING
                        dve.wait_ge(act_high, n + SH1)
                        nc.vector.tensor_tensor(a_l[:, m, :], act[:, m, :], a_h[:, m, :].bitcast(F32),
                                                ALU.subtract).then_inc(act_split, 1)
                    if known(it, r, 0, TILES1):
                        times(n + SH1, r, P)

                steps(dve, TILES1 // BODY, TILES1 + 1, step)
                dve.wait_ge(down_done, SH1 + TILES1)
                nc.vector.tensor_copy(blocks(net.delta[:, 1, :]), ps[:, 6:8, :]).then_inc(y_copied, 1)
                dve.wait_ge(y_copied, 2)


def program(nc, dram, out, upto=99):
    net = Net()
    net.dram = dram
    with ExitStack() as ctx:
        net.ctx = ctx
        sb = lambda n, s, d=F32: ctx.enter_context(nc.sbuf_tensor(n, s, d))
        net.ps = ctx.enter_context(nc.psum_tensor("ps", [P, 8, BANK], F32))
        net.x = sb("x", [P, TT, D])
        net.delta = sb("delta", [P, DC, T])
        net.xn_h, net.xn_l = sb("xn_h", [P, DC, T], F32R), sb("xn_l", [P, DC, T], F32R)
        net.ident = sb("ident", [P, P])
        net.cw_dram = [nc.dram_tensor(f"cw{n}", (EXP0, T), F32, kind="Internal").ap() for n in range(1)]
        net.cw_grains = nc.dram_tensor("cw_grains", (TILES1, P // GRAIN, T), F32, kind="Internal").ap()
        net.norm_sems = {n: ctx.enter_context(nc.semaphore(f"norm_{n}")) for n in NORM_SEMS}
        net.norm_counts = {n: 0 for n in NORM_SEMS}
        softmax_attention_phase(nc, net)
        net.xn = sb("xn", [P, DC, T])
        squared_relu_experts_phase(nc, net)
        linear_attention_phase(nc, net)
        silu_experts_phase(nc, net)
        output_phase(nc, net, out)


def kernel(**inputs):
    import numpy as _np
    import concourse.bacc as _bacc
    from concourse import mybir as _mybir
    from concourse.bass_utils import run_bass_kernel_spmd as _run

    def get(name):
        return _np.asarray(inputs[name])

    def grouped(w, groups):
        return w.reshape(DC, P, groups, -1).transpose(2, 1, 0, 3)

    def tiled(w):
        return w.reshape(-1, P, w.shape[1]).transpose(1, 0, 2)

    def flat(w):
        return tiled(w).reshape(P, -1)

    def by_feature(w):
        w = w.transpose(1, 0, 2).reshape(DC, P, TILES1, P)
        return w.transpose(2, 1, 0, 3).reshape(TILES1, P, DC * P)

    host = {
        "x": get("L0_attn_inputs_q").reshape(T, D),
        "ident": _np.eye(P, dtype=_np.float32),
        "bq": get("L0_attn_bq").reshape(HEADS, DH).T, "bk": get("L0_attn_bk").reshape(KV, DH).T, "bv": get("L0_attn_bv"), "bo": get("L0_attn_bo"),
        "wq": grouped(get("L0_attn_wq"), KV), "wk": grouped(get("L0_attn_wk"), KV), "wv": grouped(get("L0_attn_wv"), KV),
        "wo": get("L0_attn_wo").reshape(KV, PER, DH, D).transpose(0, 2, 1, 3),
        "gate0": tiled(get("L0_ffn_gate_w").T), "gate_bias": get("L0_ffn_gate_bias"),
        "fc1": flat(get("L0_ffn_fc1_w").T), "fc2": flat(get("L0_ffn_fc2_w").T),
        "sup0": flat(get("L0_ffn_shared_up_w").T), "sdn0": flat(get("L0_ffn_shared_down_w").T),
        "we0": _np.stack([get("L0_ffn_w1").transpose(0, 2, 1), get("L0_ffn_w2").transpose(0, 2, 1)], 2),
        "w1a": tiled(_np.concatenate([get("L1_attn_Wq"), get("L1_attn_Wk"), get("L1_attn_Wv"), get("L1_attn_Wg1")], 1)),
        "wg2": get("L1_attn_Wg2"), "wo1": tiled(get("L1_attn_Wo")), "norm_weight": get("L1_attn_norm_weight"),
        **{k: a.astype(_np.float32) for k, a in decay_tables().items()},
        "router": tiled(get("L1_ffn_wg_router").T), "before": _np.triu(_np.ones((P, P), _np.float32), 1),
        "wsg": flat(get("L1_ffn_ws_gate")), "wsu": flat(get("L1_ffn_ws_up")), "wsd": get("L1_ffn_ws_down"),
        "we1": _np.concatenate([by_feature(get("L1_ffn_w_gate")), by_feature(get("L1_ffn_w_up")),
                                get("L1_ffn_w_down").reshape(TILES1, P, D)], 2),
    }
    nc = _bacc.Bacc("TRN2", target_bir_lowering=False, num_devices=1)
    arrays, dram = {}, {}
    for name, a in host.items():
        a = _np.ascontiguousarray(a)
        arrays[f"in_{name}"] = a
        dram[name] = nc.dram_tensor(f"in_{name}", a.shape, _mybir.dt.from_np(a.dtype), kind="ExternalInput").ap()
    out = nc.dram_tensor("out_x", (T, D), F32, kind="ExternalOutput").ap()
    program(nc, dram, out)
    r = _run(nc, [arrays], core_ids=[0])
    return r.results[0]["out_x"].reshape(1, T, D)
```

```python
import numpy as np

import concourse.bass as bass
from concourse import mybir
from contextlib import ExitStack

F32 = mybir.dt.float32
F32R = mybir.dt.float32r
I32 = mybir.dt.int32
BF16 = mybir.dt.bfloat16
ALU = mybir.AluOpType
ACT = mybir.ActivationFunctionType
AX = mybir.AxisListType

P = 128
BANK = 512
T, D = 1024, 256
TT, DC = T // P, D // P
NB = T // BANK
LN_EPS = 1e-5


class Net:
    pass


def product(nc, out, lhs_h, lhs_l, rhs_h, rhs_l, start, stop):
    nc.tensor.matmul(out, lhs_h, rhs_h, start=start, stop=False)
    nc.tensor.matmul(out, lhs_h, rhs_l, start=False, stop=False)
    return nc.tensor.matmul(out, lhs_l, rhs_h, start=False, stop=stop)


def inverse_root(nc, dve, out, var, eps, a, s, done, n):
    nc.vector.tensor_scalar(a, var, eps, None, ALU.add).then_inc(done, 1)
    dve.wait_ge(done, n + 1)
    nc.vector.tensor_scalar(s.bitcast(I32), a.bitcast(I32), 1, None, ALU.logical_shift_right).then_inc(done, 1)
    dve.wait_ge(done, n + 2)
    nc.vector.tensor_scalar(out.bitcast(I32), s.bitcast(I32), -1.0, float(0x5F3759DF), ALU.mult, ALU.add).then_inc(done, 1)
    n += 3
    for _ in range(3):
        dve.wait_ge(done, n)
        nc.vector.scalar_tensor_tensor(s, out, -0.5, out, ALU.mult, ALU.mult).then_inc(done, 1)
        dve.wait_ge(done, n + 1)
        nc.vector.tensor_tensor(s, s, a, ALU.mult).then_inc(done, 1)
        dve.wait_ge(done, n + 2)
        nc.vector.scalar_tensor_tensor(out, s, 1.5, out, ALU.add, ALU.mult).then_inc(done, 1)
        n += 3
    return n


class Norm:

    def __init__(self, nc, net, tag, mem, load=False, full=None, xc=None):
        sb = lambda n, s, d=F32: mem.enter_context(nc.sbuf_tensor(f"{tag}_{n}", s, d))
        self.nc, self.net, self.load, self.full = nc, net, load, full
        self.xc = sb("xc", [P, TT, D]) if xc is None else xc
        self.rstd, self.root = sb("rstd", [P, TT]), sb("root", [P, 2, TT])
        self.base = dict(net.norm_counts)
        totals = {"loaded": 16 * load, "loaded_late": 32 * load, "rstd_done": 12,
                  "xc_done": TT, "xc_turned": NB, "high_done": NB * DC, "parts_done": NB * DC,
                  "full_done": NB * DC * (full is not None)}
        for name, count in totals.items():
            net.norm_counts[name] += int(count)

    def wait(self, eng, name, n):
        eng.wait_ge(self.net.norm_sems[name], self.base[name] + n)

    def wait_parts(self, eng):
        self.wait(eng, "parts_done", NB * DC)

    def wait_full(self, eng):
        self.wait(eng, "full_done", NB * DC)

    def sync(self, sp):
        sems, net = self.net.norm_sems, self.net
        for name, part in (("loaded", slice(0, TT // 2)), ("loaded_late", slice(TT // 2, TT))):
            sp.dma_start(net.x[:, part, :], net.dram["x"].rearrange("(i p) d -> p i d", p=P)[:, part, :])\
                .then_inc(sems[name], 16)
        sp.dma_start(net.ident[:, :], net.dram["ident"]).then_inc(sems["loaded_late"], 16)

    def tensor(self, pe):
        nc, net, sems = self.nc, self.net, self.net.norm_sems
        if self.load:
            self.wait(pe, "loaded_late", 32)
        for n in range(NB):
            for k in range(4):
                self.wait(pe, "xc_done", 4 * n + k + 1)
                for c in range(DC):
                    last = nc.tensor.transpose(net.ps[:, 4 + 2 * n + c, k * P:(k + 1) * P],
                                               self.xc[:, 4 * n + k, c * P:(c + 1) * P], net.ident[:, :])
            last.then_inc(sems["xc_turned"], 1)

    def vector(self, dve):
        nc, net, sems, x = self.nc, self.net, self.net.norm_sems, self.net.x
        if self.load:
            self.wait(dve, "loaded", 16)
            take_moments(nc, net, dve, range(0, TT // 2))
            self.wait(dve, "loaded_late", 32)
            take_moments(nc, net, dve, range(TT // 2, TT))
        dve.wait_ge(sems["moments_done"], net.norm_counts["moments_done"])
        n = inverse_root(nc, dve, self.rstd[:, :], net.moments[:, :, 1], LN_EPS, self.root[:, 0, :], self.root[:, 1, :],
                         sems["rstd_done"], self.base["rstd_done"])
        dve.wait_ge(sems["rstd_done"], n)
        for i in range(TT):
            nc.vector.tensor_scalar(self.xc[:, i, :], x[:, i, :], net.moments[:, i, 0:1], self.rstd[:, i:i + 1],
                                    ALU.subtract, ALU.mult).then_inc(sems["xc_done"], 1)
        for n in range(NB):
            for c in range(DC):
                cols = slice(n * BANK, (n + 1) * BANK)
                self.wait(dve, "high_done", DC * n + c + 1)
                nc.vector.tensor_tensor(net.xn_l[:, c, cols], net.ps[:, 4 + 2 * n + c, :], net.xn_h[:, c, cols].bitcast(F32),
                                        ALU.subtract).then_inc(sems["parts_done"], 1)

    def scalar(self, act):
        nc, net, sems = self.nc, self.net, self.net.norm_sems
        for n in range(NB):
            self.wait(act, "xc_turned", n + 1)
            for c in range(DC):
                nc.scalar.activation(net.xn_h[:, c, n * BANK:(n + 1) * BANK], net.ps[:, 4 + 2 * n + c, :],
                                     ACT.Copy).then_inc(sems["high_done"], 1)
        if self.full is not None:
            self.wait(act, "parts_done", NB * DC)
            for n in range(NB):
                for c in range(DC):
                    nc.scalar.activation(self.full[:, c, n * BANK:(n + 1) * BANK], net.ps[:, 4 + 2 * n + c, :],
                                         ACT.Copy).then_inc(sems["full_done"], 1)


NORM_SEMS = ("loaded", "loaded_late", "stats_done", "moments_done", "rstd_done", "xc_done", "xc_turned", "high_done",
             "parts_done", "full_done")


def take_moments(nc, net, dve, tiles):
    sems, counts = net.norm_sems, net.norm_counts
    for i in tiles:
        nc.vector.bn_stats(net.stats[:, i, :], net.x[:, i, :]).then_inc(sems["stats_done"], 1)
    for i in tiles:
        counts["stats_done"] += 1
        dve.wait_ge(sems["stats_done"], counts["stats_done"])
        nc.vector.bn_aggr(net.moments[:, i, :], net.stats[:, i, :]).then_inc(sems["moments_done"], 1)
        counts["moments_done"] += 1


def add_pairs(nc, net, dve, banks, full, added, pairs, done):
    for n, j in enumerate(pairs):
        dve.wait_ge(full, j + 1)
        add_to_x(nc, net, 2 * j, banks[:, j:j + 1, :]).then_inc(added, 1)
        if n:
            dve.wait_ge(added, done + n)
            take_moments(nc, net, dve, range(2 * j - 2, 2 * j))
    dve.wait_ge(added, done + len(pairs))
    take_moments(nc, net, dve, range(2 * pairs[-1], 2 * pairs[-1] + 2))


def tokens_of(ap, i):
    return ap[:, i // 2, (i % 2) * D:(i % 2 + 1) * D]


def add_to_x(nc, net, i, banks):
    count = banks.shape[1]
    part = net.x[:, i:i + 2 * count, :].rearrange("p (n k) d -> p n (k d)", n=count)
    return nc.vector.tensor_tensor(part, part, banks, ALU.add)


HEADS, KV, DH = 16, 4, 128
PER = HEADS // KV
Q_SCALE = float(1.0 / np.sqrt(DH))


def softmax_attention_phase(nc, net):
    UNITS = PER * NB
    KT = TT
    STEPS = UNITS * KT
    TILES = UNITS * 4
    RING = 8
    LEAD = 12
    GW = PER * DH
    PROJ = PER + 1

    opening = [("k",), ("q", 0), ("v",), ("s", 0), ("s", 1), ("vs",)] + [("s", s) for s in range(2, LEAD)] + [("t", 0)]
    steady = []
    for s in range(LEAD, STEPS):
        if s % 2 == 0 and (s // 2 + 2) % TT == 0:
            steady.append(("q", (s // 2 + 2) // TT))
        steady += [("t", s - LEAD + 1), ("s", s), ("p", s - LEAD)]
    at = STEPS - LEAD
    change = [("k",)]
    ahead = [[], [], [], [0], [1], [2], [3], [4, 5], [6], [7], [8, 9]]
    for n in range(LEAD - 1):
        change += [("v",)] if n == 2 else []
        change += [("t", at + n + 1)] + [("s", s) for s in ahead[n]] + [("p", at + n)]
    change += [("p", STEPS - 1), ("vs",), ("s", 10), ("s", 11), ("y", 0), ("t", 0), ("y", 1)]
    closing = []
    for n in range(LEAD - 1):
        closing += [("t", at + n + 1), ("p", at + n)]
    closing += [("p", STEPS - 1), ("y", 0), ("y", 1)]

    def jobs_of(events):
        return [e for e in events if e[0] in "kvqy" or (e[0] == "s" and e[1] % 2 == 0)]

    first, lap = len(jobs_of(opening)), len(jobs_of(steady + change))
    assert lap % 2 == 0

    with ExitStack() as mem:
        sb = lambda n, s, d=F32: mem.enter_context(nc.sbuf_tensor(f"at_{n}", s, d))
        sem = lambda n: net.ctx.enter_context(nc.semaphore(f"at_{n}"))
        norm = Norm(nc, net, "n0", mem, load=True)
        ps, xn_h, xn_l = net.ps, net.xn_h, net.xn_l
        wq_raw, wkv_raw, wo_raw = sb("wq_raw", [P, DC, GW]), sb("wkv_raw", [P, 2, DC, DH]), sb("wo_raw", [P, PER, D])
        wq_h, wq_l = sb("wq_h", [P, DC, GW], F32R), sb("wq_l", [P, DC, GW], F32R)
        wkv_h, wkv_l = sb("wkv_h", [P, 2, DC, DH], F32R), sb("wkv_l", [P, 2, DC, DH], F32R)
        wo_h, wo_l = sb("wo_h", [P, PER, D], F32R), sb("wo_l", [P, PER, D], F32R)
        one = sb("one", [P, 1])
        bq, bk = sb("bq", [P, HEADS]), sb("bk", [P, KV])
        bv, bo = sb("bv", [P, KV * DH]), sb("bo", [P, D])
        proj = sb("proj", [P, T])
        v_full = sb("v_full", [P, T])
        q_h, q_l = sb("q_h", [P, 2, T], F32R), sb("q_l", [P, 2, T], F32R)
        k_h, k_l = sb("k_h", [P, T], F32R), sb("k_l", [P, T], F32R)
        v_h, v_l = sb("v_h", [P, T], F32R), sb("v_l", [P, T], F32R)
        prob = sb("prob", [P, RING, T])
        pt_h, pt_l = sb("pt_h", [P, 2, BANK], F32R), sb("pt_l", [P, 2, BANK], F32R)
        o_h, o_l = sb("o_h", [P, PER, T], F32R), sb("o_l", [P, PER, T], F32R)
        neg_max, row_sum, inv_sum = sb("neg_max", [P, TILES]), sb("row_sum", [P, TILES]), sb("inv_sum", [P, TILES])

        consts, ready = sem("consts"), sem("ready")
        wq_loaded, wkv_loaded, wo_loaded = sem("wq_loaded"), sem("wkv_loaded"), sem("wo_loaded")
        w_high, wq_split, wkv_split, wo_split = sem("w_high"), sem("wq_split"), sem("wkv_split"), sem("wo_split")
        bq_scaled = sem("bq_scaled")
        bo_added = sem("bo_added")
        proj_full, proj_read = sem("proj_full"), sem("proj_read")
        proj_high, proj_split = sem("proj_high"), sem("proj_split")
        values_full, v_added, v_high, v_split = sem("values_full"), sem("v_added"), sem("v_high"), sem("v_split")
        s_full, maxed, exped, inverted, normed = sem("s_full"), sem("maxed"), sem("exped"), sem("inverted"), sem("normed")
        pt_full, pt_high, pt_split, pv_done = sem("pt_full"), sem("pt_high"), sem("pt_split"), sem("pv_done")
        o_high, o_split, y_full, y_added = sem("o_high"), sem("o_split"), sem("y_full"), sem("y_added")

        LIFT = KT + 1
        lifted = {"pe": (pt_full, pv_done), "dve": (pt_split, o_split, y_added)}

        def slot(n):
            return ps[:, 2 * (n % 2):2 * (n % 2) + 2, :]

        def turned(j):
            return ps[:, 4 + j % 2, :]

        def o_bank(u):
            return ps[:, 6 + u % 2, :]

        def halves(ap):
            return ap.rearrange("p (n t) -> p n t", n=NB)

        def proj_count(g, e):
            if e[0] == "k":
                return 2 + PROJ * (g + 1) if not (isinstance(g, int) and g < 0) else 1
            return 2 + PROJ * g + e[1] if not (isinstance(g, int) and g < 0) else 2

        def read_of(g, e, nxt):
            own = g + 1 if nxt else g
            if e[0] in "kq":
                return proj_read, proj_count(g, e)
            if e[0] == "v":
                return v_added, own + 1
            if e[0] == "s":
                return exped, own * TILES + e[1] // 2 + 1
            return y_added, LIFT + DC * own + e[1] + 1

        def laps(eng, run):
            run(-1, opening, 0)
            with eng.Fori(0, KV - 1) as g:
                run(g, steady + change, first)
            run(KV - 1, [e for e in steady if e != ("q", PER)] + closing, first)

        def belongs_next(events, n):
            if events is opening:
                return True
            e = events[n]
            return ("k",) in events[:n] and e[0] in "vs" or e[0] == "k" or (e[0] == "t" and e[1] == 0)

        with nc.Block() as block:

            @block.sync
            def _(sp):
                def load(g, *what):
                    if "q" in what:
                        sp.dma_start(wq_raw[:, :, :], net.dram["wq"][g]).then_inc(wq_loaded, 16)
                    if "kv" in what:
                        sp.dma_start(wkv_raw[:, 0, :, :], net.dram["wk"][g]).then_inc(wkv_loaded, 16)
                        sp.dma_start(wkv_raw[:, 1, :, :], net.dram["wv"][g]).then_inc(wkv_loaded, 16)

                norm.sync(sp)
                load(0, "kv", "q")
                load_ffn0_weights(sp, net)
                sp.dma_start(bq[:, :], net.dram["bq"]).then_inc(consts, 16)
                sp.dma_start(bk[:, :], net.dram["bk"]).then_inc(consts, 16)
                sp.dma_start(bv[:, :], net.dram["bv"].partition_broadcast(P)).then_inc(consts, 16)
                sp.dma_start(bo[:, :], net.dram["bo"].partition_broadcast(P)).then_inc(consts, 16)
                with sp.Fori(0, KV - 1) as g:
                    sp.wait_ge(wo_split, 1 + 4 * g)
                    sp.dma_start(wo_raw[:, :, :], net.dram["wo"][g]).then_inc(wo_loaded, 16)
                    sp.wait_ge(wkv_split, g + 1)
                    load(g + 1, "kv")
                    sp.wait_ge(wq_split, 2 * (g + 1))
                    load(g + 1, "q")
                sp.wait_ge(wo_split, 1 + 4 * (KV - 1))
                sp.dma_start(wo_raw[:, :, :], net.dram["wo"][KV - 1]).then_inc(wo_loaded, 16)

            @block.gpsimd
            def _(pool):
                def split(hi, lo, raw, highs, done):
                    shape = list(raw.shape)
                    o = one[:, :]
                    while len(o.shape) < len(shape):
                        o = o.unsqueeze(1)
                    nc.gpsimd.tensor_tensor(hi, raw, o.broadcast_to(shape), ALU.mult).then_inc(w_high, 1)
                    pool.wait_ge(w_high, highs)
                    nc.gpsimd.tensor_tensor(lo, raw, hi.bitcast(F32), ALU.subtract).then_inc(done, 1)

                def split_wkv(g, highs):
                    pool.wait_ge(wkv_loaded, 32 * (g + 1))
                    split(wkv_h[:, :, :, :], wkv_l[:, :, :, :], wkv_raw[:, :, :, :], highs, wkv_split)

                def split_wq(g, c, highs):
                    pool.wait_ge(wq_loaded, 16 * (g + 1))
                    split(wq_h[:, c, :], wq_l[:, c, :], wq_raw[:, c, :], highs, wq_split)

                def split_wo(g, k, highs):
                    pool.wait_ge(wo_loaded, 16 * (g + 1))
                    split(wo_h[:, k, :], wo_l[:, k, :], wo_raw[:, k, :], highs, wo_split)

                def normalise(count, t):
                    pool.wait_ge(inverted, count)
                    nc.gpsimd.tensor_tensor(prob[:, t % RING, :], prob[:, t % RING, :],
                                            inv_sum[:, t:t + 1].broadcast_to([P, T]), ALU.mult).then_inc(normed, 1)

                HIGHS = 1 + DC + PER

                def group(g, tiles):
                    for t in tiles:
                        normalise(g * TILES + t + 1, t % TILES)
                        base = HIGHS * g + 1 + DC
                        if 7 <= t < 7 + PER:
                            if t == 7:
                                pool.wait_ge(y_added, LIFT + DC * g)
                            split_wo(g, t - 7, base + t - 6)
                        if TILES in tiles:
                            if t == 13:
                                pool.wait_ge(v_split, g + 1)
                                split_wkv(g + 1, base + PER + 1)
                            if t in (22, 24):
                                pool.wait_ge(proj_full, proj_count(g, ("q", PER - 1)))
                                split_wq(g + 1, (t - 22) // 2, base + PER + 1 + (t - 20) // 2)
                        elif t == 16:
                            pool.wait_ge(consts, 64)
                            nc.gpsimd.tensor_tensor(net.x[:, :, :], net.x[:, :, :],
                                                    bo[:, :].unsqueeze(1).broadcast_to([P, TT, D]), ALU.add).then_inc(bo_added, 1)

                nc.gpsimd.memset(one[:, :], 1.0).then_inc(ready, 1)
                pool.sem_inc(wo_split, 1)
                pool.wait_ge(ready, 1)
                split_wkv(0, 1)
                for c in range(DC):
                    split_wq(0, c, 2 + c)
                for t in range(LEAD // 2):
                    normalise(t + 1, t)
                with pool.Fori(0, KV - 1) as g:
                    group(g, range(LEAD // 2, TILES + LEAD // 2))
                group(KV - 1, range(LEAD // 2, TILES))

            @block.tensor
            def _(pe):
                def run(g, events, start):
                    jobs = jobs_of(events)
                    spots = [n for n, e in enumerate(events) if e in jobs and (e[0] in "kvqy" or e[1] % 2 == 0)]
                    before = jobs_of(steady + change)[-2:]
                    n = start - 1

                    def begin(place):
                        k = spots.index(place)
                        if k >= 2:
                            q = spots[k - 2]
                            sem_, count = read_of(g, events[q], belongs_next(events, q))
                        elif start == 0:
                            return
                        elif isinstance(g, int):
                            sem_, count = read_of(g - 1, before[k], False)
                        else:
                            sem_, count = read_before(g, k)
                        pe.wait_ge(sem_, count)

                    def read_before(g, k):
                        return y_added, LIFT + DC * g - DC + k + 1

                    if start and not (isinstance(g, int)):
                        pe.wait_ge(exped, TILES * g + LEAD // 2)

                    for place, e in enumerate(events):
                        nxt = belongs_next(events, place)
                        own = g + 1 if nxt else g
                        if place in spots:
                            begin(place)
                            n += 1
                        if e[0] in "kq":
                            if e[0] == "k":
                                pe.wait_ge(wkv_split, g + 2)
                            elif start == 0 or e[1] == PER:
                                pe.wait_ge(wq_split, DC * (g + 2))
                            for b in range(NB):
                                cols = slice(b * BANK, (b + 1) * BANK)
                                for c in range(DC):
                                    hh = slice(e[1] % PER * DH, (e[1] % PER + 1) * DH) if e[0] == "q" else None
                                    wt = (wkv_h[:, 0, c, :], wkv_l[:, 0, c, :]) if e[0] == "k" else \
                                        (wq_h[:, c, hh], wq_l[:, c, hh])
                                    last = product(nc, slot(n)[:, b, :], *wt, xn_h[:, c, cols], xn_l[:, c, cols],
                                                   c == 0, c == DC - 1)
                            last.then_inc(proj_full, 1)
                        if e[0] == "v":
                            for i in range(TT):
                                toks = slice(i * P, (i + 1) * P)
                                for c in range(DC):
                                    last = product(nc, slot(n)[:, i // 4, (i % 4) * P:(i % 4 + 1) * P], xn_h[:, c, toks],
                                                   xn_l[:, c, toks], wkv_h[:, 1, c, :], wkv_l[:, 1, c, :], c == 0, c == DC - 1)
                            last.then_inc(values_full, 1)
                        if e[0] == "s":
                            t, b = divmod(e[1], 2)
                            hh, i = divmod(t, TT)
                            if e[1] % (2 * TT) == 0:
                                pe.wait_ge(proj_split, 2 + PROJ * own + hh)
                            keys = slice(b * BANK, (b + 1) * BANK)
                            last = product(nc, slot(n)[:, b, :], q_h[:, hh % 2, i * P:(i + 1) * P],
                                           q_l[:, hh % 2, i * P:(i + 1) * P], k_h[:, keys], k_l[:, keys], True, True)
                            if b == 1:
                                last.then_inc(s_full, 1)
                        if e[0] == "t":
                            u, kt = divmod(e[1], KT)
                            if kt == 0:
                                pe.wait_ge(normed, own * TILES + 4 * u + 4)
                            pe.wait_ge(pt_split, LIFT + own * STEPS + e[1] - 1)
                            for i in range(4):
                                last = nc.tensor.transpose(turned(e[1])[:, i * P:(i + 1) * P],
                                                           prob[:, (4 * u + i) % RING, kt * P:(kt + 1) * P], net.ident[:, :])
                            last.then_inc(pt_full, 1)
                        if e[0] == "p":
                            u, kt = divmod(e[1], KT)
                            if e[1] == 0:
                                pe.wait_ge(v_split, g + 1)
                            if kt == 0:
                                pe.wait_ge(o_split, LIFT + g * UNITS + u - 1)
                            pe.wait_ge(pt_split, LIFT + g * STEPS + e[1] + 1)
                            keys = slice(kt * P, (kt + 1) * P)
                            product(nc, o_bank(u), v_h[:, keys], v_l[:, keys], pt_h[:, e[1] % 2, :], pt_l[:, e[1] % 2, :],
                                    kt == 0, kt == KT - 1).then_inc(pv_done, 1)
                        if e[0] == "y":
                            if e[1] == 0:
                                pe.wait_ge(wo_split, 1 + 4 * (g + 1))
                                pe.wait_ge(o_split, LIFT + UNITS * (g + 1))
                            for i in range(TT // 2):
                                toks = slice((e[1] * TT // 2 + i) * P, (e[1] * TT // 2 + i + 1) * P)
                                for hh in range(PER):
                                    last = product(nc, tokens_of(slot(n), i), o_h[:, hh, toks], o_l[:, hh, toks],
                                                   wo_h[:, hh, :], wo_l[:, hh, :], hh == 0, hh == PER - 1)
                            last.then_inc(y_full, 1)

                for s in lifted["pe"]:
                    pe.sem_inc(s, LIFT)
                norm.tensor(pe)
                norm.wait_parts(pe)
                laps(pe, run)

            @block.scalar
            def _(act):
                def run(g, events, start):
                    waiting = []
                    later = []
                    n = start - 1

                    def highs(least):
                        while later and later[0][1] >= least:
                            e, _ = later.pop(0)
                            to = k_h[:, :] if e[0] == "k" else q_h[:, e[1] % 2, :]
                            act.wait_ge(proj_read, proj_count(g, e))
                            nc.scalar.activation(to, proj[:, :], ACT.Copy).then_inc(proj_high, 1)

                    def exps():
                        for own, t, k in waiting:
                            act.wait_ge(maxed, own * TILES + t + 1)
                            u = t // 4
                            act.wait_ge(pt_full, LIFT + own * STEPS + KT * (u - 1))
                            nc.scalar.activation(halves(prob[:, t % RING, :]), slot(k), ACT.Exp, bias=neg_max[:, t:t + 1],
                                                 accum_out=row_sum[:, t:t + 1]).then_inc(exped, 1)
                        waiting.clear()

                    for place, e in enumerate(events):
                        own = g + 1 if belongs_next(events, place) else g
                        if e in jobs_of([e]):
                            n += 1
                        if e[0] in "kq":
                            exps()
                            count = proj_count(g, e)
                            act.wait_ge(proj_full, count)
                            if not (isinstance(g, int) and count == 1):
                                act.wait_ge(proj_split, count - 1)
                            if e[0] == "k":
                                ins = nc.scalar.activation(halves(proj[:, :]), slot(n), ACT.Identity,
                                                           bias=bk[:, bass.ds(g + 1, 1)])
                            else:
                                h = 0 if start == 0 else g * PER + e[1]
                                ins = nc.scalar.activation(halves(proj[:, :]), slot(n), ACT.Identity,
                                                           bias=bq[:, bass.ds(h, 1)], scale=Q_SCALE)
                            ins.then_inc(proj_read, 1)
                            later.append([e, 0])
                            highs(0 if start == 0 else 1)
                        if e[0] == "s" and e[1] % 2 == 1:
                            exps()
                            waiting.append((own, e[1] // 2, n))
                        if e[0] == "t":
                            act.wait_ge(pt_full, LIFT + own * STEPS + e[1] + 1)
                            act.wait_ge(pv_done, LIFT + own * STEPS + e[1] - 1)
                            nc.scalar.activation(pt_h[:, e[1] % 2, :], turned(e[1]), ACT.Copy).then_inc(pt_high, 1)
                            exps()
                            for w in later:
                                w[1] += 1
                            highs(2)
                        if e[0] == "y":
                            exps()
                        if e[0] == "p" and e[1] % KT == KT - 1:
                            u = e[1] // KT
                            if u == 0:
                                act.wait_ge(y_added, LIFT + DC * g)
                            act.wait_ge(pv_done, LIFT + g * STEPS + e[1] + 1)
                            nc.scalar.activation(o_h[:, u // NB, (u % NB) * BANK:(u % NB + 1) * BANK], o_bank(u),
                                                 ACT.Copy).then_inc(o_high, 1)
                    exps()
                    highs(0)

                norm.scalar(act)
                act.wait_ge(bq_scaled, 1)
                act.wait_ge(consts, 64)
                laps(act, run)

            @block.vector
            def _(dve):
                def run(g, events, start):
                    n = start - 1
                    waiting = []
                    later = []

                    def inverts(least):
                        while waiting and waiting[0][2] >= least:
                            own, t, _ = waiting.pop(0)
                            dve.wait_ge(exped, own * TILES + t + 1)
                            nc.vector.reciprocal(inv_sum[:, t:t + 1], row_sum[:, t:t + 1]).then_inc(inverted, 1)

                    def lows(least):
                        while later and later[0][1] >= least:
                            e, _ = later.pop(0)
                            dve.wait_ge(proj_high, proj_count(g, e))
                            hi, lo = (k_h[:, :], k_l[:, :]) if e[0] == "k" else (q_h[:, e[1] % 2, :], q_l[:, e[1] % 2, :])
                            nc.vector.tensor_tensor(lo, proj[:, :], hi.bitcast(F32), ALU.subtract).then_inc(proj_split, 1)

                    for place, e in enumerate(events):
                        own = g + 1 if belongs_next(events, place) else g
                        if e in jobs_of([e]):
                            n += 1
                        if e[0] in "kq":
                            later.append([e, 0])
                            lows(0 if start == 0 else 1)
                        if e[0] == "v":
                            dve.wait_ge(values_full, own + 1)
                            if start:
                                dve.wait_ge(v_split, g + 1)
                            nc.vector.tensor_tensor(v_full[:, :].rearrange("p (i d) -> p i d", d=DH),
                                                    slot(n).rearrange("p n (i d) -> p (n i) d", d=DH),
                                                    bv[:, bass.ds(own * DH, DH)].unsqueeze(1).broadcast_to([P, TT, DH]),
                                                    ALU.add).then_inc(v_added, 1)
                        if e[0] == "vs":
                            if start:
                                dve.wait_ge(pv_done, LIFT + STEPS * (g + 1))
                            dve.wait_ge(v_added, own + 1)
                            nc.vector.tensor_copy(v_h[:, :], v_full[:, :]).then_inc(v_high, 1)
                            dve.wait_ge(v_high, own + 1)
                            nc.vector.tensor_tensor(v_l[:, :], v_full[:, :], v_h[:, :].bitcast(F32), ALU.subtract)\
                                .then_inc(v_split, 1)
                        if e[0] == "s" and e[1] % 2 == 1:
                            t = e[1] // 2
                            dve.wait_ge(s_full, own * TILES + t + 1)
                            nc.vector.tensor_reduce(neg_max[:, t:t + 1], slot(n), AX.XY, ALU.max, negate=True).then_inc(maxed, 1)
                            inverts(0)
                            waiting.append([own, t, 0])
                        if e[0] == "t":
                            for w in waiting:
                                w[2] += 1
                            inverts(2)
                            dve.wait_ge(pt_high, own * STEPS + e[1] + 1)
                            nc.vector.tensor_tensor(pt_l[:, e[1] % 2, :], turned(e[1]), pt_h[:, e[1] % 2, :].bitcast(F32),
                                                    ALU.subtract).then_inc(pt_split, 1)
                            for w in later:
                                w[1] += 1
                            lows(2 if later and later[0][0] == ("k",) else 3)
                        if e[0] == "p" and e[1] % KT == KT - 1:
                            u = e[1] // KT
                            dve.wait_ge(o_high, g * UNITS + u + 1)
                            cols = slice((u % NB) * BANK, (u % NB + 1) * BANK)
                            nc.vector.tensor_tensor(o_l[:, u // NB, cols], o_bank(u), o_h[:, u // NB, cols].bitcast(F32),
                                                    ALU.subtract).then_inc(o_split, 1)
                        if e[0] == "y":
                            dve.wait_ge(y_full, DC * g + e[1] + 1)
                            dve.wait_ge(y_added, LIFT + DC * g)
                            if isinstance(g, int):
                                dve.wait_ge(bo_added, 1)
                            add_to_x(nc, net, e[1] * TT // 2, slot(n)).then_inc(y_added, 1)
                            if isinstance(g, int):
                                dve.wait_ge(y_added, LIFT + DC * g + e[1] + 1)
                                take_moments(nc, net, dve, range(e[1] * TT // 2, (e[1] + 1) * TT // 2))
                    inverts(0)
                    lows(0)

                for s in lifted["dve"]:
                    dve.sem_inc(s, LIFT)
                norm.vector(dve)
                dve.wait_ge(consts, 64)
                nc.vector.tensor_scalar(bq[:, :], bq[:, :], Q_SCALE, None, ALU.mult).then_inc(bq_scaled, 1)
                laps(dve, run)
                dve.wait_ge(y_added, LIFT + DC * KV)


EXP0, GROUPS, LAT, INTER, SHARED0 = 32, 4, 128, 128, 512
ROUTED_SCALE = 2.5
SH0 = SHARED0 // P
BIG, TAKEN = 1e30, 3e38


FC1, UP = 0, DC * LAT
DOWN = UP + DC * SHARED0
FC2 = DOWN + SH0 * D
RAW0 = FC2 + D
PIECES0 = (("fc1", FC1, UP), ("sup0", UP, DOWN), ("sdn0", DOWN, FC2), ("fc2", FC2, RAW0))


def load_ffn0_weights(sp, net):
    for name, at, end in PIECES0:
        sp.dma_start(net.raw[:, at:end], net.dram[name]).then_inc(net.raw_loaded, 16)


def squared_relu_experts_phase(nc, net):
    BODY, RAW, RING, ROWS = 8, 4, 4, 2
    SPLIT_LAG, DOWN_LAG, AHEAD = 2, 4, 2
    EARLY = SH0 // 2
    EG = EXP0 // GROUPS
    with ExitStack() as mem:
        sb = lambda n, s, d=F32: mem.enter_context(nc.sbuf_tensor(f"f0_{n}", s, d))
        sem = lambda n: net.ctx.enter_context(nc.semaphore(f"f0_{n}"))
        ps, xn_h, xn_l = net.ps, net.xn_h, net.xn_l
        xn = sb("xn", [P, DC, T])
        gate, gate_bias = sb("gate", [P, DC, EXP0]), sb("gate_bias", [P, EXP0])
        w = net.raw
        w_h, w_l = sb("w_h", [P, RAW0], F32R), sb("w_l", [P, RAW0], F32R)
        e_raw = sb("e_raw", [P, RAW, 2, P])
        e_h, e_l = sb("e_h", [P, BODY, 2, P], F32R), sb("e_l", [P, BODY, 2, P], F32R)
        lat_h, lat_l = sb("lat_h", [P, T], F32R), sb("lat_l", [P, T], F32R)
        relu, act = sb("relu", [P, 2, T]), sb("act", [P, RING, T])
        a_h, a_l = sb("a_h", [P, RING, T], F32R), sb("a_l", [P, RING, T], F32R)
        s_h, s_l = sb("s_h", [P, SH0, T], F32R), sb("s_l", [P, SH0, T], F32R)
        cw_row = sb("cw_row", [P, ROWS, T])
        score, biased = sb("score", [P, TT, EXP0]), sb("biased", [P, TT, EXP0])
        best, found = sb("best", [P, TT, GROUPS, 8]), sb("found", [P, TT, EXP0])
        g_score, g_out = sb("g_score", [P, TT, GROUPS + 6]), sb("g_out", [P, TT, GROUPS + 6])
        g_best, g_take = sb("g_best", [P, TT, 8]), sb("g_take", [P, TT, 8])
        cw, total = sb("cw", [P, TT, EXP0]), sb("total", [P, TT])
        cw_t = sb("cw_t", [EXP0, T])
        cw_dram = net.cw_dram
        norm = Norm(nc, net, "n1", mem, full=xn[:, :, :], xc=cw_row[:, :, :].rearrange("p r (k d) -> p (r k) d", d=D))

        consts = sem("consts")
        w_high, w_split = sem("w_high"), sem("w_split")
        logits, scored, routed = sem("logits"), sem("scored"), sem("routed")
        cw_turned, cw_copied, cw_stored = sem("cw_turned"), sem("cw_copied"), sem("cw_stored")
        e_loaded = [sem(f"e_loaded{r}") for r in range(RAW)]
        row_loaded = [sem(f"row_loaded{r}") for r in range(ROWS)]
        e_high, e_split = sem("e_high"), sem("e_split")
        slot_full = sem("slot_full")
        lat_high, lat_split = sem("lat_high"), sem("lat_split")
        relued, squared, weighed = sem("relued"), sem("squared"), sem("weighed")
        early_split = sem("early_split")
        act_high, act_split, down_done = sem("act_high"), sem("act_split"), sem("down_done")
        shared_full, shared_added = sem("shared_full"), sem("shared_added")
        y_full, y_added, chain = sem("y_full"), sem("y_added"), sem("chain")

        def slot(n):
            return ps[:, 2 * (n % 2):2 * (n % 2) + 2, :]

        def blocks(ap):
            return ap.rearrange("p (n t) -> p n t", n=NB)

        def steps(eng, loop_end, last, step):
            for n in range(BODY):
                step(0, n)
            with eng.Fori(1, loop_end) as it:
                for r in range(BODY):
                    step(it, r)
            for n in range(loop_end * BODY, last):
                step(*divmod(n, BODY))

        def known(it, r, low, high=EXP0 + BODY):
            return not isinstance(it, int) or low <= it * BODY + r < high

        with nc.Block() as block:

            @block.sync
            def _(sp):
                sp.dma_start(gate[:, :, :], net.dram["gate0"]).then_inc(consts, 16)
                sp.dma_start(gate_bias[:, :], net.dram["gate_bias"].partition_broadcast(P)).then_inc(consts, 16)

                def load_expert(it, r):
                    n = it * BODY + r
                    if known(it, r, RAW):
                        sp.wait_ge(e_split, n - RAW + 1)
                    sp.dma_start(e_raw[:, r % RAW, :, :], net.dram["we0"][n]).then_inc(e_loaded[r % RAW], 16)

                def load_row(it, r):
                    n = it * BODY + r
                    if known(it, r, ROWS):
                        sp.wait_ge(weighed, n - ROWS + 1)
                    sp.dma_start(cw_row[:, r % ROWS, :], cw_dram[n].partition_broadcast(P))\
                        .then_inc(row_loaded[r % ROWS], 16)

                for r in range(RAW):
                    load_expert(0, r)
                sp.wait_ge(w_high, len(PIECES0))
                sp.wait_ge(w_split, len(PIECES0))
                load_linear_weights(sp, net)
                sp.wait_ge(cw_copied, 1)
                sp.dma_start(cw_dram, cw_t[:, :]).then_inc(cw_stored, 16)
                sp.wait_ge(cw_stored, 16)

                def step(it, r):
                    load_row(it, r)
                    if known(it, r, 0, EXP0 - RAW):
                        load_expert(it, r + RAW)

                steps(sp, EXP0 // BODY - 1, EXP0, step)

            @block.tensor
            def _(pe):
                norm.tensor(pe)
                norm.wait_parts(pe)
                def project(n, at, width, k):
                    for b in range(NB):
                        cols = slice(b * BANK, (b + 1) * BANK)
                        for c in range(DC):
                            part = slice(at + c * width + k * P, at + c * width + (k + 1) * P)
                            last = product(nc, slot(n)[:, b, :], w_h[:, part], w_l[:, part], xn_h[:, c, cols],
                                           xn_l[:, c, cols], c == 0, c == DC - 1)
                    last.then_inc(slot_full, 1)

                pe.wait_ge(w_split, 2)
                project(0, FC1, LAT, 0)
                norm.wait_full(pe)
                pe.wait_ge(consts, 34)
                for i in range(TT):
                    for c in range(DC):
                        last = nc.tensor.matmul(ps[:, 6, i * EXP0:(i + 1) * EXP0], xn[:, c, i * P:(i + 1) * P],
                                                gate[:, c, :], start=c == 0, stop=c == DC - 1)
                last.then_inc(logits, 1)
                for k in range(SH0):
                    if k == 1:
                        pe.wait_ge(lat_split, 1)
                    if k > 1:
                        pe.wait_ge(relued, k - 1)
                    project(1 + k, UP, SHARED0, k)
                pe.wait_ge(routed, 1)
                for i in range(TT):
                    last = nc.tensor.transpose(ps[0:EXP0, 6 + i // 4, (i % 4) * P:(i % 4 + 1) * P], cw[:, i, :], net.ident[:, :])
                last.then_inc(cw_turned, 1)
                def shared_down(j):
                    if j == 0:
                        pe.wait_ge(w_split, 4)
                        pe.wait_ge(early_split, EARLY)
                        pe.wait_ge(act_split, SH0 - EARLY)
                    if j == TT // 4:
                        pe.wait_ge(cw_copied, 1)
                    for i in (2 * j, 2 * j + 1):
                        for k in range(SH0):
                            toks, part = slice(i * P, (i + 1) * P), slice(DOWN + k * D, DOWN + (k + 1) * D)
                            last = product(nc, tokens_of(ps[:, 4:8, :], i), s_h[:, k, toks], s_l[:, k, toks], w_h[:, part],
                                           w_l[:, part], k == 0, k == SH0 - 1)
                    last.then_inc(shared_full, 1)

                def step(it, r):
                    n = it * BODY + r
                    if known(it, r, 0, EXP0):
                        pe.wait_ge(e_split, n + 1)
                        pe.wait_ge(squared, n + SH0 - 1)
                        for b in range(NB):
                            cols = slice(b * BANK, (b + 1) * BANK)
                            last = product(nc, slot(1 + SH0 + r)[:, b, :], e_h[:, r, 0, :], e_l[:, r, 0, :],
                                           lat_h[:, cols], lat_l[:, cols], True, True)
                        last.then_inc(slot_full, 1)
                        if isinstance(it, int) and n < TT // 2:
                            shared_down(n)
                    if known(it, r, DOWN_LAG):
                        m = (r - DOWN_LAG) % BODY
                        pe.wait_ge(act_split, n - DOWN_LAG + 1 + SH0 - EARLY)
                        first = it == 0 and r == DOWN_LAG if isinstance(it, int) else False
                        final = n == EXP0 - 1 + DOWN_LAG if isinstance(it, int) else False
                        if first:
                            pe.wait_ge(shared_added, 1)
                        for b in range(NB):
                            cols = slice(b * BANK, (b + 1) * BANK)
                            last = product(nc, ps[:, 4 + b, :], e_h[:, m, 1, :], e_l[:, m, 1, :], a_h[:, m % RING, cols],
                                           a_l[:, m % RING, cols], first, final)
                        last.then_inc(down_done, 1)

                steps(pe, EXP0 // BODY, EXP0 + DOWN_LAG, step)
                pe.wait_ge(squared, SH0 + EXP0)
                pe.wait_ge(lat_split, 2)
                for i in range(TT):
                    toks = slice(i * P, (i + 1) * P)
                    last = product(nc, tokens_of(ps[:, 0:4, :], i), lat_h[:, toks], lat_l[:, toks], w_h[:, FC2:RAW0],
                                   w_l[:, FC2:RAW0], True, True)
                    if i % 2:
                        last.then_inc(y_full, 1)

            @block.scalar
            def _(act_e):
                act_e.wait_ge(net.raw_loaded, 16 * len(PIECES0))
                for _, at, end in PIECES0:
                    nc.scalar.activation(w_h[:, at:end], w[:, at:end], ACT.Copy).then_inc(w_high, 1)
                norm.scalar(act_e)
                def high_weights(it, r):
                    act_e.wait_ge(e_loaded[r % RAW], 16 * (it * (BODY // RAW) + r // RAW) + 16)
                    if known(it, r, BODY):
                        act_e.wait_ge(down_done, it * BODY + (r - BODY + 1))
                    nc.scalar.activation(e_h[:, r % BODY, :, :], e_raw[:, r % RAW, :, :], ACT.Copy).then_inc(e_high, 1)

                act_e.wait_ge(slot_full, 1)
                nc.scalar.activation(blocks(lat_h[:, :]), slot(0), ACT.Copy).then_inc(lat_high, 1)
                act_e.wait_ge(logits, 1)
                nc.scalar.activation(score[:, :, :], ps[:, 6, 0:TT * EXP0].rearrange("p (i e) -> p i e", e=EXP0),
                                     ACT.Sigmoid).then_inc(scored, 1)

                def relu_slot(n, k):
                    act_e.wait_ge(slot_full, n + 2)
                    if not isinstance(n, int) or n >= 2:
                        act_e.wait_ge(squared, n - 1)
                    nc.scalar.activation(blocks(relu[:, k % 2, :]), slot(1 + k), ACT.Relu).then_inc(relued, 1)

                def high_shared(k):
                    act_e.wait_ge(squared, k + 1)
                    nc.scalar.activation(s_h[:, k, :], act[:, k % RING, :], ACT.Copy).then_inc(act_high, 1)

                for r in range(AHEAD):
                    high_weights(0, r)
                for k in range(SH0):
                    relu_slot(k, k)
                    if k < EARLY:
                        act_e.wait_ge(relued, k + 1)
                        nc.scalar.activation(act[:, k % RING, :], relu[:, k % 2, :], ACT.Square).then_inc(squared, 1)
                    elif k == EARLY:
                        continue
                    else:
                        high_shared(k - 1)
                    high_shared(k)

                def step(it, r):
                    n = it * BODY + r
                    if known(it, r, 0, EXP0):
                        relu_slot(n + SH0, r + SH0)
                    if known(it, r, 0, EXP0 - AHEAD):
                        high_weights(it, r + AHEAD)
                    if known(it, r, SPLIT_LAG):
                        m = (r - SPLIT_LAG) % RING
                        act_e.wait_ge(weighed, n - SPLIT_LAG + 1)
                        if known(it, r, SPLIT_LAG + RING):
                            act_e.wait_ge(down_done, n - SPLIT_LAG - RING + 1)
                        nc.scalar.activation(a_h[:, m, :], act[:, m, :], ACT.Copy).then_inc(act_high, 1)

                steps(act_e, EXP0 // BODY - 1, EXP0 + SPLIT_LAG, step)
                act_e.wait_ge(down_done, EXP0)
                nc.scalar.activation(blocks(lat_h[:, :]), ps[:, 4:6, :], ACT.Copy).then_inc(lat_high, 1)

            @block.gpsimd
            def _(pool):
                nc.gpsimd.memset(g_score[:, :, :], -BIG).then_inc(consts, 1)
                nc.gpsimd.memset(g_take[:, :, :], -BIG).then_inc(consts, 1)
                for k, (_, at, end) in enumerate(PIECES0):
                    pool.wait_ge(w_high, k + 1)
                    nc.gpsimd.tensor_tensor(w_l[:, at:end], w[:, at:end], w_h[:, at:end].bitcast(F32), ALU.subtract)\
                        .then_inc(w_split, 1)

                for k in range(EARLY):
                    pool.wait_ge(act_high, k + 1)
                    nc.gpsimd.tensor_tensor(s_l[:, k, :], act[:, k % RING, :], s_h[:, k, :].bitcast(F32),
                                            ALU.subtract).then_inc(early_split, 1)

                def step(it, r):
                    pool.wait_ge(row_loaded[r % ROWS], 16 * (it * (BODY // ROWS) + r // ROWS) + 16)
                    pool.wait_ge(squared, it * BODY + r + SH0 + 1)
                    nc.gpsimd.tensor_tensor(act[:, r % RING, :], act[:, r % RING, :], cw_row[:, r % ROWS, :],
                                            ALU.mult).then_inc(weighed, 1)

                steps(pool, EXP0 // BODY, EXP0, step)

            @block.vector
            def _(dve):
                links = [0]

                def link(ins):
                    ins.then_inc(chain, 1)
                    links[0] += 1
                    dve.wait_ge(chain, links[0])

                norm.vector(dve)
                dve.wait_ge(consts, 34)
                dve.wait_ge(lat_high, 1)
                nc.vector.tensor_tensor(blocks(lat_l[:, :]), slot(0), blocks(lat_h[:, :]).bitcast(F32),
                                        ALU.subtract).then_inc(lat_split, 1)
                dve.wait_ge(scored, 1)
                link(nc.vector.tensor_tensor(biased[:, :, :], score[:, :, :],
                                             gate_bias[:, :].unsqueeze(1).broadcast_to([P, TT, EXP0]), ALU.add))
                for i in range(TT):
                    for g in range(GROUPS):
                        last = nc.vector.max(best[:, i, g, :], biased[:, i, g * EG:(g + 1) * EG])
                link(last)
                def square(n, k):
                    if not isinstance(n, int) or n >= RING:
                        if isinstance(n, int) and n - RING < EARLY:
                            dve.wait_ge(early_split, n - RING + 1)
                        else:
                            dve.wait_ge(act_split, n - RING + 1 - EARLY)
                    dve.wait_ge(relued, n + 1)
                    nc.vector.scalar_tensor_tensor(blocks(act[:, k % RING, :]), slot(1 + k), 0.0, blocks(relu[:, k % 2, :]),
                                                   ALU.max, ALU.mult).then_inc(squared, 1)

                link(nc.vector.tensor_tensor(g_score[:, :, 0:GROUPS], best[:, :, :, 0], best[:, :, :, 1], ALU.add))
                for i in range(TT):
                    last = nc.vector.max(g_best[:, i, :], g_score[:, i, 0:8])
                link(last)
                link(nc.vector.tensor_copy(g_take[:, :, 0:2], g_best[:, :, 0:2]))
                for i in range(TT):
                    last = nc.vector.match_replace(g_out[:, i, :], g_take[:, i, :], g_score[:, i, :], TAKEN)
                link(last)
                link(nc.vector.tensor_scalar(g_out[:, :, :], g_out[:, :, :], TAKEN, None, ALU.is_equal))
                link(nc.vector.tensor_scalar(g_out[:, :, :], g_out[:, :, :], 1.0, BIG, ALU.subtract, ALU.mult))
                link(nc.vector.tensor_tensor(biased[:, :, :].rearrange("p i (g e) -> p i g e", g=GROUPS),
                                             biased[:, :, :].rearrange("p i (g e) -> p i g e", g=GROUPS),
                                             g_out[:, :, 0:GROUPS].unsqueeze(3).broadcast_to([P, TT, GROUPS, EG]), ALU.add))
                for i in range(TT):
                    last = nc.vector.max(g_best[:, i, :], biased[:, i, :])
                link(last)
                for i in range(TT):
                    last = nc.vector.match_replace(found[:, i, :], g_best[:, i, :], biased[:, i, :], TAKEN)
                link(last)
                link(nc.vector.scalar_tensor_tensor(cw[:, :, :], found[:, :, :], TAKEN, score[:, :, :], ALU.is_equal, ALU.mult))
                link(nc.vector.tensor_reduce(total[:, :], cw[:, :, :], AX.X, ALU.add))
                link(nc.vector.reciprocal(total[:, :], total[:, :]))
                nc.vector.scalar_tensor_tensor(cw[:, :, :], cw[:, :, :], ROUTED_SCALE,
                                               total[:, :].unsqueeze(2).broadcast_to([P, TT, EXP0]), ALU.mult, ALU.mult)\
                    .then_inc(routed, 1)
                def low_weights(it, r):
                    dve.wait_ge(e_high, it * BODY + r + 1)
                    nc.vector.tensor_tensor(e_l[:, r % BODY, :, :], e_raw[:, r % RAW, :, :], e_h[:, r % BODY, :, :].bitcast(F32),
                                            ALU.subtract).then_inc(e_split, 1)

                for r in range(AHEAD):
                    low_weights(0, r)
                square(2, 2)
                dve.wait_ge(cw_turned, 1)
                nc.vector.tensor_copy(blocks(cw_t[:, :]), ps[0:EXP0, 6:8, :]).then_inc(cw_copied, 1)
                square(3, 3)
                for k in range(EARLY, SH0):
                    dve.wait_ge(act_high, k + 1)
                    nc.vector.tensor_tensor(s_l[:, k, :], act[:, k % RING, :], s_h[:, k, :].bitcast(F32),
                                            ALU.subtract).then_inc(act_split, 1)


                def step(it, r):
                    n = it * BODY + r
                    if known(it, r, 0, EXP0):
                        square(n + SH0, r + SH0)
                    if known(it, r, 0, EXP0 - AHEAD):
                        low_weights(it, r + AHEAD)
                    if known(it, r, SPLIT_LAG):
                        m = (r - SPLIT_LAG) % RING
                        dve.wait_ge(act_high, n - SPLIT_LAG + 1 + SH0)
                        nc.vector.tensor_tensor(a_l[:, m, :], act[:, m, :], a_h[:, m, :].bitcast(F32),
                                                ALU.subtract).then_inc(act_split, 1)
                    if isinstance(it, int) and n in (2, 4):
                        half = n // 2 - 1
                        dve.wait_ge(shared_full, (half + 1) * TT // 4)
                        add_to_x(nc, net, half * TT // 2, ps[:, 4 + 2 * half:6 + 2 * half, :]).then_inc(shared_added, 1)

                steps(dve, EXP0 // BODY - 1, EXP0 + SPLIT_LAG, step)
                dve.wait_ge(lat_high, 2)
                nc.vector.tensor_tensor(blocks(lat_l[:, :]), ps[:, 4:6, :], blocks(lat_h[:, :]).bitcast(F32),
                                        ALU.subtract).then_inc(lat_split, 1)
                dve.wait_ge(shared_added, NB)
                add_pairs(nc, net, dve, ps[:, 0:4, :], y_full, y_added, range(TT // 2), 0)


H1, HD, CHUNK = 16, 16, 128
ROPE_BASE, RMS_EPS = 10000.0, 1e-6


def decay_tables():
    half = HD // 2
    theta = ROPE_BASE ** (-2.0 * np.arange(half, dtype=np.float32) / HD)
    angle = (np.arange(T, dtype=np.float32)[:, None] * theta.astype(np.float32)[None, :]).astype(np.float32)
    cos, sin = np.cos(angle), np.sin(angle)
    by_tile = lambda a: a.reshape(TT, P, -1).transpose(1, 0, 2)
    log_lam = -(2.0 ** (-8.0 * (np.arange(H1, dtype=np.float32) + 1.0) / H1))
    at = np.arange(CHUNK, dtype=np.float32)
    diff = at[None, :] - at[:, None]
    decay = np.where(diff[:, None, :] >= 0, np.exp(np.minimum(log_lam[None, :, None] * diff[:, None, :], 0)), 0)
    head = np.arange(P) // HD
    return {
        "cos": by_tile(np.concatenate([cos, cos], 1)), "sin": by_tile(np.concatenate([-sin, sin], 1)),
        "decay": decay,
        "decay_q": np.exp(log_lam[None, :] * (at[:, None] + 1)),
        "decay_k": np.exp(log_lam[None, :] * (CHUNK - 1 - at[:, None])),
        "lam_c": np.exp(log_lam.reshape(DC, P // HD)[:, head].T * CHUNK),
        "same_head": (head[:, None] == head[None, :]) * 1.0,
        "in_pair": (head[:, None] % 2 == np.arange(2)[None, :]) * 1.0,
    }


QK, VG = 2 * D, D + HD
W1 = QK + VG
RAW1 = DC * (W1 + D)


def load_linear_weights(sp, net):
    sp.dma_start(net.raw[:, 0:DC * W1].rearrange("p (c n) -> p c n", c=DC), net.dram["w1a"]).then_inc(net.raw_loaded, 16)
    sp.dma_start(net.raw[:, DC * W1:RAW1].rearrange("p (c n) -> p c n", c=DC), net.dram["wo1"]).then_inc(net.raw_loaded, 16)


def linear_attention_phase(nc, net):
    W = W1
    PAIRS = P // 32
    with ExitStack() as mem:
        sb = lambda n, s, d=F32: mem.enter_context(nc.sbuf_tensor(f"la_{n}", s, d))
        sem = lambda n: net.ctx.enter_context(nc.semaphore(f"la_{n}"))
        ps, xn_h, xn_l = net.ps, net.xn_h, net.xn_l
        w = net.raw[:, 0:DC * W].rearrange("p (c n) -> p c n", c=DC)
        wo = net.raw[:, DC * W:RAW1].rearrange("p (c n) -> p c n", c=DC)
        w_h, w_l = sb("w_h", [P, DC, W], F32R), sb("w_l", [P, DC, W], F32R)
        wo_h, wo_l = sb("wo_h", [P, DC, D], F32R), sb("wo_l", [P, DC, D], F32R)
        wg2, weight = sb("wg2", [HD, D]), sb("weight", [P, DC])
        cos, sin = sb("cos", [P, TT, HD]), sb("sin", [P, TT, HD])
        decay = sb("decay", [P, H1, CHUNK])
        decay_q, decay_k = sb("decay_q", [P, H1]), sb("decay_k", [P, H1])
        lam_c, same_head, in_pair = sb("lam_c", [P, DC]), sb("same_head", [P, P]), sb("in_pair", [P, 2])
        act = sb("act", [P, 2, QK])
        by_cos, by_sin = sb("by_cos", [P, 2, QK]), sb("by_sin", [P, 2, QK])
        rot = sb("rot", [P, 2, QK])
        v = sb("v", [P, TT, D])
        kd = sb("kd", [P, 4, D])
        q_t = sb("q_t", [P, 4, DC, P])
        qp_h, qp_l = sb("qp_h", [P, 2, DC, 2, P], F32R), sb("qp_l", [P, 2, DC, 2, P], F32R)
        k_h, k_l = sb("k_h", [P, 2, DC, P], F32R), sb("k_l", [P, 2, DC, P], F32R)
        sc = sb("sc", [P, 2, H1, CHUNK])
        state, kv = sb("state", [P, DC, P]), sb("kv", [P, DC, P])
        inter = sb("inter", [P, 2, D])
        o, gate, sq = sb("o", [P, TT, D]), sb("gate", [P, TT, D]), sb("sq", [P, TT, D])
        g1_t = sb("g1_t", [HD, T])
        ms, rms, root = sb("ms", [P, TT, H1]), sb("rms", [P, TT, H1]), sb("root", [P, 2, TT * H1])
        o_h, o_l = sb("o_h", [P, DC, T], F32R), sb("o_l", [P, DC, T], F32R)

        consts = sem("consts")
        w_high, w_split = sem("w_high"), sem("w_split")
        projected, act_done, v_done = sem("projected"), sem("act_done"), sem("v_done")
        cos_done, sin_done, rotated, kd_done = sem("cos_done"), sem("sin_done"), sem("rotated"), sem("kd_done")
        turned, t_high, t_split = sem("turned"), sem("t_high"), sem("t_split")
        sc_full, sc_done = sem("sc_full"), sem("sc_done")
        out_full, decayed, state_done = sem("out_full"), sem("decayed"), sem("state_done")
        inter_done, o_done = sem("inter_done"), sem("o_done")
        g1_full, g1_copied, gate_full, gate_done = sem("g1_full"), sem("g1_copied"), sem("gate_full"), sem("gate_done")
        gated, squares, scaled, chain = sem("gated"), sem("squares"), sem("scaled"), sem("chain")
        o_turned, o_high, o_split = sem("o_turned"), sem("o_high"), sem("o_split")
        y_full, y_added = sem("y_full"), sem("y_added")

        norm = Norm(nc, net, "n2", mem, xc=sq[:, :, :])
        SCORE_BANKS = [5, 6, 7, 4]
        O_BANKS = [[5, 6], [7, 4]]
        STEPS = TT + 2
        GROUPS1 = TT // 2
        G1 = slice(QK + D, W)

        WEIGHTS = [(w_h[:, :, G1], w_l[:, :, G1], w[:, :, G1]),
                   (w_h[:, :, 0:QK + D], w_l[:, :, 0:QK + D], w[:, :, 0:QK + D]),
                   (wo_h[:, :, :], wo_l[:, :, :], wo[:, :, :])]

        def heads(ap):
            return ap.rearrange("p (h e) -> p h e", e=HD)

        def pair(k):
            return slice(2 * k, 2 * k + 2)

        def group_at(n):
            return (n - 4) // 2 if n >= 4 and n % 2 == 0 else None

        def of_pair(ap, r):
            return ap.rearrange("p (c r j) t -> p c r (j t)", c=DC, j=2)[:, :, r, :]

        with nc.Block() as block:

            @block.sync
            def _(sp):
                for to, name in ((cos[:, :, :], "cos"), (sin[:, :, :], "sin"), (decay_k[:, :], "decay_k"),
                                 (in_pair[:, :], "in_pair"), (decay[:, :, :], "decay"), (decay_q[:, :], "decay_q"),
                                 (lam_c[:, :], "lam_c"), (same_head[:, :], "same_head"), (wg2[:, :], "wg2")):
                    sp.dma_start(to, net.dram[name]).then_inc(consts, 16)
                sp.dma_start(weight[:, :], net.dram["norm_weight"]).then_inc(consts, 16)
                sp.wait_ge(w_high, len(WEIGHTS))
                sp.wait_ge(w_split, len(WEIGHTS))
                load_ffn1_weights(sp, net)

            @block.gpsimd
            def _(pool):
                nc.gpsimd.memset(state[:, :, :], 0.0).then_inc(state_done, 1)
                for k, (hi, lo, raw) in enumerate(WEIGHTS):
                    pool.wait_ge(w_high, k + 1)
                    nc.gpsimd.tensor_tensor(lo, raw, hi.bitcast(F32), ALU.subtract).then_inc(w_split, 1)
                pool.wait_ge(consts, 160)

                def gate_output(i):
                    pool.wait_ge(o_done, i + 1)
                    pool.wait_ge(gate_done, i // 2 + 1)
                    nc.gpsimd.tensor_tensor(o[:, i, :], o[:, i, :], gate[:, i, :], ALU.mult).then_inc(gated, 1)

                for n in range(TT):
                    if n >= 3:
                        gate_output(n - 3)
                    a = act[:, n % 2, :].rearrange("p (h j e) -> p h j e", j=2, e=HD // 2)
                    b = by_sin[:, n % 2, :].rearrange("p (h j e) -> p h j e", j=2, e=HD // 2)
                    s = sin[:, n, :].rearrange("p (j e) -> p j e", j=2)
                    pool.wait_ge(act_done, n + 1)
                    if n >= 2:
                        pool.wait_ge(rotated, n - 1)
                    for j in range(2):
                        nc.gpsimd.tensor_tensor(b[:, :, j, :], a[:, :, 1 - j, :],
                                                s[:, j, :].unsqueeze(1).broadcast_to([P, 2 * H1, HD // 2]), ALU.mult)\
                            .then_inc(sin_done, 1)
                    pool.wait_ge(rotated, n + 1)
                    if n >= 4:
                        pool.wait_ge(out_full, n - 3)
                    nc.gpsimd.tensor_tensor(heads(kd[:, n % 4, :]), heads(rot[:, n % 2, D:]),
                                            decay_k[:, :].unsqueeze(2).broadcast_to([P, H1, HD]), ALU.mult).then_inc(kd_done, 1)
                for i in range(TT - 3, TT):
                    gate_output(i)

            @block.tensor
            def _(pe):
                def projections(n):
                    toks = slice(n * P, (n + 1) * P)
                    if n:
                        pe.wait_ge(act_done, n)
                        pe.wait_ge(v_done, n)
                    for bank, cols in ((0, slice(0, QK)), (1, slice(QK, QK + D))):
                        for c in range(DC):
                            last = product(nc, ps[:, bank, 0:cols.stop - cols.start], xn_h[:, c, toks], xn_l[:, c, toks],
                                           w_h[:, c, cols], w_l[:, c, cols], c == 0, c == DC - 1)
                    last.then_inc(projected, 1)

                def transposes(n):
                    pe.wait_ge(rotated, n + 1)
                    if n:
                        pe.wait_ge(t_split, n)
                    else:
                        pe.wait_ge(g1_copied, 1)
                    for b in range(2 * DC):
                        last = nc.tensor.transpose(ps[:, 2, b * P:(b + 1) * P], rot[:, n % 2, b * P:(b + 1) * P], net.ident[:, :])
                    last.then_inc(turned, 1)

                def scores(n):
                    pe.wait_ge(t_split, n + 1)
                    if n:
                        pe.wait_ge(sc_done, PAIRS * n)
                    else:
                        pe.wait_ge(gate_done, GROUPS1)
                    for c, r in ((0, 0), (0, 1), (0, 2), (1, 0), (1, 1), (1, 2), (0, 3), (1, 3)):
                        rows = slice(32 * r, 32 * (r + 1))
                        if (c, r) == (0, PAIRS - 1) and n:
                            pe.wait_ge(o_done, n)
                        last = product(nc, ps[:, SCORE_BANKS[r], c * 2 * P:(c + 1) * 2 * P], k_h[rows, n % 2, c, :],
                                       k_l[rows, n % 2, c, :], qp_h[rows, n % 2, c, :, :].rearrange("p j t -> p (j t)"),
                                       qp_l[rows, n % 2, c, :, :].rearrange("p j t -> p (j t)"), True, True)
                        if c == DC - 1:
                            last.then_inc(sc_full, 1)

                def outputs(n):
                    pe.wait_ge(kd_done, n + 1)
                    pe.wait_ge(v_done, n + 1)
                    pe.wait_ge(state_done, n + 1)
                    if n:
                        pe.wait_ge(inter_done, n)
                    for c in range(DC):
                        nc.tensor.matmul(ps[:, 3, c * P:(c + 1) * P], kd[:, n % 4, c * P:(c + 1) * P],
                                         v[:, n, c * P:(c + 1) * P], start=True, stop=True)
                    for c in range(DC):
                        nc.tensor.matmul(ps[:, 3, D + c * P:D + (c + 1) * P], q_t[:, n % 4, c, :], state[:, c, :],
                                         start=True, stop=True)
                    pe.wait_ge(sc_done, PAIRS * (n + 1))
                    for h in range(H1):
                        last = nc.tensor.matmul(ps[:, 4, h * HD:(h + 1) * HD], sc[:, n % 2, h, :],
                                                v[:, n, h * HD:(h + 1) * HD], start=True, stop=True)
                    last.then_inc(out_full, 1)

                norm.tensor(pe)
                norm.wait_parts(pe)
                pe.wait_ge(w_split, 1)
                for b in range(NB):
                    cols = slice(b * BANK, (b + 1) * BANK)
                    for c in range(DC):
                        last = product(nc, ps[0:HD, 2 + b, :], w_h[:, c, G1], w_l[:, c, G1], xn_h[:, c, cols],
                                       xn_l[:, c, cols], c == 0, c == DC - 1)
                last.then_inc(g1_full, 1)
                pe.wait_ge(w_split, 2)
                projections(0)
                pe.wait_ge(consts, 160)
                for n in range(1, STEPS):
                    if n == 2:
                        for k in range(GROUPS1):
                            for i in (2 * k, 2 * k + 1):
                                last = nc.tensor.matmul(tokens_of(ps[:, 4:8, :], i), g1_t[:, i * P:(i + 1) * P],
                                                        wg2[:, :], start=True, stop=True)
                            last.then_inc(gate_full, 1)
                    if n >= 2:
                        scores(n - 2)
                    if n < TT:
                        projections(n)
                    if n - 1 < TT:
                        transposes(n - 1)
                    if n >= 2:
                        outputs(n - 2)
                pe.wait_ge(w_split, 3)
                for b in range(NB):
                    pe.wait_ge(scaled, GROUPS1 // NB * (b + 1))
                    for c in range(DC):
                        for k in range(4):
                            last = nc.tensor.transpose(ps[:, O_BANKS[b][c], k * P:(k + 1) * P],
                                                       o[:, 4 * b + k, c * P:(c + 1) * P], net.ident[:, :])
                        last.then_inc(o_turned, 1)
                    if b:
                        pe.wait_ge(inter_done, TT)
                    else:
                        pe.wait_ge(act_done, TT)
                    pe.wait_ge(o_split, DC * (b + 1))
                    for i in range(4 * b, 4 * b + 4):
                        for c in range(DC):
                            toks = slice(i * P, (i + 1) * P)
                            last = product(nc, tokens_of(ps[:, 0:4, :], i), o_h[:, c, toks], o_l[:, c, toks], wo_h[:, c, :],
                                           wo_l[:, c, :], c == 0, c == DC - 1)
                        if i % 2:
                            last.then_inc(y_full, 1)

            @block.scalar
            def _(act_e):
                act_e.wait_ge(net.raw_loaded, 16 * len(PIECES0) + 32)
                for hi, _, raw in WEIGHTS:
                    nc.scalar.activation(hi, raw, ACT.Copy).then_inc(w_high, 1)
                norm.scalar(act_e)
                act_e.wait_ge(consts, 160)
                act_e.wait_ge(g1_full, 1)
                nc.scalar.activation(g1_t[:, :].rearrange("p (n t) -> p n t", n=NB), ps[0:HD, 2:4, :], ACT.Copy).then_inc(g1_copied, 1)

                def square(k):
                    act_e.wait_ge(gated, 2 * k + 2)
                    nc.scalar.activation(sq[:, pair(k), :], o[:, pair(k), :], ACT.Square, scale=HD ** -0.5).then_inc(squares, 1)

                for n in range(TT + 1):
                    if n == 2:
                        for k in range(GROUPS1):
                            act_e.wait_ge(gate_full, k + 1)
                            nc.scalar.activation(gate[:, pair(k), :], ps[:, 4 + k, :].rearrange("p (i d) -> p i d", i=2),
                                                 ACT.Sigmoid).then_inc(gate_done, 1)
                    if group_at(n) is not None:
                        square(group_at(n))
                    if n < TT:
                        act_e.wait_ge(projected, n + 1)
                        if n >= 2:
                            act_e.wait_ge(rotated, n - 1)
                        nc.scalar.activation(act[:, n % 2, :], ps[:, 0, :], ACT.Silu).then_inc(act_done, 1)
                        nc.scalar.activation(v[:, n, :], ps[:, 1, 0:D], ACT.Copy).then_inc(v_done, 1)
                    i = n - 1
                    if i >= 0:
                        act_e.wait_ge(turned, i + 1)
                        if i >= 2:
                            act_e.wait_ge(sc_full, PAIRS * (i - 1))
                        if i >= 4:
                            act_e.wait_ge(out_full, i - 3)
                        q_ps = ps[:, 2, 0:D].rearrange("p (c t) -> p c t", c=DC)
                        nc.scalar.activation(q_t[:, i % 4, :, :], q_ps, ACT.Copy)
                        for j in range(2):
                            nc.scalar.activation(qp_h[:, i % 2, :, j, :], q_ps, ACT.Copy, scale=in_pair[:, j:j + 1])
                        nc.scalar.activation(k_h[:, i % 2, :, :], ps[:, 2, D:].rearrange("p (c t) -> p c t", c=DC),
                                             ACT.Copy).then_inc(t_high, 1)
                for b in range(NB):
                    for c in range(DC):
                        act_e.wait_ge(o_turned, DC * b + c + 1)
                        nc.scalar.activation(o_h[:, c, b * BANK:(b + 1) * BANK], ps[:, O_BANKS[b][c], :], ACT.Copy,
                                             scale=weight[:, c:c + 1]).then_inc(o_high, 1)
                    if b == 0:
                        square(GROUPS1 - 1)
            @block.vector
            def _(dve):
                links = 0

                def norm_scale(k):
                    nonlocal links
                    flat = lambda ap: ap.rearrange("p i h -> p (i h)")
                    cols = slice(2 * k * H1, (2 * k + 2) * H1)
                    dve.wait_ge(squares, k + 1)
                    nc.vector.tensor_reduce(ms[:, pair(k), :], sq[:, pair(k), :].rearrange("p i (h e) -> p i h e", e=HD),
                                            AX.X, ALU.add).then_inc(chain, 1)
                    dve.wait_ge(chain, links + 1)
                    links = inverse_root(nc, dve, flat(rms[:, pair(k), :]), flat(ms[:, pair(k), :]), RMS_EPS,
                                         root[:, 0, cols], root[:, 1, cols], chain, links + 1)
                    dve.wait_ge(chain, links)
                    by_head = o[:, pair(k), :].rearrange("p i (h e) -> p (i h) e", e=HD)
                    nc.vector.tensor_tensor(by_head, by_head, flat(rms[:, pair(k), :]).unsqueeze(2).broadcast_to([P, 2 * H1, HD]),
                                            ALU.mult).then_inc(scaled, 1)

                norm.vector(dve)
                dve.wait_ge(consts, 160)
                for n in range(STEPS):
                    i = n - 2
                    if i >= 0:
                        for r in range(PAIRS):
                            dve.wait_ge(sc_full, PAIRS * i + r + 1)
                            nc.vector.tensor_tensor(of_pair(sc[:, i % 2, :, :], r),
                                                    ps[:, SCORE_BANKS[r], :].rearrange("p (c x) -> p c x", c=DC),
                                                    of_pair(decay[:, :, :], r), ALU.mult).then_inc(sc_done, 1)
                    if group_at(n) is not None:
                        norm_scale(group_at(n))
                    if n < TT:
                        dve.wait_ge(act_done, n + 1)
                        wide = lambda ap: ap.rearrange("p (h e) -> p h e", e=HD)
                        nc.vector.tensor_tensor(wide(by_cos[:, n % 2, :]), wide(act[:, n % 2, :]),
                                                cos[:, n, :].unsqueeze(1).broadcast_to([P, 2 * H1, HD]), ALU.mult).then_inc(cos_done, 1)
                        dve.wait_ge(cos_done, n + 1)
                        dve.wait_ge(sin_done, 2 * n + 2)
                        if n >= 2:
                            dve.wait_ge(turned, n - 1)
                            dve.wait_ge(kd_done, n - 1)
                        nc.vector.tensor_tensor(rot[:, n % 2, :], by_cos[:, n % 2, :], by_sin[:, n % 2, :], ALU.add).then_inc(rotated, 1)
                    i = n - 1
                    if 0 <= i < TT:
                        dve.wait_ge(t_high, i + 1)
                        q_ps = ps[:, 2, 0:D].rearrange("p (c t) -> p c t", c=DC)
                        for j in range(2):
                            nc.vector.scalar_tensor_tensor(qp_l[:, i % 2, :, j, :], q_ps, in_pair[:, j:j + 1],
                                                           qp_h[:, i % 2, :, j, :].bitcast(F32), ALU.mult, ALU.subtract)
                        nc.vector.tensor_tensor(k_l[:, i % 2, :, :], ps[:, 2, D:].rearrange("p (c t) -> p c t", c=DC),
                                                k_h[:, i % 2, :, :].bitcast(F32), ALU.subtract).then_inc(t_split, 1)
                    i = n - 2
                    if i >= 0:
                        dve.wait_ge(out_full, i + 1)
                        nc.vector.tensor_tensor(heads(inter[:, i % 2, :]), heads(ps[:, 3, D:]),
                                                decay_q[:, :].unsqueeze(2).broadcast_to([P, H1, HD]), ALU.mult).then_inc(decayed, 1)
                        nc.vector.tensor_tensor(kv[:, :, :], ps[:, 3, 0:D].rearrange("p (c t) -> p c t", c=DC),
                                                same_head[:, :].unsqueeze(1).broadcast_to([P, DC, P]), ALU.mult).then_inc(inter_done, 1)
                        dve.wait_ge(decayed, i + 1)
                        nc.vector.tensor_tensor(o[:, i, :], inter[:, i % 2, :], ps[:, 4, 0:D], ALU.add).then_inc(o_done, 1)
                        dve.wait_ge(inter_done, i + 1)
                        for c in range(DC):
                            last = nc.vector.scalar_tensor_tensor(state[:, c, :], state[:, c, :], lam_c[:, c:c + 1], kv[:, c, :],
                                                                  ALU.mult, ALU.add)
                        last.then_inc(state_done, 1)
                        dve.wait_ge(state_done, i + 2)
                for b in range(NB):
                    for c in range(DC):
                        cols = slice(b * BANK, (b + 1) * BANK)
                        dve.wait_ge(o_high, DC * b + c + 1)
                        nc.vector.scalar_tensor_tensor(o_l[:, c, cols], ps[:, O_BANKS[b][c], :], weight[:, c:c + 1],
                                                       o_h[:, c, cols].bitcast(F32), ALU.mult, ALU.subtract).then_inc(o_split, 1)
                    if b == 0:
                        norm_scale(GROUPS1 - 1)
                        add_pairs(nc, net, dve, ps[:, 0:4, :], y_full, y_added, range(0, TT // 4), 0)
                add_pairs(nc, net, dve, ps[:, 0:4, :], y_full, y_added, range(TT // 4, TT // 2), TT // 4)


EXP1, F1, TOP1 = 32, 176, 6
SHARED1 = 2 * F1
CAPACITY = 2 * (T * TOP1 // EXP1)
TILES1 = EXP1 * F1 // P
GRAIN = 16
SH1 = -(-SHARED1 // P)
SHARED_TILES = [min(P, SHARED1 - k * P) for k in range(SH1)]


SG, SU = 0, DC * SHARED1
SD = 2 * SU
SW = SD + (SH1 - 1) * D
RAW2 = SW + D
TAIL = SHARED_TILES[-1]


def load_ffn1_weights(sp, net):
    for to, src in ((net.raw[:, SG:SU], net.dram["wsg"]), (net.raw[:, SU:SD], net.dram["wsu"]),
                    (net.raw[:, SD:SW].rearrange("p (k d) -> p k d", d=D),
                     net.dram["wsd"][0:(SH1 - 1) * P, :].rearrange("(k p) d -> p k d", p=P)),
                    (net.raw[0:TAIL, SW:RAW2], net.dram["wsd"][(SH1 - 1) * P:SHARED1, :])):
        sp.dma_start(to, src).then_inc(net.raw_loaded, 16)


def silu_experts_phase(nc, net, out):
    BODY, RAW, RING, WRING = 4, 2, 2, 4
    AHEAD = 2
    GATE, UP, DOWN, W = 0, DC * P, 2 * DC * P, 2 * DC * P + D
    SENT = 8 - TOP1
    assert TILES1 % BODY == 0
    with ExitStack() as mem:
        sb = lambda n, s, d=F32: mem.enter_context(nc.sbuf_tensor(f"f1_{n}", s, d))
        sem = lambda n: net.ctx.enter_context(nc.semaphore(f"f1_{n}"))
        ps, xn_h, xn_l = net.ps, net.xn_h, net.xn_l
        router, before = sb("router", [P, DC, EXP1]), sb("before", [P, P])
        xn = sb("xn", [P, DC, T])
        before_b, ones_b = sb("before_b", [P, P], BF16), sb("ones_b", [P, P], BF16)
        sw, st = net.raw[:, 0:SW], net.raw[0:TAIL, SW:RAW2]
        sw_h, sw_l = sb("sw_h", [P, SW], F32R), sb("sw_l", [P, SW], F32R)
        st_h, st_l = sb("st_h", [TAIL, D], F32R), sb("st_l", [TAIL, D], F32R)
        e_raw = sb("e_raw", [P, RAW, W])
        e_h, e_l = sb("e_h", [P, WRING, W], F32R), sb("e_l", [P, WRING, W], F32R)
        one = sb("one", [P, 1])
        silu, act = sb("silu", [P, RING, T]), sb("act", [P, RING, T])
        a_h, a_l = sb("a_h", [P, RING, T], F32R), sb("a_l", [P, RING, T], F32R)
        s_h, s_l = sb("s_h", [P, SH1, T], F32R), sb("s_l", [P, SH1, T], F32R)
        cw_row = sb("cw_row", [P, RING, T])
        logit = sb("logit", [P, TT, EXP1 + SENT])
        score, found = sb("score", [P, TT, EXP1]), sb("found", [P, TT, EXP1 + SENT])
        best, take = sb("best", [P, TT, 8]), sb("take", [P, TT, 8])
        total, cw = sb("total", [P, TT]), sb("cw", [P, TT, EXP1])
        chosen = sb("chosen", [P, TT, EXP1], BF16)
        cw_t = sb("cw_t", [EXP1, T])
        y = sb("y", [P, DC, T])
        grains = net.cw_grains

        consts = sem("consts")
        s_high, s_split = sem("s_high"), sem("s_split")
        logits, scored, exped, marked, ranked = sem("logits"), sem("scored"), sem("exped"), sem("marked"), sem("ranked")
        routed, cw_turned, cw_copied, cw_stored = sem("routed"), sem("cw_turned"), sem("cw_copied"), sem("cw_stored")
        e_loaded = [sem(f"e_loaded{r}") for r in range(RAW)]
        row_loaded = [sem(f"row_loaded{r}") for r in range(RING)]
        e_high, e_split = sem("e_high"), sem("e_split")
        gate_full, up_full, silued, timed, weighed = sem("gate_full"), sem("up_full"), sem("silued"), sem("timed"), sem("weighed")
        act_high, act_split, down_done = sem("act_high"), sem("act_split"), sem("down_done")
        y_copied, y_turned = [sem(f"y_copied{c}") for c in range(DC)], sem("y_turned")
        y_added, stored, chain = sem("y_added"), sem("stored"), sem("chain")

        norm = Norm(nc, net, "n3", mem, full=xn[:, :, :], xc=cw_row[:, :, :].rearrange("p r (k d) -> p (r k) d", d=D))

        def blocks(ap):
            return ap.rearrange("p (n t) -> p n t", n=NB)

        def steps(eng, loop_end, last, step):
            for n in range(BODY):
                step(0, n)
            with eng.Fori(1, loop_end) as it:
                for r in range(BODY):
                    step(it, r)
            for n in range(loop_end * BODY, last):
                step(*divmod(n, BODY))

        def known(it, r, low, high=TILES1 + BODY):
            return not isinstance(it, int) or low <= it * BODY + r < high

        with nc.Block() as block:

            @block.sync
            def _(sp):
                sp.dma_start(router[:, :, :], net.dram["router"]).then_inc(consts, 16)
                sp.dma_start(before[:, :], net.dram["before"]).then_inc(consts, 16)

                def load_weights(it, r):
                    n = it * BODY + r
                    if known(it, r, RAW):
                        sp.wait_ge(e_split, n - RAW + 1)
                    sp.dma_start(e_raw[:, r % RAW, :], net.dram["we1"][n]).then_inc(e_loaded[r % RAW], 16)

                def load_row(it, r):
                    n = it * BODY + r
                    if known(it, r, RING):
                        sp.wait_ge(weighed, n - RING + 1)
                    sp.dma_start(cw_row[:, r % RING, :],
                                 grains[n].unsqueeze(1).broadcast_to([P // GRAIN, GRAIN, T])).then_inc(row_loaded[r % RING], 16)

                for r in range(RAW):
                    load_weights(0, r)
                sp.wait_ge(cw_copied, 1)
                sp.dma_start(grains.rearrange("a b t -> (a b) t").rearrange("(e g) t -> e g t", e=EXP1),
                             cw_t[:, :].unsqueeze(1).broadcast_to([EXP1, F1 // GRAIN, T])).then_inc(cw_stored, 16)
                sp.wait_ge(cw_stored, 16)

                def step(it, r):
                    load_row(it, r)
                    if known(it, r, 0, TILES1 - RAW):
                        load_weights(it, r + RAW)

                steps(sp, TILES1 // BODY - 1, TILES1, step)
                for j in range(TT // 2):
                    sp.wait_ge(y_added, j + 1)
                    sp.dma_start(out.rearrange("(i p) d -> p i d", p=P)[:, 2 * j:2 * j + 2, :],
                                 net.x[:, 2 * j:2 * j + 2, :]).then_inc(stored, 16)
                sp.wait_ge(stored, 16 * (TT // 2))

            @block.tensor
            def _(pe):
                norm.tensor(pe)
                norm.wait_parts(pe)
                def project(bank, rows, weight, full):
                    for b in range(NB):
                        cols = slice(b * BANK, (b + 1) * BANK)
                        for c in range(DC):
                            last = product(nc, ps[0:rows, bank + b, :], *weight(c), xn_h[:, c, cols], xn_l[:, c, cols],
                                           c == 0, c == DC - 1)
                    last.then_inc(full, 1)

                def down(weight, rows, h, l, first, final):
                    for m in range(DC):
                        for b in range(NB):
                            cols = slice(b * BANK, (b + 1) * BANK)
                            wt = weight(m)
                            last = product(nc, ps[:, 4 + 2 * m + b, :], *wt, h[0:rows, cols], l[0:rows, cols], first, final)
                    last.then_inc(down_done, 1)

                def logits_of_tokens():
                    norm.wait_full(pe)
                    pe.wait_ge(consts, 35)
                    for i in range(TT):
                        for c in range(DC):
                            last = nc.tensor.matmul(ps[:, 7, i * EXP1:(i + 1) * EXP1], xn[:, c, i * P:(i + 1) * P],
                                                    router[:, c, :], start=c == 0, stop=c == DC - 1)
                    last.then_inc(logits, 1)

                pe.wait_ge(s_split, 2)
                for k, rows in enumerate(SHARED_TILES):
                    def piece(base):
                        def weight(c):
                            part = slice(base + c * SHARED1 + k * P, base + c * SHARED1 + k * P + rows)
                            return sw_h[:, part], sw_l[:, part]
                        return weight
                    if k:
                        pe.wait_ge(silued, k)
                    project(0, rows, piece(SG), gate_full)
                    if k:
                        pe.wait_ge(timed, k)
                    project(2, rows, piece(SU), up_full)
                    if k == 0:
                        logits_of_tokens()
                pe.wait_ge(marked, 1)
                for i in range(TT):
                    for k in range(i + 1):
                        last = nc.tensor.matmul(ps[:, 6, i * EXP1:(i + 1) * EXP1], before_b[:, :] if k == i else ones_b[:, :],
                                                chosen[:, k, :], start=k == 0, stop=k == i)
                last.then_inc(ranked, 1)
                pe.wait_ge(routed, 1)
                for i in range(TT):
                    last = nc.tensor.transpose(ps[0:EXP1, 4 + i // 4, (i % 4) * P:(i % 4 + 1) * P], cw[:, i, :], net.ident[:, :])
                last.then_inc(cw_turned, 1)
                pe.wait_ge(cw_copied, 1)
                for k, rows in enumerate(SHARED_TILES):
                    pe.wait_ge(act_split, k + 1)
                    if k < SH1 - 1:
                        weight = lambda m: (sw_h[:, SD + k * D + m * P:SD + k * D + (m + 1) * P],
                                            sw_l[:, SD + k * D + m * P:SD + k * D + (m + 1) * P])
                    else:
                        weight = lambda m: (st_h[:, m * P:(m + 1) * P], st_l[:, m * P:(m + 1) * P])
                    down(weight, rows, s_h[:, k, :], s_l[:, k, :], k == 0, False)

                def step(it, r):
                    n = it * BODY + r

                    def piece(slot, base):
                        return lambda c: (e_h[:, slot, base + c * P:base + (c + 1) * P],
                                          e_l[:, slot, base + c * P:base + (c + 1) * P])

                    if known(it, r, 0, TILES1):
                        pe.wait_ge(e_split, n + 1)
                        pe.wait_ge(silued, n + SH1)
                        project(0, P, piece(r % WRING, GATE), gate_full)
                        pe.wait_ge(timed, n + SH1)
                        project(2, P, piece(r % WRING, UP), up_full)
                    if known(it, r, 1):
                        m = (r - 1) % BODY
                        pe.wait_ge(act_split, n + SH1)
                        final = isinstance(it, int) and n == TILES1
                        down(piece(m % WRING, DOWN), P, a_h[:, m % RING, :], a_l[:, m % RING, :], False, final)

                steps(pe, TILES1 // BODY, TILES1 + 1, step)
                for j in range(TT // 2):
                    pe.wait_ge(y_copied[0], j // 2 + 1)
                    pe.wait_ge(y_copied[1], j // 2 + 1)
                    for i in (2 * j, 2 * j + 1):
                        for c in range(DC):
                            last = nc.tensor.transpose(tokens_of(ps[:, 0:4, :], i)[:, c * P:(c + 1) * P],
                                                       y[:, c, i * P:(i + 1) * P], net.ident[:, :])
                    last.then_inc(y_turned, 1)

            @block.scalar
            def _(act_e):
                def high_weights(it, r):
                    act_e.wait_ge(e_loaded[r % RAW], 16 * (it * (BODY // RAW) + r // RAW) + 16)
                    if known(it, r, WRING):
                        act_e.wait_ge(down_done, it * BODY + (r - WRING + 1 + SH1))
                    nc.scalar.activation(e_h[:, r % WRING, :], e_raw[:, r % RAW, :], ACT.Copy).then_inc(e_high, 1)


                act_e.wait_ge(net.raw_loaded, 16 * len(PIECES0) + 96)
                nc.scalar.activation(sw_h[:, :], sw[:, :], ACT.Copy).then_inc(s_high, 1)
                nc.scalar.activation(st_h[:, :], st[:, :], ACT.Copy).then_inc(s_high, 1)
                norm.scalar(act_e)
                high_weights(0, 0)
                high_weights(0, 1)

                def silu_gate(n, k, rows):
                    act_e.wait_ge(gate_full, n + 1)
                    if not isinstance(n, int) or n >= RING:
                        act_e.wait_ge(timed, n - RING + 1)
                    nc.scalar.activation(blocks(silu[0:rows, k % RING, :]), ps[0:rows, 0:2, :], ACT.Silu).then_inc(silued, 1)

                for k, rows in enumerate(SHARED_TILES):
                    silu_gate(k, k, rows)
                    if k == 0:
                        act_e.wait_ge(scored, 1)
                        nc.scalar.activation(score[:, :, :], score[:, :, :], ACT.Exp).then_inc(exped, 1)
                    act_e.wait_ge(timed, k + 1)
                    nc.scalar.activation(s_h[0:rows, k, :], act[0:rows, k % RING, :], ACT.Copy).then_inc(act_high, 1)

                def step(it, r):
                    n = it * BODY + r
                    if known(it, r, 1):
                        m = (r - 1) % RING
                        act_e.wait_ge(weighed, n)
                        if known(it, r, 1 + RING):
                            act_e.wait_ge(down_done, n - RING + SH1)
                        nc.scalar.activation(a_h[:, m, :], act[:, m, :], ACT.Copy).then_inc(act_high, 1)
                    if known(it, r, 0, TILES1):
                        silu_gate(n + SH1, r, P)
                    if known(it, r, 0, TILES1 - AHEAD):
                        high_weights(it, r + AHEAD)

                steps(act_e, TILES1 // BODY - 1, TILES1 + 1, step)
                act_e.wait_ge(down_done, SH1 + TILES1)
                for b in range(NB):
                    nc.scalar.activation(y[:, 0, b * BANK:(b + 1) * BANK], ps[:, 4 + b, :], ACT.Copy).then_inc(y_copied[0], 1)

            @block.gpsimd
            def _(pool):
                nc.gpsimd.memset(logit[:, :, EXP1:], BIG).then_inc(consts, 1)
                nc.gpsimd.memset(take[:, :, TOP1:], BIG).then_inc(consts, 1)
                nc.gpsimd.memset(ones_b[:, :], 1.0).then_inc(consts, 1)
                pool.wait_ge(s_high, 2)
                nc.gpsimd.tensor_tensor(sw_l[:, :], sw[:, :], sw_h[:, :].bitcast(F32), ALU.subtract).then_inc(s_split, 1)
                nc.gpsimd.tensor_tensor(st_l[:, :], st[:, :], st_h[:, :].bitcast(F32), ALU.subtract).then_inc(s_split, 1)

                def low_weights(it, r):
                    pool.wait_ge(e_high, it * BODY + r + 1)
                    nc.gpsimd.tensor_tensor(e_l[:, r % WRING, :], e_raw[:, r % RAW, :], e_h[:, r % WRING, :].bitcast(F32),
                                            ALU.subtract).then_inc(e_split, 1)

                for r in range(AHEAD):
                    low_weights(0, r)
                for k, rows in enumerate(SHARED_TILES):
                    pool.wait_ge(act_high, k + 1)
                    nc.gpsimd.tensor_tensor(s_l[0:rows, k, :], act[0:rows, k % RING, :], s_h[0:rows, k, :].bitcast(F32),
                                            ALU.subtract).then_inc(act_split, 1)

                def step(it, r):
                    n = it * BODY + r
                    if known(it, r, 0, TILES1 - AHEAD):
                        low_weights(it, r + AHEAD)
                    if known(it, r, 0, TILES1):
                        pool.wait_ge(row_loaded[r % RING], 16 * (it * (BODY // RING) + r // RING) + 16)
                        pool.wait_ge(timed, n + SH1 + 1)
                        nc.gpsimd.tensor_tensor(act[:, r % RING, :], act[:, r % RING, :], cw_row[:, r % RING, :],
                                                ALU.mult).then_inc(weighed, 1)

                steps(pool, TILES1 // BODY - 1, TILES1, step)

            @block.vector
            def _(dve):
                links = [0]

                def link(ins):
                    ins.then_inc(chain, 1)
                    links[0] += 1
                    dve.wait_ge(chain, links[0])

                def times(n, k, rows):
                    dve.wait_ge(up_full, n + 1)
                    dve.wait_ge(silued, n + 1)
                    if not isinstance(n, int) or n >= RING:
                        dve.wait_ge(act_split, n - RING + 1)
                    nc.vector.tensor_tensor(blocks(act[0:rows, k % RING, :]), ps[0:rows, 2:4, :], blocks(silu[0:rows, k % RING, :]),
                                            ALU.mult).then_inc(timed, 1)

                norm.vector(dve)
                dve.wait_ge(consts, 35)
                times(0, 0, SHARED_TILES[0])
                dve.wait_ge(logits, 1)
                nc.vector.tensor_copy(before_b[:, :], before[:, :])
                link(nc.vector.tensor_copy(logit[:, :, 0:EXP1], ps[:, 7, 0:TT * EXP1].rearrange("p (i e) -> p i e", e=EXP1)))
                for i in range(TT):
                    last = nc.vector.max(best[:, i, :], logit[:, i, 0:EXP1])
                link(last)
                nc.vector.tensor_tensor(score[:, :, :], logit[:, :, 0:EXP1], best[:, :, 0:1].broadcast_to([P, TT, EXP1]),
                                        ALU.subtract).then_inc(scored, 1)
                link(nc.vector.tensor_copy(take[:, :, 0:TOP1], best[:, :, 0:TOP1]))
                for i in range(TT):
                    last = nc.vector.match_replace(found[:, i, :], take[:, i, :], logit[:, i, :], TAKEN)
                link(last)
                nc.vector.tensor_scalar(chosen[:, :, :], found[:, :, 0:EXP1], TAKEN, None, ALU.is_equal).then_inc(marked, 1)
                dve.wait_ge(exped, 1)
                link(nc.vector.tensor_reduce(total[:, :], score[:, :, :], AX.X, ALU.add))
                link(nc.vector.reciprocal(total[:, :], total[:, :]))
                link(nc.vector.tensor_tensor(score[:, :, :], score[:, :, :], total[:, :].unsqueeze(2).broadcast_to([P, TT, EXP1]),
                                             ALU.mult))
                link(nc.vector.scalar_tensor_tensor(cw[:, :, :], found[:, :, 0:EXP1], TAKEN, score[:, :, :], ALU.is_equal, ALU.mult))
                link(nc.vector.tensor_reduce(total[:, :], cw[:, :, :], AX.X, ALU.add))
                link(nc.vector.tensor_scalar(total[:, :], total[:, :], 1e-20, None, ALU.add))
                link(nc.vector.reciprocal(total[:, :], total[:, :]))
                link(nc.vector.tensor_tensor(cw[:, :, :], cw[:, :, :], total[:, :].unsqueeze(2).broadcast_to([P, TT, EXP1]),
                                             ALU.mult))
                for k in range(1, SH1):
                    times(k, k, SHARED_TILES[k])
                dve.wait_ge(ranked, 1)
                nc.vector.scalar_tensor_tensor(cw[:, :, :], ps[:, 6, 0:TT * EXP1].rearrange("p (i e) -> p i e", e=EXP1),
                                               float(CAPACITY), cw[:, :, :], ALU.is_lt, ALU.mult).then_inc(routed, 1)
                dve.wait_ge(cw_turned, 1)
                nc.vector.tensor_copy(blocks(cw_t[:, :]), ps[0:EXP1, 4:6, :]).then_inc(cw_copied, 1)

                def step(it, r):
                    n = it * BODY + r
                    if known(it, r, 1):
                        m = (r - 1) % RING
                        dve.wait_ge(act_high, n + SH1)
                        nc.vector.tensor_tensor(a_l[:, m, :], act[:, m, :], a_h[:, m, :].bitcast(F32),
                                                ALU.subtract).then_inc(act_split, 1)
                    if known(it, r, 0, TILES1):
                        times(n + SH1, r, P)

                steps(dve, TILES1 // BODY, TILES1 + 1, step)
                dve.wait_ge(down_done, SH1 + TILES1)
                for b in range(NB):
                    nc.vector.tensor_copy(y[:, 1, b * BANK:(b + 1) * BANK], ps[:, 6 + b, :]).then_inc(y_copied[1], 1)
                for j in range(TT // 2):
                    dve.wait_ge(y_turned, j + 1)
                    add_to_x(nc, net, 2 * j, ps[:, j:j + 1, :]).then_inc(y_added, 1)


def program(nc, dram, out):
    net = Net()
    net.dram = dram
    with ExitStack() as ctx:
        net.ctx = ctx
        sb = lambda n, s, d=F32: ctx.enter_context(nc.sbuf_tensor(n, s, d))
        net.ps = ctx.enter_context(nc.psum_tensor("ps", [P, 8, BANK], F32))
        net.x = sb("x", [P, TT, D])
        net.xn_h, net.xn_l = sb("xn_h", [P, DC, T], F32R), sb("xn_l", [P, DC, T], F32R)
        net.ident = sb("ident", [P, P])
        net.raw = sb("raw", [P, max(RAW0, RAW1, RAW2)])
        net.raw_loaded = ctx.enter_context(nc.semaphore("raw_loaded"))
        net.stats, net.moments = sb("stats", [P, TT, 6]), sb("moments", [P, TT, 2])
        net.cw_dram = nc.dram_tensor("cw", (EXP0, T), F32, kind="Internal").ap()
        net.cw_grains = nc.dram_tensor("cw_grains", (TILES1, P // GRAIN, T), F32, kind="Internal").ap()
        net.norm_sems = {n: ctx.enter_context(nc.semaphore(f"norm_{n}")) for n in NORM_SEMS}
        net.norm_counts = {n: 0 for n in NORM_SEMS}
        softmax_attention_phase(nc, net)
        squared_relu_experts_phase(nc, net)
        linear_attention_phase(nc, net)
        silu_experts_phase(nc, net, out)


def kernel(**inputs):
    import numpy as _np
    import concourse.bacc as _bacc
    from concourse import mybir as _mybir
    from concourse.bass_utils import run_bass_kernel_spmd as _run

    def get(name):
        return _np.asarray(inputs[name])

    def grouped(w, groups):
        return w.reshape(DC, P, groups, -1).transpose(2, 1, 0, 3)

    def tiled(w):
        return w.reshape(-1, P, w.shape[1]).transpose(1, 0, 2)

    def flat(w):
        return tiled(w).reshape(P, -1)

    def by_feature(w):
        w = w.transpose(1, 0, 2).reshape(DC, P, TILES1, P)
        return w.transpose(2, 1, 0, 3).reshape(TILES1, P, DC * P)

    host = {
        "x": get("L0_attn_inputs_q").reshape(T, D),
        "ident": _np.eye(P, dtype=_np.float32),
        "bq": get("L0_attn_bq").reshape(HEADS, DH).T, "bk": get("L0_attn_bk").reshape(KV, DH).T, "bv": get("L0_attn_bv"), "bo": get("L0_attn_bo"),
        "wq": grouped(get("L0_attn_wq"), KV), "wk": grouped(get("L0_attn_wk"), KV), "wv": grouped(get("L0_attn_wv"), KV),
        "wo": get("L0_attn_wo").reshape(KV, PER, DH, D).transpose(0, 2, 1, 3),
        "gate0": tiled(get("L0_ffn_gate_w").T), "gate_bias": get("L0_ffn_gate_bias"),
        "fc1": flat(get("L0_ffn_fc1_w").T), "fc2": flat(get("L0_ffn_fc2_w").T),
        "sup0": flat(get("L0_ffn_shared_up_w").T), "sdn0": flat(get("L0_ffn_shared_down_w").T),
        "we0": _np.stack([get("L0_ffn_w1").transpose(0, 2, 1), get("L0_ffn_w2").transpose(0, 2, 1)], 2),
        "w1a": tiled(_np.concatenate([get("L1_attn_Wq"), get("L1_attn_Wk"), get("L1_attn_Wv"), get("L1_attn_Wg1")], 1)),
        "wg2": get("L1_attn_Wg2"), "wo1": tiled(get("L1_attn_Wo")), "norm_weight": get("L1_attn_norm_weight").reshape(DC, P).T,
        **{k: a.astype(_np.float32) for k, a in decay_tables().items()},
        "router": tiled(get("L1_ffn_wg_router").T), "before": _np.triu(_np.ones((P, P), _np.float32), 1),
        "wsg": flat(get("L1_ffn_ws_gate")), "wsu": flat(get("L1_ffn_ws_up")), "wsd": get("L1_ffn_ws_down"),
        "we1": _np.concatenate([by_feature(get("L1_ffn_w_gate")), by_feature(get("L1_ffn_w_up")),
                                get("L1_ffn_w_down").reshape(TILES1, P, D)], 2),
    }
    nc = _bacc.Bacc("TRN2", target_bir_lowering=False, num_devices=1)
    arrays, dram = {}, {}
    for name, a in host.items():
        a = _np.ascontiguousarray(a)
        arrays[f"in_{name}"] = a
        dram[name] = nc.dram_tensor(f"in_{name}", a.shape, _mybir.dt.from_np(a.dtype), kind="ExternalInput").ap()
    out = nc.dram_tensor("out_x", (T, D), F32, kind="ExternalOutput").ap()
    program(nc, dram, out)
    r = _run(nc, [arrays], core_ids=[0])
    return r.results[0]["out_x"].reshape(1, T, D)
```
